# Optimizing a Trainium2 kernel written in Bass

```python
import numpy as np
import jax
import jax.numpy as jnp

def _softmax(x, axis=-1):
    return jax.nn.softmax(x, axis=axis)

def _gelu(x):
    return jax.nn.gelu(x, approximate=True)

def _silu(x):
    return jax.nn.silu(x)

def _sigmoid(x):
    return jax.nn.sigmoid(x)

def _layernorm(x, axis=-1, eps=1e-05):
    m = jnp.mean(x, axis=axis, keepdims=True)
    v = jnp.var(x, axis=axis, keepdims=True)
    return (x - m) / jnp.sqrt(v + eps)

def _scatter_add(tgt, idx, src, axis=0):
    return tgt.at[idx].add(src)

def _segment_sum(src, seg, n):
    return jax.ops.segment_sum(src, seg, n)
kernel_name = 'mk_xattn_ffn_d2_seqx_r8_96d312'

def setup_inputs(seed: int=0):
    np.random.seed(seed)
    _w = jnp.asarray

    def _rec_inputs():
        import jax
        import jax.numpy as jnp
        _rk = jax.random.key(seed)
        x = -0.0002928 + 1 * jax.random.normal(jax.random.fold_in(_rk, 1), (16, 128, 128), jnp.float32)
        _lenS = 128 - jax.random.randint(jax.random.fold_in(_rk, 7), (16,), 0, max(1, 128 // 4) + 1, jnp.int32)
        _lenS2 = 77 - jax.random.randint(jax.random.fold_in(_rk, 8), (16,), 0, max(1, 77 // 4) + 1, jnp.int32)
        _ctx_1024P = jax.random.normal(jax.random.fold_in(_rk, 11), (16, 16, 128), jnp.float32)
        _ctx_1024c = jax.random.dirichlet(jax.random.fold_in(_rk, 511), 0.3 * jnp.ones((16,), jnp.float32), (16, 77))
        _ctx_1024t = jnp.einsum('bsk,bkd->bsd', _ctx_1024c, _ctx_1024P)
        _ctx_1024t = _ctx_1024t * jax.lax.rsqrt(jnp.mean(jnp.square(_ctx_1024t)) + 1e-12) * 0.953939
        ctx_1024 = -1.39393e-06 + 0.999914 * (_ctx_1024t + 0.3 * jax.random.normal(jax.random.fold_in(_rk, 611), (16, 77, 128), jnp.float32))
        return (x, ctx_1024, _lenS2)
    x, ctx_1024, _lenS2 = _rec_inputs()

    def _L0_xattn_setup():
        import jax, jax.numpy as jnp
        import numpy as np
        EMBED_DIM = 128
        NUM_HEADS = 16
        HEAD_DIM = EMBED_DIM // NUM_HEADS
        SCALE = HEAD_DIM ** (-0.5)

        def _split_heads(x, B):
            return x.reshape(B, -1, NUM_HEADS, HEAD_DIM).transpose(0, 2, 1, 3)
        key = jax.random.key(seed)
        ks = jax.random.split(key, 11)
        B, S, D = (2, 256, EMBED_DIM)
        std = D ** (-0.5)
        return {'query': jax.random.normal(ks[0], (B, S, D), jnp.float32), 'key': jax.random.normal(ks[1], (B, S, D), jnp.float32), 'value': jax.random.normal(ks[2], (B, S, D), jnp.float32), 'q_w': jax.random.normal(ks[3], (D, D), jnp.float32) * std, 'q_b': jnp.zeros((D,), jnp.float32), 'k_w': jax.random.normal(ks[4], (D, D), jnp.float32) * std, 'k_b': jnp.zeros((D,), jnp.float32), 'v_w': jax.random.normal(ks[5], (D, D), jnp.float32) * std, 'v_b': jnp.zeros((D,), jnp.float32), 'o_w': jax.random.normal(ks[6], (D, D), jnp.float32) * std, 'o_b': jnp.zeros((D,), jnp.float32)}
    _L0_xattn_all = _L0_xattn_setup()
    _L0_xattn_in = {k: v for k, v in _L0_xattn_all.items() if k in ('q_w', 'q_b', 'k_w', 'k_b', 'v_w', 'v_b', 'o_w', 'o_b')}
    del _L0_xattn_all

    def _L0_ffn_setup():
        import jax, jax.numpy as jnp
        import numpy as np
        EPS = 1e-05

        def rmsnorm(x):
            return x * jax.lax.rsqrt(jnp.mean(x * x, axis=-1, keepdims=True) + EPS)

        def act_quant(x):
            scale = 127.0 / jnp.clip(jnp.max(jnp.abs(x), axis=-1, keepdims=True), 1e-05)
            q = jnp.clip(jnp.round(x * scale), -128.0, 127.0) / scale
            return x + jax.lax.stop_gradient(q - x)

        def weight_quant(w):
            scale = 1.0 / jnp.clip(jnp.mean(jnp.abs(w)), 1e-05)
            q = jnp.clip(jnp.round(w * scale), -1.0, 1.0) / scale
            return w + jax.lax.stop_gradient(q - w)

        def bitlinear(x, w, b):
            xq = act_quant(rmsnorm(x))
            wq = weight_quant(w)
            return jnp.einsum('bsd,fd->bsf', xq, wq) + b
        key = jax.random.key(seed)
        k0, k1, k2 = jax.random.split(key, 3)
        B, S, D, F = (2, 1024, 128, 512)
        x = jax.random.normal(k0, (B, S, D), dtype=jnp.float32)
        w1 = jax.random.normal(k1, (F, D), dtype=jnp.float32) * (1.0 / np.sqrt(D))
        b1 = jnp.zeros((F,), dtype=jnp.float32)
        w2 = jax.random.normal(k2, (D, F), dtype=jnp.float32) * (1.0 / np.sqrt(F))
        b2 = jnp.zeros((D,), dtype=jnp.float32)
        return {'x': x, 'w1': w1, 'b1': b1, 'w2': w2, 'b2': b2}
    _L0_ffn_all = _L0_ffn_setup()
    _L0_ffn_in = {k: v for k, v in _L0_ffn_all.items() if k in ('w1', 'b1', 'w2', 'b2')}
    del _L0_ffn_all

    def _L1_xattn_setup():
        import jax, jax.numpy as jnp
        import numpy as np
        D_MODEL = 128
        N_HEADS = 16
        D_Q = 64
        D_V = 64
        D_OUT = 128
        B, S = (4, 256)

        def _layer_norm(x, g, b, eps=1e-05):
            mu = jnp.mean(x, axis=-1, keepdims=True)
            var = jnp.mean((x - mu) ** 2, axis=-1, keepdims=True)
            return (x - mu) * jax.lax.rsqrt(var + eps) * g + b

        def _rope(x, theta=10000.0):
            D = x.shape[-1]
            inv_freq = 1.0 / theta ** (jnp.arange(0, D, 2, dtype=jnp.float32) / D)
            t = jnp.arange(x.shape[-2], dtype=jnp.float32)
            freqs = t[:, None] * inv_freq[None, :]
            freqs = jnp.repeat(freqs, 2, axis=-1)
            cos, sin = (jnp.cos(freqs), jnp.sin(freqs))
            x1, x2 = (x[..., 0::2], x[..., 1::2])
            rot = jnp.stack([-x2, x1], axis=-1).reshape(x.shape)
            return x * cos + rot * sin
        key = jax.random.key(seed)
        ks = jax.random.split(key, 10)
        x = jax.random.normal(ks[0], (B, S, D_MODEL), dtype=jnp.float32)
        sc = 1.0 / np.sqrt(D_MODEL)
        return {'query_sequences': x, 'key_sequences': x, 'value_sequences': x, 'key_value_sequence_lengths': jax.random.randint(ks[1], (B,), 1, S + 1), 'ln_g': jnp.ones((D_MODEL,), jnp.float32), 'ln_b': jnp.zeros((D_MODEL,), jnp.float32), 'Wq': jax.random.normal(ks[2], (D_MODEL, N_HEADS * D_Q), jnp.float32) * sc, 'bq': jnp.zeros((N_HEADS * D_Q,), jnp.float32), 'Wk': jax.random.normal(ks[3], (D_MODEL, N_HEADS * D_Q), jnp.float32) * sc, 'bk': jnp.zeros((N_HEADS * D_Q,), jnp.float32), 'Wv': jax.random.normal(ks[4], (D_MODEL, N_HEADS * D_V), jnp.float32) * sc, 'bv': jnp.zeros((N_HEADS * D_V,), jnp.float32), 'Wo': jax.random.normal(ks[5], (N_HEADS * D_V, D_OUT), jnp.float32) * (1.0 / np.sqrt(N_HEADS * D_V)), 'bo': jnp.zeros((D_OUT,), jnp.float32)}
    _L1_xattn_all = _L1_xattn_setup()
    _L1_xattn_in = {k: v for k, v in _L1_xattn_all.items() if k in ('ln_g', 'ln_b', 'Wq', 'bq', 'Wk', 'bk', 'Wv', 'bv', 'Wo', 'bo')}
    del _L1_xattn_all

    def _L1_ffn_setup():
        import math
        import jax, jax.numpy as jnp
        import numpy as np
        B, L, D, F_FF, E = (4, 256, 128, 512, 8)
        TOP_K = 1
        CAPACITY_FACTOR = 1.25
        key = jax.random.key(seed)
        ks = jax.random.split(key, 4)
        h = jax.random.normal(ks[0], (B, L, D), dtype=jnp.float32)
        gate_w = jax.random.normal(ks[1], (E, D), dtype=jnp.float32) * 0.02
        gate_b = jnp.zeros((E,), dtype=jnp.float32)
        w1 = jax.random.normal(ks[2], (E, D, F_FF), dtype=jnp.float32) * 0.02
        b1 = jnp.zeros((E, F_FF), dtype=jnp.float32)
        w2 = jax.random.normal(ks[3], (E, F_FF, D), dtype=jnp.float32) * 0.02
        b2 = jnp.zeros((E, D), dtype=jnp.float32)
        return {'h': h, 'gate_w': gate_w, 'gate_b': gate_b, 'w1': w1, 'b1': b1, 'w2': w2, 'b2': b2}
    _L1_ffn_all = _L1_ffn_setup()
    _L1_ffn_in = {k: v for k, v in _L1_ffn_all.items() if k in ('gate_w', 'gate_b', 'w1', 'b1', 'w2', 'b2')}
    del _L1_ffn_all
    return {'x': x, 'ctx_1024': ctx_1024, '_lenS2': _lenS2, 'L0_xattn_q_w': _L0_xattn_in['q_w'], 'L0_xattn_q_b': _L0_xattn_in['q_b'], 'L0_xattn_k_w': _L0_xattn_in['k_w'], 'L0_xattn_k_b': _L0_xattn_in['k_b'], 'L0_xattn_v_w': _L0_xattn_in['v_w'], 'L0_xattn_v_b': _L0_xattn_in['v_b'], 'L0_xattn_o_w': _L0_xattn_in['o_w'], 'L0_xattn_o_b': _L0_xattn_in['o_b'], 'L0_ffn_w1': _L0_ffn_in['w1'], 'L0_ffn_b1': _L0_ffn_in['b1'], 'L0_ffn_w2': _L0_ffn_in['w2'], 'L0_ffn_b2': _L0_ffn_in['b2'], 'L1_xattn_ln_g': _L1_xattn_in['ln_g'], 'L1_xattn_ln_b': _L1_xattn_in['ln_b'], 'L1_xattn_Wq': _L1_xattn_in['Wq'], 'L1_xattn_bq': _L1_xattn_in['bq'], 'L1_xattn_Wk': _L1_xattn_in['Wk'], 'L1_xattn_bk': _L1_xattn_in['bk'], 'L1_xattn_Wv': _L1_xattn_in['Wv'], 'L1_xattn_bv': _L1_xattn_in['bv'], 'L1_xattn_Wo': _L1_xattn_in['Wo'], 'L1_xattn_bo': _L1_xattn_in['bo'], 'L1_ffn_gate_w': _L1_ffn_in['gate_w'], 'L1_ffn_gate_b': _L1_ffn_in['gate_b'], 'L1_ffn_w1': _L1_ffn_in['w1'], 'L1_ffn_b1': _L1_ffn_in['b1'], 'L1_ffn_w2': _L1_ffn_in['w2'], 'L1_ffn_b2': _L1_ffn_in['b2']}

def reference(x, ctx_1024, _lenS2, L0_xattn_q_w, L0_xattn_q_b, L0_xattn_k_w, L0_xattn_k_b, L0_xattn_v_w, L0_xattn_v_b, L0_xattn_o_w, L0_xattn_o_b, L0_ffn_w1, L0_ffn_b1, L0_ffn_w2, L0_ffn_b2, L1_xattn_ln_g, L1_xattn_ln_b, L1_xattn_Wq, L1_xattn_bq, L1_xattn_Wk, L1_xattn_bk, L1_xattn_Wv, L1_xattn_bv, L1_xattn_Wo, L1_xattn_bo, L1_ffn_gate_w, L1_ffn_gate_b, L1_ffn_w1, L1_ffn_b1, L1_ffn_w2, L1_ffn_b2):
    import jax
    import jax.numpy as jnp

    def _L0_xattn_ref(query, key, value, q_w, q_b, k_w, k_b, v_w, v_b, o_w, o_b):
        import jax, jax.numpy as jnp
        import numpy as np
        EMBED_DIM = 128
        NUM_HEADS = 16
        HEAD_DIM = EMBED_DIM // NUM_HEADS
        SCALE = HEAD_DIM ** (-0.5)

        def _split_heads(x, B):
            return x.reshape(B, -1, NUM_HEADS, HEAD_DIM).transpose(0, 2, 1, 3)
        B = query.shape[0]
        q = _split_heads(query @ q_w + q_b, B)
        k = _split_heads(key @ k_w + k_b, B)
        v = _split_heads(value @ v_w + v_b, B)
        scores = jnp.einsum('bhqd,bhkd->bhqk', q, k) * SCALE
        attn = jax.nn.softmax(scores, axis=-1)
        out = jnp.einsum('bhqk,bhkd->bhqd', attn, v)
        out = out.transpose(0, 2, 1, 3).reshape(B, -1, EMBED_DIM)
        return out @ o_w + o_b

    def _L0_ffn_ref(x, w1, b1, w2, b2):
        import jax, jax.numpy as jnp
        import numpy as np
        EPS = 1e-05

        def rmsnorm(x):
            return x * jax.lax.rsqrt(jnp.mean(x * x, axis=-1, keepdims=True) + EPS)

        def act_quant(x):
            scale = 127.0 / jnp.clip(jnp.max(jnp.abs(x), axis=-1, keepdims=True), 1e-05)
            q = jnp.clip(jnp.round(x * scale), -128.0, 127.0) / scale
            return x + jax.lax.stop_gradient(q - x)

        def weight_quant(w):
            scale = 1.0 / jnp.clip(jnp.mean(jnp.abs(w)), 1e-05)
            q = jnp.clip(jnp.round(w * scale), -1.0, 1.0) / scale
            return w + jax.lax.stop_gradient(q - w)

        def bitlinear(x, w, b):
            xq = act_quant(rmsnorm(x))
            wq = weight_quant(w)
            return jnp.einsum('bsd,fd->bsf', xq, wq) + b
        h = bitlinear(x, w1, b1)
        h = jax.nn.gelu(h, approximate=False)
        return bitlinear(h, w2, b2)

    def _L1_xattn_ref(query_sequences, key_sequences, value_sequences, key_value_sequence_lengths, ln_g, ln_b, Wq, bq, Wk, bk, Wv, bv, Wo, bo):
        import jax, jax.numpy as jnp
        import numpy as np
        D_MODEL = 128
        N_HEADS = 16
        D_Q = 64
        D_V = 64
        D_OUT = 128
        B, S = (4, 256)

        def _layer_norm(x, g, b, eps=1e-05):
            mu = jnp.mean(x, axis=-1, keepdims=True)
            var = jnp.mean((x - mu) ** 2, axis=-1, keepdims=True)
            return (x - mu) * jax.lax.rsqrt(var + eps) * g + b

        def _rope(x, theta=10000.0):
            D = x.shape[-1]
            inv_freq = 1.0 / theta ** (jnp.arange(0, D, 2, dtype=jnp.float32) / D)
            t = jnp.arange(x.shape[-2], dtype=jnp.float32)
            freqs = t[:, None] * inv_freq[None, :]
            freqs = jnp.repeat(freqs, 2, axis=-1)
            cos, sin = (jnp.cos(freqs), jnp.sin(freqs))
            x1, x2 = (x[..., 0::2], x[..., 1::2])
            rot = jnp.stack([-x2, x1], axis=-1).reshape(x.shape)
            return x * cos + rot * sin
        b, sq, _ = query_sequences.shape
        sk = key_sequences.shape[1]
        q_in = _layer_norm(query_sequences, ln_g, ln_b)
        k_in = _layer_norm(key_sequences, ln_g, ln_b)
        v_in = _layer_norm(value_sequences, ln_g, ln_b)
        q = (q_in @ Wq + bq).reshape(b, sq, N_HEADS, D_Q).transpose(0, 2, 1, 3)
        k = (k_in @ Wk + bk).reshape(b, sk, N_HEADS, D_Q).transpose(0, 2, 1, 3)
        v = (v_in @ Wv + bv).reshape(b, sk, N_HEADS, D_V).transpose(0, 2, 1, 3)
        q = _rope(q)
        k = _rope(k)
        scores = jnp.einsum('bhqd,bhkd->bhqk', q, k) * (1.0 / np.sqrt(D_Q))
        valid = jnp.arange(sk)[None, :] < key_value_sequence_lengths[:, None]
        scores = jnp.where(valid[:, None, None, :], scores, -jnp.inf)
        attn = jax.nn.softmax(scores, axis=-1)
        out = jnp.einsum('bhqk,bhkd->bhqd', attn, v)
        out = out.transpose(0, 2, 1, 3).reshape(b, sq, N_HEADS * D_V)
        return out @ Wo + bo

    def _L1_ffn_ref(h, gate_w, gate_b, w1, b1, w2, b2):
        import math
        import jax, jax.numpy as jnp
        import numpy as np
        B, L, D, F_FF, E = (4, 256, 128, 512, 8)
        TOP_K = 1
        CAPACITY_FACTOR = 1.25
        Bh, Lh, Dh = h.shape
        T = Bh * Lh
        capacity = max(1, math.ceil(CAPACITY_FACTOR * (T * TOP_K / E)))
        x = h.reshape(T, Dh)
        logits = x @ gate_w.T + gate_b
        probs = jax.nn.softmax(logits, axis=-1)
        idx = jnp.argmax(probs, axis=-1)
        top_prob = jnp.max(probs, axis=-1)
        one_hot = jax.nn.one_hot(idx, E, dtype=jnp.int32)
        pos = jnp.take_along_axis(jnp.cumsum(one_hot, axis=0), idx[:, None], axis=1)[:, 0] - 1
        keep = pos < capacity
        safe_pos = jnp.where(keep, pos, 0)
        buf = jnp.zeros((E, capacity, Dh), dtype=x.dtype)
        buf = buf.at[idx, safe_pos].add(x * keep[:, None].astype(x.dtype))
        hdn = jax.nn.relu(jnp.einsum('ecd,edf->ecf', buf, w1) + b1[:, None, :])
        eout = jnp.einsum('ecf,efd->ecd', hdn, w2) + b2[:, None, :]
        gathered = eout[idx, safe_pos]
        out = gathered * (top_prob * keep.astype(x.dtype))[:, None]
        return out.reshape(Bh, Lh, Dh)
    x = x + _L0_xattn_ref(_layernorm(x, axis=-1), ctx_1024, ctx_1024, L0_xattn_q_w, L0_xattn_q_b, L0_xattn_k_w, L0_xattn_k_b, L0_xattn_v_w, L0_xattn_v_b, L0_xattn_o_w, L0_xattn_o_b)
    x = x + _L0_ffn_ref(_layernorm(x, axis=-1), L0_ffn_w1, L0_ffn_b1, L0_ffn_w2, L0_ffn_b2)
    x = x + _L1_xattn_ref(_layernorm(x, axis=-1), ctx_1024, ctx_1024, _lenS2, L1_xattn_ln_g, L1_xattn_ln_b, L1_xattn_Wq, L1_xattn_bq, L1_xattn_Wk, L1_xattn_bk, L1_xattn_Wv, L1_xattn_bv, L1_xattn_Wo, L1_xattn_bo)
    x = x + _L1_ffn_ref(_layernorm(x, axis=-1), L1_ffn_gate_w, L1_ffn_gate_b, L1_ffn_w1, L1_ffn_b1, L1_ffn_w2, L1_ffn_b2)
    return x

_drawn_inputs = setup_inputs


def setup_inputs(seed=0):
    import zlib

    import numpy as np

    out = dict(_drawn_inputs(seed))
    spreads = {'L0_xattn_q_b': (0.0, 0.382),
     'L0_xattn_k_b': (0.0, 0.8),
     'L0_xattn_v_b': (0.0, 0.1),
     'L0_xattn_o_b': (0.0, 0.1),
     'L0_ffn_b1': (0.0, 0.1),
     'L0_ffn_b2': (0.0, 0.1),
     'L1_xattn_ln_g': (1.0, 0.2),
     'L1_xattn_ln_b': (0.0, 0.1),
     'L1_xattn_bq': (0.0, 0.623),
     'L1_xattn_bk': (0.0, 0.8),
     'L1_xattn_bv': (0.0, 0.1),
     'L1_xattn_bo': (0.0, 0.1),
     'L1_ffn_gate_b': (0.0, 0.8),
     'L1_ffn_b1': (0.0, 0.8),
     'L1_ffn_b2': (0.0, 0.73)}
    factors = {'L1_ffn_gate_w': 4.177, 'L1_ffn_w1': 8.0, 'L1_ffn_w2': 6.762}
    for name, (base, spread) in spreads.items():
        noise = np.random.default_rng([zlib.crc32(name.encode()), seed]).standard_normal(out[name].shape)
        drawn = base * np.exp(spread * noise) if base else spread * noise
        out[name] = jnp.asarray(drawn.astype(out[name].dtype))
    for name, factor in factors.items():
        out[name] = (out[name] * factor).astype(out[name].dtype)
    return out
```

```python
from contextlib import ExitStack

import numpy as np

import concourse.bass as bass
from concourse import mybir

ALU = mybir.AluOpType
ACT = mybir.ActivationFunctionType
AX = mybir.AxisListType.X
F32 = mybir.dt.float32
BF16 = mybir.dt.bfloat16
I32 = mybir.dt.int32
U32 = mybir.dt.uint32

B = 16
T = 128
D = 128
KEYS = 77
H = 16
DH0, DH1 = 8, 64
F = 512
E = 8
CAP = 320
ROWS = E * CAP
EPS = 1e-5
MAGIC = 12582912.0
MASKED = -1e30


class Step:

    def __init__(self, i, p, lo):
        self.i, self.p, self.lo = i, p, lo

    def next(self, k=1):
        return Step(self.i + k, (self.p + k) % 2, self.lo + k)


def run_steps(eng, step, first, last, head, tail):
    start, stop = first + head, last + 1 - tail
    assert (stop - start) % 2 == 0
    for i in range(first, start):
        step(Step(i, i % 2, i), last)
    with eng.Fori(0, (stop - start) // 2) as r:
        step(Step(r * 2 + start, start % 2, start), last)
        step(Step(r * 2 + (start + 1), (start + 1) % 2, start + 1), last)
    for i in range(stop, last + 1):
        step(Step(i, i % 2, i), last)


def tile_at(t, i, width):
    return t[:, bass.ts(i, width)]


class Store:

    def __init__(self, nc, ctx):
        self.nc, self.ctx, self.sems = nc, ctx, {}

    def sb(self, name, shape, dt=F32):
        return self.ctx.enter_context(self.nc.sbuf_tensor(name, shape, dt))

    def sem(self, name):
        if name not in self.sems:
            self.sems[name] = self.ctx.enter_context(self.nc.semaphore(name))
        return self.sems[name]


def setup(nc, S, A):
    loads = [
        ("eye", S.eye[:, :], A["c_eye"]),
        ("x", S.x[:, :].rearrange("t (b d) -> t b d", d=D), A["x"].rearrange("b t d -> t b d")),
        ("wq0", S.wq0[:, :], A["L0_xattn_q_w"]), ("wk0", S.wk0[:, :], A["L0_xattn_k_w"]),
        ("wv0", S.wv0[:, :], A["L0_xattn_v_w"]), ("wo0", S.wo0[:, :], A["L0_xattn_o_w"]),
        ("cols", S.cols[:, 0:1], A["L0_xattn_q_b"].rearrange("(p a) -> p a", a=1)),
        ("cols", S.cols[:, 1:2], A["L0_xattn_k_b"].rearrange("(p a) -> p a", a=1)),
        ("cols", S.cols[:, 2:3], A["L0_xattn_v_b"].rearrange("(p a) -> p a", a=1)),
        ("cols", S.cols[:, 3:4], A["L1_xattn_ln_g"].rearrange("(p a) -> p a", a=1)),
        ("cols", S.cols[:, 4:5], A["L1_xattn_ln_b"].rearrange("(p a) -> p a", a=1)),
        ("cols", S.bvcol[:, :], A["L1_xattn_bv"].rearrange("(j p) -> p j", p=D)),
        ("rows", S.row_o[:, 0, :], A["L0_xattn_o_b"].rearrange("(a n) -> a n", a=1)),
        ("rows", S.row_o[:, 1, :], A["L1_xattn_bo"].rearrange("(a n) -> a n", a=1)),
        ("slotmask", S.slotmask[:, :], A["c_slotmask"]),
        ("negsel32", S.negsel32[:, :, :], A["c_negsel"]),
        ("len", S.len_i[:, :], A["_lenS2"].rearrange("(a n) -> a n", a=1).to_broadcast([D, B])),
        ("w1n", S.w1n[:, :, :], A["L0_ffn_w1"].rearrange("(c p) d -> p c d", p=D)),
        ("w2n", S.w2n[:, :], A["L0_ffn_w2"]),
        ("b1bc", S.b1bc[:, :], A["L0_ffn_b1"].rearrange("(a n) -> a n", a=1).to_broadcast([D, F])),
        ("b2bc", S.b2bc[:, :], A["L0_ffn_b2"].rearrange("(a n) -> a n", a=1).to_broadcast([D, D])),
        ("bias8", S.bias8[:, 0, :], A["L1_xattn_bq"].rearrange("(p j) -> p j", p=D)),
        ("bias8", S.bias8[:, 1, :], A["L1_xattn_bk"].rearrange("(p j) -> p j", p=D)),
        ("kpos", S.kpos[:, :], A["c_kpos"]),
        ("krow", S.krow[:, :], A["c_krow"]),
        ("wq1", S.wq1[:, :], A["L1_xattn_Wq"]), ("wk1", S.wk1[:, :], A["L1_xattn_Wk"]),
        ("wv1", S.wv1[:, :], A["L1_xattn_Wv"]),
        ("wo1", S.wo1[:, :, :], A["L1_xattn_Wo"].rearrange("(j p) n -> p j n", p=D)),
        ("rope", S.cosq[:, :], A["c_cosq"]), ("rope", S.sinq[:, :], A["c_sinq"]),
        ("rope", S.cosk[:, :], A["c_cosk"]), ("rope", S.sink[:, :], A["c_sink"]),
        ("gate", S.gate_w[:, :], A["L1_ffn_gate_w"]),
        ("gate", S.gate_b[:, :], A["L1_ffn_gate_b"].rearrange("(a n) -> a n", a=1)),
        ("moec", S.upto32[:, :], A["c_upto"]), ("moec", S.experts[:, :], A["c_experts"]),
        ("moec", S.dropped_row[:, :], A["c_dropped"]),
    ]
    total = {}
    for name, _, _ in loads:
        total[name] = total.get(name, 0) + 16

    def loaded(eng, *names):
        for n in names:
            eng.wait_ge(S.sem("ld_" + n), total[n])

    for n in total:
        S.sem("ld_" + n)
    zero_done, cast, quant, ps, rotk, split = (S.sem(n) for n in ("zeros", "cast", "quant", "set_pe", "rotk", "split"))
    zero_rows, rows3, step_v, step_g, evac = (S.sem(n) for n in ("zero_rows", "rows3", "set_v", "set_g", "set_act"))
    bank = S.bank

    with nc.Block() as block:
        @block.sync
        def _(sp):
            for name, dst, src in loads:
                sp.dma_start(dst, src, allow_slow_non_contiguous=True).then_inc(S.sem("ld_" + name), 16)
            sp.wait_ge(zero_done, 1)
            sp.dma_start(S.dispatch[0:ROWS, :].rearrange("(p n) d -> p (n d)", p=D), S.zeros[:, :]).then_inc(zero_rows, 16)
            sp.wait_ge(split, 6)
            for which in range(3):
                for part in range(3):
                    sp.dma_start(S.bias3[part:part + 1, which, :], S.parts[:, part, which, :]).then_inc(rows3, 16)
            sp.wait_ge(rows3, 9 * 16)
            sp.wait_ge(zero_rows, 16)

        @block.gpsimd
        def _(g):
            nc.gpsimd.memset(S.minus_half[:, :], -0.5)
            nc.gpsimd.memset(S.zeros[:, :], 0.0).then_inc(zero_done, 1)
            loaded(g, "wk1")
            even = S.wk1[:, :].rearrange("d (n two) -> d n two", two=2)
            rot = S.wk1r[:, :].rearrange("d (n two) -> d n two", two=2)
            nc.gpsimd.tensor_scalar(rot[:, :, 0], even[:, :, 1], -1.0, None, ALU.mult)
            nc.gpsimd.tensor_copy(rot[:, :, 1], even[:, :, 0])
            g.wait_ge(step_v, 1)
            loaded(g, "krow")
            nc.gpsimd.tensor_tensor(S.maskrow32[:, :, :], S.len_f[0:1, :].unsqueeze(2).to_broadcast([1, B, KEYS]),
                                    S.krow[:, :].unsqueeze(1).to_broadcast([1, B, KEYS]), ALU.subtract).then_inc(step_g, 1)
            g.wait_ge(step_g, 1)
            for s in range(4):
                nc.gpsimd.tensor_scalar(S.maskrow[:, :].rearrange("a (b s k) -> a b s k", b=B, s=4)[:, :, s, :],
                                        S.maskrow32[:, :, :], 0.0, MASKED, ALU.is_le, ALU.mult)

        @block.vector
        def _(v):
            loaded(v, "len")
            nc.vector.tensor_copy(S.len_f[:, :], S.len_i[:, :]).then_inc(step_v, 1)
            for p in range(2):
                nc.vector.memset(S.vaug[0][:, p, :, :], 1.0)
                nc.vector.memset(S.vaug[1][:, p, :, :], 1.0)
            nc.vector.memset(S.ones_row[:, :], 1.0).then_inc(cast, 1)
            nc.vector.memset(S.ones_bf[:, :], 1.0).then_inc(cast, 1)
            nc.vector.memset(S.ones_mean[:, :], 1.0 / (F * D)).then_inc(cast, 1)
            nc.vector.memset(S.count[:, :, :], 0.0)
            nc.vector.memset(S.varx[:, :, :], 1.0)
            nc.vector.memset(S.minus_magic[:, :], -MAGIC)
            loaded(v, "eye", "negsel32", "moec")
            nc.vector.tensor_copy(S.eye_bf[:, :], S.eye[:, :]).then_inc(cast, 1)
            nc.vector.tensor_copy(S.negsel[:, :, :], S.negsel32[:, :, :])
            nc.vector.memset(S.rowmax[0][:, :, :], 0.0)
            nc.vector.memset(S.rowmax[1][:, :, :], 0.0)
            nc.vector.tensor_copy(S.upto[:, :], S.upto32[:, :])
            loaded(v, "bias8")
            kb = S.bias8[:, 1, :].rearrange("p (n two) -> p n two", two=2)
            kr = S.bias8[:, 2, :].rearrange("p (n two) -> p n two", two=2)
            nc.vector.tensor_scalar(kr[:, :, 0], kb[:, :, 1], -1.0, None, ALU.mult).then_inc(split, 1)
            nc.vector.tensor_copy(kr[:, :, 1], kb[:, :, 0]).then_inc(split, 1)
            v.wait_ge(split, 2)
            nc.vector.tensor_copy(S.parts[:, 0, :, :], S.bias8[:, :, :]).then_inc(split, 1)
            v.wait_ge(split, 3)
            nc.vector.tensor_tensor(S.bias8[:, :, :], S.bias8[:, :, :], S.parts[:, 0, :, :], ALU.subtract).then_inc(split, 1)
            v.wait_ge(split, 4)
            nc.vector.tensor_copy(S.parts[:, 1, :, :], S.bias8[:, :, :]).then_inc(split, 1)
            v.wait_ge(split, 5)
            nc.vector.tensor_tensor(S.parts[:, 2, :, :], S.bias8[:, :, :], S.parts[:, 1, :, :], ALU.subtract).then_inc(split, 1)
            v.wait_ge(step_v, 1)
            loaded(v, "kpos")
            nc.vector.tensor_scalar(S.maskcol[:, :], S.len_f[:, :], S.kpos[:, 0:1], MASKED, ALU.is_le, ALU.mult)
            loaded(v, "w1n", "w2n")
            nc.vector.tensor_reduce(S.wabs[:, 0:1], S.w1n[:, :, :].rearrange("p c d -> p (c d)"), AX, ALU.add,
                                    apply_absolute_value=True).then_inc(quant, 1)
            nc.vector.tensor_reduce(S.wabs[:, 1:2], S.w2n[:, :], AX, ALU.add, apply_absolute_value=True).then_inc(quant, 1)
            v.wait_ge(ps, 1)
            nc.vector.tensor_scalar(S.wmean[:, :], bank[0][:, 0:2], EPS, None, ALU.max).then_inc(quant, 1)
            v.wait_ge(quant, 3)
            nc.vector.reciprocal(S.wscale[:, :], S.wmean[:, :]).then_inc(quant, 1)
            nc.vector.tensor_scalar(S.wmean127[:, :], S.wmean[:, :], 1.0 / 127.0, None, ALU.mult)
            v.wait_ge(quant, 4)
            w1f, w2f = S.w1n[:, :, :].rearrange("p c d -> p (c d)"), S.w2n[:, :]
            n = 4
            for k, (w, wb) in enumerate(((w1f, S.w1t), (w2f, S.w2t))):
                nc.vector.tensor_scalar(w, w, S.wscale[:, k:k + 1], MAGIC, ALU.mult, ALU.add).then_inc(quant, 1)
                n += 1
                v.wait_ge(quant, n)
                nc.vector.tensor_scalar(w, w, -MAGIC, 1.0, ALU.add, ALU.min).then_inc(quant, 1)
                n += 1
                v.wait_ge(quant, n)
                nc.vector.tensor_scalar(wb[:, :], w, -1.0, None, ALU.max).then_inc(quant, 1)
                n += 1
            v.wait_ge(ps, 4)
            loaded(v, "rows")
            nc.vector.tensor_tensor(S.row_o[:, 0, :], bank[1][0:1, 0:D], S.row_o[:, 0, :], ALU.add)
            nc.vector.tensor_tensor(S.row_o[:, 1, :], bank[1][0:1, D:2 * D], S.row_o[:, 1, :], ALU.add)

        @block.tensor
        def _(pe):
            pe.wait_ge(cast, 4)
            pe.wait_ge(quant, 2)
            nc.tensor.matmul(bank[0][:, 0:2], S.ones_mean[:, :], S.wabs[:, :], start=True, stop=True).then_inc(ps, 1)
            pe.wait_ge(quant, 10)
            for k, (wb, b) in enumerate(((S.w1t, 2), (S.w2t, 3))):
                for c in range(F // D):
                    mm = nc.tensor.transpose(S.bank_bf[b][:, c * D:(c + 1) * D], wb[:, c * D:(c + 1) * D], S.eye_bf[:, :])
                mm.then_inc(ps, 1)
            loaded(pe, "cols", "wo0", "wo1", "gate", "eye")
            nc.tensor.matmul(bank[1][0:1, 0:D], S.cols[:, 2:3], S.wo0[:, :], start=True, stop=True)
            for j in range(H * DH1 // D):
                mm = nc.tensor.matmul(bank[1][0:1, D:2 * D], S.bvcol[:, j:j + 1], S.wo1[:, j, :],
                                      start=(j == 0), stop=(j == 7))
            mm.then_inc(ps, 1)
            nc.tensor.transpose(bank[4][:, 0:E], S.gate_w[:, :], S.eye[0:E, 0:E]).then_inc(ps, 1)

        @block.scalar
        def _(act):
            act.wait_ge(ps, 2)
            nc.scalar.copy(S.w1q[:, :], S.bank_bf[2][:, 0:F])
            act.wait_ge(ps, 3)
            nc.scalar.copy(S.w2q[:, :], S.bank_bf[3][:, 0:F])
            act.wait_ge(ps, 5)
            nc.scalar.copy(S.gate_t[:, :], bank[4][:, 0:E]).then_inc(evac, 1)


def normalise_steps(nc, S, v, L, n):
    ln, ln_pow, xn_ready = S.sem(f"ln{L}"), S.sem(f"ln_pow{L}"), S.sem(f"xn_ready{L}")
    i, p = n.i, n.p
    parts = 2 if L == 1 else 1
    per = 3 * parts

    def statistics():
        if L == 1:
            v.wait_ge(S.sem(f"ctx_in{L}_{p}"), i * 8 + (16 - 8 * p))
            nc.vector.memset(S.fence[:, :], 0.0)
            nc.vector.bn_stats(S.stats[0:KEYS, p, 1, :], S.ctx_in[:, p, :]).then_inc(ln, 1)
        nc.vector.bn_stats(S.stats[:, p, 0, :], tile_at(S.x, i, D)).then_inc(ln, 1)
        v.wait_ge(ln, i * per + parts)
        nc.vector.memset(S.fence[:, :], 0.0)
        nc.vector.bn_aggr(S.meanvar[:, p, 0, :], S.stats[:, p, 0, :]).then_inc(ln, 1)
        if L == 1:
            nc.vector.bn_aggr(S.meanvar[0:KEYS, p, 1, :], S.stats[0:KEYS, p, 1, :]).then_inc(ln, 1)
        v.wait_ge(ln, i * per + 2 * parts)
        if L == 0:
            nc.vector.tensor_scalar(S.varx[:, p, 0:1], S.meanvar[:, p, 0, 1:2], EPS, None, ALU.add).then_inc(ln, 1)
        else:
            nc.vector.tensor_scalar(S.varx[0:KEYS, p, 1:2], S.meanvar[0:KEYS, p, 1, 1:2], EPS, None, ALU.add).then_inc(ln, 1)
            nc.vector.tensor_scalar(S.varx[:, p, 0:1], S.meanvar[:, p, 0, 1:2], 1.0 + EPS, EPS * EPS,
                                    ALU.mult, ALU.add).then_inc(ln, 1)

    def scale():
        v.wait_ge(ln_pow, i + 1)
        if L == 1:
            nc.vector.tensor_scalar(S.cn[:, p, :], S.ctx_in[:, p, :], S.meanvar[0:KEYS, p, 1, 0:1], S.rstd[0:KEYS, p, 1:2],
                                    ALU.subtract, ALU.mult)
        nc.vector.tensor_scalar(S.xn[:, p, :], tile_at(S.x, i, D), S.meanvar[:, p, 0, 0:1], S.rstd[:, p, 0:1],
                                ALU.subtract, ALU.mult).then_inc(xn_ready, 1)

    return statistics, scale


def attention(nc, S, A, L):
    dh = DH1 if L else DH0
    tiles = H * dh // D
    scale = float(dh) ** -0.5
    bank = S.bank
    ST, SM, PV, M0, M1 = (0, 1), (2, 3), (4, 5), bank[6], bank[7]
    xT, cT, qT, vaug, attn, attnT = S.xT, S.cT, S.qT[L], S.vaug[L], S.attn[L], S.attnT
    kT = S.kT[L]
    last = B - 1

    def sem(n):
        return S.sem(f"{n}{L}")

    xn_ready, a1_done, a1_out = sem("xn_ready"), sem("a1_done"), sem("a1_out")
    m1_done, m1_out, sm_done, mx_out = sem("m1_done"), sem("m1_out"), sem("sm_done"), sem("mx_out")
    mt_done, mt_out, st_done, ex_out = sem("mt_done"), sem("mt_out"), sem("st_done"), sem("ex_out")
    pv_done, pve_out, pv_rec, ta_done, ta_out = sem("pv_done"), sem("pve_out"), sem("pv_rec"), sem("ta_done"), sem("ta_out")
    o_done, o_out, k_ready, q_ready = sem("o_done"), sem("o_out"), sem("k_ready"), sem("q_ready")
    v_done, v_out, tq_done, tq_out, mcol_out = sem("v_done"), sem("v_out"), sem("tq_done"), sem("tq_out"), sem("mcol_out")
    ln, ln_pow, ctx_used = sem("ln"), sem("ln_pow"), sem("ctx_used")
    ctx_in = [S.sem(f"ctx_in{L}_{p}") for p in range(2)]
    M1_USES = 6 if L else 1
    TQ = 2 * L

    def head(half, c, s):
        return 8 * half + (2 * s + c if L else 4 * c + s)

    def q_rows(h):
        return slice(64 * (h % 2), 64 * (h % 2) + 64) if L else slice(32 * (h // 4), 32 * (h // 4) + 32)

    def max_cols(t, half, c):
        if L:
            return t[:, 64 * c + 4 * half:64 * c + 4 * half + 4]
        return t[:, 32 * (2 * half + c):32 * (2 * half + c) + 4]

    def head_cols(t, half, c):
        return t[:, 8 * half + c:8 * half + 8:2] if L else t[:, 8 * half + 4 * c:8 * half + 4 * c + 4]

    with nc.Block() as block:
        @block.sync
        def _(sp):
            def load(n, _):
                if n.lo >= 2:
                    if L:
                        sp.wait_ge(xn_ready, n.i - 1)
                    else:
                        sp.wait_ge(a1_done, n.i - 1)
                sp.dma_start(S.ctx_in[:, n.p, :], A["ctx_1024"][bass.ds(n.i, 1)].rearrange("b k d -> k (b d)")
                             ).then_inc(ctx_in[n.p], 16)
            run_steps(sp, load, 0, last, 2, 0)

        @block.gpsimd
        def _(g):
            def step(s, _):
                n, n2 = s.next(), s.next(2)
                if n2.lo <= last:
                    g.wait_ge(ln, n2.i * (3 + 3 * L) + (3 + 3 * L))
                    nc.gpsimd.tensor_tensor(S.rstd[:, n2.p, 0:1 + L], S.varx[:, n2.p, 0:1 + L], S.minus_half[:, 0:1 + L],
                                            ALU.pow).then_inc(ln_pow, 1)
                if not 0 <= n.lo <= last:
                    return
                if L == 0:
                    g.wait_ge(m1_out, n.i * 2 + 1)
                    nc.gpsimd.tensor_tensor(S.kmask[:, n.p, :, :], kT[:, n.p, :].unsqueeze(1).to_broadcast([D, 4, KEYS]),
                                            S.slotmask[:, :].unsqueeze(2).to_broadcast([D, 4, KEYS]), ALU.mult).then_inc(k_ready, 1)
                else:
                    for c in range(2):
                        g.wait_ge(m1_out, n.i * 6 + (c + 1))
                        nc.gpsimd.tensor_tensor(S.qrot[:, c, :], S.qcos[:, c, :], S.qsin[:, c, :], ALU.add).then_inc(q_ready, 1)
                    for c in range(2):
                        g.wait_ge(m1_out, n.i * 6 + (2 * c + 4))
                        nc.gpsimd.tensor_tensor(kT[:, n.p, 4 * c:4 * c + 4, :], S.kcos[:, c, :, :], S.ksin[:, c, :, :],
                                                ALU.add).then_inc(k_ready, 1)
            run_steps(g, step, -2, last, 3, 3)

        @block.vector
        def _(v):
            def evacuate_qkv(n):
                v.wait_ge(m1_done, n.i + 1)
                nc.vector.tensor_scalar(qT[:, n.p, :], M1[:, 0:D], S.cols[:, 0:1], None, ALU.add)
                nc.vector.tensor_scalar(kT[:, n.p, :], M1[:, D:D + KEYS], S.cols[:, 1:2], None, ALU.add).then_inc(m1_out, 1)
                nc.vector.tensor_copy(vaug[:, n.p, :, 0:dh], M1[0:KEYS, 256:256 + D].rearrange("k (h d) -> k h d", h=H)
                                      ).then_inc(m1_out, 1)

            def rotate_q(n, c):
                v.wait_ge(m1_done, n.i * 6 + (c + 1))
                ps = M1[:, 0:512].rearrange("t (h d) -> t h d", h=8)
                pair = M1[:, 0:512].rearrange("t (h n two) -> t h n two", h=8, two=2)
                qs = S.qsin[:, c, :].rearrange("t (h n two) -> t h n two", h=8, two=2)
                sn = S.sinq[:, :].rearrange("t (n two) -> t n two", two=2)
                nc.vector.tensor_tensor(S.qcos[:, c, :].rearrange("t (h d) -> t h d", h=8), ps,
                                        S.cosq[:, :].unsqueeze(1).to_broadcast([T, 8, DH1]), ALU.mult)
                nc.vector.tensor_tensor(qs[:, :, :, 0], pair[:, :, :, 1],
                                        sn[:, :, 0].unsqueeze(1).to_broadcast([T, 8, DH1 // 2]), ALU.mult)
                nc.vector.tensor_tensor(qs[:, :, :, 1], pair[:, :, :, 0],
                                        sn[:, :, 1].unsqueeze(1).to_broadcast([T, 8, DH1 // 2]), ALU.mult).then_inc(m1_out, 1)

            def rotate_k(n, c, rotated):
                v.wait_ge(m1_done, n.i * 6 + (3 + 2 * c + rotated))
                out, table = (S.ksin, S.sink) if rotated else (S.kcos, S.cosk)
                nc.vector.tensor_tensor(out[:, c, :, :], M1[:, 0:4 * KEYS].rearrange("d (j k) -> d j k", j=4),
                                        table[:, :].unsqueeze(1).to_broadcast([D, 4, KEYS]), ALU.mult).then_inc(m1_out, 1)

            def divide(s, half):
                for c in range(2):
                    v.wait_ge(pv_done, s.i * 4 + (2 * half + c + 1))
                    pvb = bank[PV[c]][:, 0:4 * (dh + 1)].rearrange("t (s d) -> t s d", s=4)
                    nc.vector.reciprocal(S.recip[:, c, :], pvb[:, :, dh]).then_inc(pv_rec, 1)
                    v.wait_ge(pv_rec, s.i * 4 + (2 * half + c + 1))
                    nc.vector.tensor_tensor(head_cols(attn[:, s.p, :].rearrange("t (h d) -> t h d", h=H), half, c), pvb[:, :, 0:dh],
                                            S.recip[:, c, :].unsqueeze(2).to_broadcast([T, 4, dh]), ALU.mult).then_inc(pve_out, 1)

            def maximum(n, half):
                for c in range(2):
                    v.wait_ge(sm_done, n.i * 4 + (2 * half + c + 1))
                    nc.vector.tensor_reduce(max_cols(S.rowmax[L][:, n.p, :], half, c),
                                            bank[SM[c]][:, 0:4 * KEYS].rearrange("t (s k) -> t s k", s=4), AX, ALU.max
                                            ).then_inc(mx_out, 1)

            def step(s, _):
                n, n2 = s.next(), s.next(2)
                cur, nxt, nxt2 = s.lo >= 0, 0 <= n.lo <= last, n2.lo <= last
                statistics, normalise = normalise_steps(nc, S, v, L, n2)
                if nxt2:
                    statistics()
                if nxt and L:
                    nc.vector.tensor_copy(S.mcol[:, n.p:n.p + 1], S.maskcol[0:KEYS, bass.ds(n.i, 1)]).then_inc(mcol_out, 1)
                if nxt and L == 0:
                    evacuate_qkv(n)
                if nxt and L:
                    rotate_q(n, 0)
                    rotate_q(n, 1)
                if cur:
                    divide(s, 0)
                if nxt and L:
                    for c in range(2):
                        rotate_k(n, c, 0)
                        rotate_k(n, c, 1)
                if L and cur:
                    divide(s, 1)
                if nxt:
                    maximum(n, 0)
                if L == 0 and cur:
                    divide(s, 1)
                if nxt:
                    maximum(n, 1)
                if nxt2:
                    normalise()
                if cur:
                    v.wait_ge(o_done, s.i + 1)
                    nc.vector.tensor_tensor(tile_at(S.x, s.i, D), M1[:, 0:D], tile_at(S.x, s.i, D), ALU.add).then_inc(o_out, 1)
            run_steps(v, step, -2, last, 3, 3)

        @block.scalar
        def _(act):
            def exponent(s, half):
                for c in range(2):
                    act.wait_ge(st_done, s.i * 4 + (2 * half + c + 1))
                    if L == 0:
                        nc.scalar.activation(S.probs[:, half, c, :], bank[ST[c]][0:KEYS, :], ACT.Exp, scale=scale).then_inc(ex_out, 1)
                    else:
                        if half == 0 and c == 0:
                            act.wait_ge(mcol_out, s.i + 1)
                        nc.scalar.activation(S.probs[:, half, c, :], bank[ST[c]][0:KEYS, :], ACT.Exp, scale=scale,
                                             bias=S.mcol[:, s.p:s.p + 1]).then_inc(ex_out, 1)

            def step(s, _):
                n = s.next()
                cur, nxt = s.lo >= 0, n.lo <= last
                if nxt:
                    act.wait_ge(a1_done, n.i + 1)
                    if L == 0:
                        nc.scalar.copy(xT[:, n.p, :], M0[:, 0:D])
                        nc.scalar.copy(cT[:, n.p, :], M0[:, D:D + KEYS]).then_inc(a1_out, 1)
                    else:
                        nc.scalar.activation(xT[:, n.p, :], M0[:, 0:D], ACT.Identity, bias=S.cols[:, 4:5], scale=S.cols[:, 3:4])
                        nc.scalar.activation(cT[:, n.p, :], M0[:, D:D + KEYS], ACT.Identity, bias=S.cols[:, 4:5],
                                             scale=S.cols[:, 3:4]).then_inc(a1_out, 1)
                if cur:
                    exponent(s, 0)
                if nxt and L:
                    for c in range(2):
                        act.wait_ge(v_done, n.i * 2 + (c + 1))
                        nc.scalar.copy(vaug[:, n.p, 8 * c:8 * c + 8, 0:dh], M0[0:KEYS, :].rearrange("k (h d) -> k h d", h=8)
                                       ).then_inc(v_out, 1)
                if cur:
                    exponent(s, 1)
                if nxt and L:
                    for c in range(2):
                        act.wait_ge(tq_done, n.i * 2 + (c + 1))
                        nc.scalar.copy(qT[:, n.p, 4 * c:4 * c + 4, :].rearrange("d j t -> d (j t)"), M0[:, :]).then_inc(tq_out, 1)
                if cur:
                    for c in range(1 + L):
                        act.wait_ge(ta_done, s.i * (1 + L) + (c + 1))
                        w = min(tiles, 4)
                        nc.scalar.copy(attnT[:, 4 * c:4 * c + w, :].rearrange("d j t -> d (j t)"), M0[:, 0:w * T]).then_inc(ta_out, 1)
                if nxt:
                    act.wait_ge(mt_done, n.i + 1)
                    nc.scalar.copy(S.maxT[:, n.p, :], S.bank_bf[6][:, 0:T]).then_inc(mt_out, 1)
            run_steps(act, step, -1, last, 2, 3)

        @block.tensor
        def _(pe):
            def transpose_rows(n):
                pe.wait_ge(xn_ready, n.i + 1)
                if L == 0:
                    pe.wait_ge(ctx_in[n.p], n.i * 8 + (16 - 8 * n.p))
                if n.lo >= 1:
                    pe.wait_ge(mt_out, n.i)
                nc.tensor.transpose(M0[:, 0:D], S.xn[:, n.p, :], S.eye[:, :])
                c = S.cn if L else S.ctx_in
                nc.tensor.transpose(M0[:, D:D + KEYS], c[:, n.p, :], S.eye[0:KEYS, 0:KEYS]).then_inc(a1_done, 1)

            def m1_free(n):
                if n.lo >= 2:
                    pe.wait_ge(o_out, n.i - 1)
                elif n.lo == 1:
                    pe.wait_ge(m1_out, 6 if L else 2)

            def project_qkv(n):
                pe.wait_ge(a1_out, n.i + 1)
                m1_free(n)
                nc.tensor.matmul(M1[:, 0:D], S.wq0[:, :], xT[:, n.p, :], start=True, stop=True)
                nc.tensor.matmul(M1[:, D:D + KEYS], S.wk0[:, :], cT[:, n.p, :], start=True, stop=True)
                nc.tensor.matmul(M1[0:KEYS, 256:256 + D], cT[:, n.p, :], S.wv0[:, :], start=True, stop=True).then_inc(m1_done, 1)

            def project_q(n, c):
                if c == 0:
                    pe.wait_ge(a1_out, n.i + 1)
                    m1_free(n)
                else:
                    pe.wait_ge(m1_out, n.i * 6 + 1)
                nc.tensor.matmul(M1[:, :], S.ones_bf[0:3, :], S.bias3[:, 0, 512 * c:512 * c + 512], start=True, stop=False)
                nc.tensor.matmul(M1[:, :], xT[:, n.p, :], S.wq1[:, 512 * c:512 * c + 512], start=False, stop=True).then_inc(m1_done, 1)

            def project_v(n, c):
                if c:
                    pe.wait_ge(v_out, n.i * 2 + 1)
                nc.tensor.matmul(M0[0:KEYS, :], cT[:, n.p, :], S.wv1[:, 512 * c:512 * c + 512], start=True, stop=True).then_inc(v_done, 1)

            def project_k(n, c, rotated):
                pe.wait_ge(m1_out, n.i * 6 + (2 + 2 * c + rotated))
                w = S.wk1r if rotated else S.wk1
                for j in range(4):
                    cols = slice((4 * c + j) * D, (4 * c + j + 1) * D)
                    out = M1[:, j * KEYS:(j + 1) * KEYS]
                    nc.tensor.matmul(out, S.bias3[:, 1 + rotated, cols], S.ones_bf[0:3, 0:KEYS], start=True, stop=False)
                    mm = nc.tensor.matmul(out, w[:, cols], cT[:, n.p, :], start=False, stop=True)
                mm.then_inc(m1_done, 1)

            def transpose_q(n, c):
                pe.wait_ge(q_ready, n.i * 2 + (c + 1))
                if c == 0:
                    pe.wait_ge(v_out, n.i * 2 + 2)
                else:
                    pe.wait_ge(tq_out, n.i * 2 + 1)
                for j in range(4):
                    mm = nc.tensor.transpose(M0[:, j * T:(j + 1) * T], S.qrot[:, c, j * D:(j + 1) * D], S.eye[:, :])
                mm.then_inc(tq_done, 1)

            def scores_for_max(n, half):
                if half == 0:
                    if L:
                        pe.wait_ge(tq_out, n.i * 2 + 2)
                        pe.wait_ge(k_ready, n.i * 2 + 2)
                    else:
                        pe.wait_ge(k_ready, n.i + 1)
                if half or n.lo >= 1:
                    pe.wait_ge(mx_out, n.i * 4 + 2 * half)
                if L == 0:
                    for c in range(2):
                        rows = q_rows(head(half, c, 0))
                        nc.tensor.matmul(bank[SM[c]][:, 0:4 * KEYS], qT[rows, n.p, :],
                                         S.kmask[rows, n.p, :, :].rearrange("d s k -> d (s k)"), start=True, stop=True
                                         ).then_inc(sm_done, 1)
                    return
                for s4 in range(4):
                    for c in range(2):
                        h = head(half, c, s4)
                        nc.tensor.matmul(bank[SM[c]][:, s4 * KEYS:(s4 + 1) * KEYS], qT[q_rows(h), n.p, h // 2, :],
                                         kT[q_rows(h), n.p, h // 2, :], start=(s4 == 0), stop=False, skip_group_check=True)
                for c in range(2):
                    nc.tensor.matmul(bank[SM[c]][:, 0:4 * KEYS], S.ones_bf[0:1, :], tile_at(S.maskrow, n.i, 4 * KEYS),
                                     start=False, stop=True, skip_group_check=True).then_inc(sm_done, 1)

            def transpose_max(n):
                pe.wait_ge(mx_out, n.i * 4 + 4)
                if n.lo >= 1:
                    pe.wait_ge(ta_out, n.i * (1 + L))
                elif L:
                    pe.wait_ge(tq_out, 2)
                else:
                    pe.wait_ge(a1_out, 1)
                nc.tensor.transpose(S.bank_bf[6][:, 0:T], S.rowmax[L][:, n.p, :], S.eye_bf[:, :]).then_inc(mt_done, 1)

            def scores(s, half):
                if half == 0:
                    pe.wait_ge(mt_out, s.i + 1)
                if half or s.lo >= 1:
                    pe.wait_ge(ex_out, s.i * 4 + 2 * half)
                for s4 in range(4):
                    for c in range(2):
                        h = head(half, c, s4)
                        out = bank[ST[c]][0:KEYS, s4 * T:(s4 + 1) * T]
                        nc.tensor.matmul(out, S.negsel[q_rows(h), L, h * KEYS:(h + 1) * KEYS], S.maxT[q_rows(h), s.p, :], start=True, stop=False)
                        k = kT[q_rows(h), s.p, h // 2, :] if L else S.kmask[q_rows(h), s.p, s4, :]
                        q = qT[q_rows(h), s.p, h // 2, :] if L else qT[q_rows(h), s.p, :]
                        mm = nc.tensor.matmul(out, k, q, start=False, stop=True)
                        if s4 == 3:
                            mm.then_inc(st_done, 1)

            def times_v(s, half):
                for c in range(2):
                    pe.wait_ge(ex_out, s.i * 4 + (2 * half + c + 1))
                    if half or s.lo >= 1:
                        pe.wait_ge(pve_out, s.i * 4 + (2 * half + c - 1))
                    if L and half == 0 and c == 0:
                        pe.wait_ge(v_out, s.i * 2 + 2)
                    for s4 in range(4):
                        mm = nc.tensor.matmul(bank[PV[c]][:, s4 * (dh + 1):(s4 + 1) * (dh + 1)],
                                              S.probs[:, half, c, s4 * T:(s4 + 1) * T],
                                              vaug[:, s.p, head(half, c, s4), :], start=True, stop=True)
                    mm.then_inc(pv_done, 1)

            def transpose_out(s, c, nxt):
                pe.wait_ge(pve_out, s.i * 4 + (2 + 2 * c if L else 4))
                if c:
                    pe.wait_ge(ta_out, s.i * 2 + 1)
                elif nxt and L:
                    pe.wait_ge(tq_out, s.i * 2 + 4)
                elif nxt:
                    pe.wait_ge(a1_out, s.i + 2)
                else:
                    pe.wait_ge(mt_out, s.i + 1)
                for j in range(min(tiles, 4)):
                    mm = nc.tensor.transpose(M0[:, j * T:(j + 1) * T], attn[:, s.p, (4 * c + j) * D:(4 * c + j + 1) * D], S.eye[:, :])
                mm.then_inc(ta_done, 1)

            def project_out(s, nxt):
                pe.wait_ge(ta_out, (s.i + 1) * (1 + L))
                if nxt:
                    pe.wait_ge(m1_out, s.i * (6 if L else 2) + (12 if L else 4))
                else:
                    pe.wait_ge(o_out, s.i)
                nc.tensor.matmul(M1[:, 0:D], S.ones_row[:, :], S.row_o[:, L, :], start=True, stop=False)
                for j in range(tiles):
                    w = S.wo1[:, j, :] if L else S.wo0[:, :]
                    mm = nc.tensor.matmul(M1[:, 0:D], attnT[:, j, :], w, start=False, stop=(j == tiles - 1))
                mm.then_inc(o_done, 1)

            def step(s, _):
                n = s.next()
                cur, nxt = s.lo >= 0, n.lo <= last
                if nxt:
                    transpose_rows(n)
                if cur:
                    scores(s, 0)
                if nxt and L:
                    project_q(n, 0)
                    project_v(n, 0)
                    project_q(n, 1)
                    project_v(n, 1)
                if nxt and L == 0:
                    project_qkv(n)
                if cur:
                    times_v(s, 0)
                if nxt and L:
                    project_k(n, 0, 0)
                if cur:
                    scores(s, 1)
                if nxt and L:
                    project_k(n, 0, 1)
                    transpose_q(n, 0)
                    project_k(n, 1, 0)
                    transpose_q(n, 1)
                    project_k(n, 1, 1)
                if L and cur:
                    times_v(s, 1)
                if nxt:
                    scores_for_max(n, 0)
                if cur:
                    if L:
                        transpose_out(s, 0, nxt)
                    else:
                        times_v(s, 1)
                if nxt:
                    scores_for_max(n, 1)
                if cur:
                    transpose_out(s, L, nxt)
                    if L:
                        project_out(s, nxt)
                if nxt:
                    transpose_max(n)
                if cur and L == 0:
                    project_out(s, nxt)
            run_steps(pe, step, -1, last, 2, 3)


def pool_fence(nc, S, g, n, phase, sem, value):
    done = S.sem(phase + "_fence")
    if n.lo >= 1:
        g.wait_ge(done, n.i)
    g.wait_ge(sem, value)
    nc.gpsimd.tensor_tensor(S.fence_g[:, :], S.minus_half[:, 0:1], S.minus_half[:, 0:1], ALU.add).then_inc(done, 1)


def ffn0(nc, S):
    last = B
    bank, bank_bf = S.bank, S.bank_bf
    ZT, H1, GT, OUT = bank[0], (bank[1], bank[2]), bank[3], bank[4]

    def sem(n):
        return S.sem(f"f_{n}")

    ln, ln_pow, zq_ready, rec = sem("ln"), sem("ln_pow"), sem("zq_ready"), sem("rec")
    zt_done, zt_out, h_done, h_out, g_ready, sq_ready = sem("zt_done"), sem("zt_out"), sem("h_done"), sem("h_out"), sem("g_ready"), sem("sq_ready")
    rms_in, rms_pow, gq_ready, gt_done, gt_out, y_done, y_out = (sem("rms_in"), sem("rms_pow"), sem("gq_ready"), sem("gt_done"),
                                                                  sem("gt_out"), sem("y_done"), sem("y_out"))
    z_done, xb_done, rec2 = sem("z_done"), sem("xb_done"), sem("rec2")

    with nc.Block() as block:
        @block.gpsimd
        def _(g):
            def step(s, _):
                n, n2 = s.next(), s.next(2)
                if n2.lo < B:
                    g.wait_ge(ln, n2.i * 3 + 3)
                    nc.gpsimd.tensor_tensor(S.rstd[:, n2.p, 0:1], S.varx[:, n2.p, 0:1], S.minus_half[:, 0:1], ALU.pow).then_inc(ln_pow, 1)
                if 0 <= n.lo < B:
                    pool_fence(nc, S, g, n, 'f', z_done, n.i + 1)
                    nc.gpsimd.tensor_tensor(tile_at(S.x, n.i, D), tile_at(S.x, n.i, D), S.b2bc[:, :], ALU.add).then_inc(xb_done, 1)
                if 0 <= s.lo < B:
                    g.wait_ge(rms_in, s.i + 1)
                    nc.gpsimd.tensor_tensor(S.rms[:, :], S.meansq[:, :], S.minus_half[:, 0:1], ALU.pow).then_inc(rms_pow, 1)
            run_steps(g, step, -2, last, 4, 3)

        @block.vector
        def _(v):
            def statistics(n):
                nc.vector.bn_stats(S.stats[:, n.p, 0, :], tile_at(S.x, n.i, D)).then_inc(ln, 1)
                v.wait_ge(ln, n.i * 3 + 1)
                nc.vector.memset(S.fence[:, :], 0.0)
                nc.vector.bn_aggr(S.meanvar[:, n.p, 0, :], S.stats[:, n.p, 0, :]).then_inc(ln, 1)
                v.wait_ge(ln, n.i * 3 + 2)
                nc.vector.tensor_scalar(S.varx[:, n.p, 0:1], S.meanvar[:, n.p, 0, 1:2], 1.0 + EPS, EPS * EPS,
                                        ALU.mult, ALU.add).then_inc(ln, 1)

            def quantise_z(n):
                p = n.p
                v.wait_ge(ln_pow, n.i + 1)
                nc.vector.tensor_scalar(S.z[:, :], tile_at(S.x, n.i, D), S.meanvar[:, p, 0, 0:1], S.rstd[:, p, 0:1],
                                        ALU.subtract, ALU.mult).then_inc(z_done, 1)
                v.wait_ge(z_done, n.i + 1)
                nc.vector.tensor_reduce(S.zmax[:, p, :], S.z[:, :], AX, ALU.max, apply_absolute_value=True).then_inc(rec, 1)
                v.wait_ge(rec, n.i * 4 + 1)
                nc.vector.tensor_scalar(S.zmax[:, p, :], S.zmax[:, p, :], EPS, None, ALU.max).then_inc(rec, 1)
                v.wait_ge(rec, n.i * 4 + 2)
                nc.vector.reciprocal(S.zinv[:, :], S.zmax[:, p, :]).then_inc(rec, 1)
                v.wait_ge(rec, n.i * 4 + 3)
                nc.vector.tensor_scalar(S.zinv[:, :], S.zinv[:, :], 127.0, None, ALU.mult).then_inc(rec, 1)
                nc.vector.tensor_scalar(S.zout[:, p, :], S.zmax[:, p, :], S.wmean127[:, 0:1], None, ALU.mult)
                v.wait_ge(rec, n.i * 4 + 4)
                nc.vector.tensor_scalar(S.zq[:, p, :], S.z[:, :], S.zinv[:, :], MAGIC, ALU.mult, ALU.add).then_inc(zq_ready, 1)

            def hidden(s):
                v.wait_ge(h_done, s.i + 1)
                nc.vector.scalar_tensor_tensor(S.hid[:, s.p, :], H1[s.p][:, :], S.zout[:, s.p, :], S.b1bc[:, :],
                                               ALU.mult, ALU.add).then_inc(h_out, 1)

            def quantise_g(s):
                v.wait_ge(sq_ready, s.i + 1)
                nc.vector.tensor_scalar(S.meansq[:, :], S.sumsq[:, :], 1.0 / F, EPS, ALU.mult, ALU.add).then_inc(rms_in, 1)
                nc.vector.tensor_reduce(S.gmax[:, :], S.gel[:, s.p, :], AX, ALU.max, apply_absolute_value=True).then_inc(rec2, 1)
                v.wait_ge(rec2, s.i * 5 + 1)
                v.wait_ge(rms_pow, s.i + 1)
                nc.vector.tensor_scalar(S.gmax[:, :], S.gmax[:, :], S.rms[:, :], EPS, ALU.mult, ALU.max).then_inc(rec2, 1)
                v.wait_ge(rec2, s.i * 5 + 2)
                nc.vector.reciprocal(S.ginv[:, :], S.gmax[:, :]).then_inc(rec2, 1)
                nc.vector.tensor_scalar(S.gout[:, s.p, :], S.gmax[:, :], S.wmean127[:, 1:2], None, ALU.mult).then_inc(rec2, 1)
                v.wait_ge(rec2, s.i * 5 + 4)
                nc.vector.tensor_scalar(S.ginv[:, :], S.ginv[:, :], S.rms[:, :], 127.0, ALU.mult, ALU.mult).then_inc(rec2, 1)
                v.wait_ge(rec2, s.i * 5 + 5)
                nc.vector.tensor_scalar(S.gq[:, s.p, :], S.gel[:, s.p, :], S.ginv[:, :], MAGIC, ALU.mult, ALU.add).then_inc(gq_ready, 1)

            def residual(b):
                v.wait_ge(xb_done, b.i + 1)
                v.wait_ge(y_done, b.i + 1)
                nc.vector.scalar_tensor_tensor(tile_at(S.x, b.i, D), OUT[:, 0:D], S.gout[:, b.p, :], tile_at(S.x, b.i, D),
                                               ALU.mult, ALU.add).then_inc(y_out, 1)

            def step(s, _):
                n, n2, b = s.next(), s.next(2), s.next(-1)
                if n2.lo < B:
                    statistics(n2)
                if 0 <= s.lo < B:
                    hidden(s)
                if b.lo >= 0:
                    residual(b)
                if 0 <= n.lo < B:
                    quantise_z(n)
                if 0 <= s.lo < B:
                    quantise_g(s)
            run_steps(v, step, -2, last, 4, 3)

        @block.scalar
        def _(act):
            def step(s, _):
                n = s.next()
                if 0 <= s.lo < B:
                    act.wait_ge(h_out, s.i + 1)
                    nc.scalar.activation(S.gel[:, s.p, :], S.hid[:, s.p, :], ACT.Gelu).then_inc(g_ready, 1)
                    act.wait_ge(g_ready, s.i + 1)
                    nc.scalar.activation(S.gsq[:, :], S.gel[:, s.p, :], ACT.Square, accum_out=S.sumsq[:, :]).then_inc(sq_ready, 1)
                if 0 <= n.lo < B:
                    act.wait_ge(zt_done, n.i + 1)
                    nc.scalar.activation(S.zT[:, n.p, :], ZT[:, 0:T], ACT.Identity, bias=S.minus_magic[:, :]).then_inc(zt_out, 1)
                if 0 <= s.lo < B:
                    act.wait_ge(gt_done, s.i + 1)
                    nc.scalar.activation(S.gT[:, :], GT[:, :], ACT.Identity, bias=S.minus_magic[:, :]).then_inc(gt_out, 1)
            run_steps(act, step, -2, last, 4, 3)

        @block.tensor
        def _(pe):
            def step(s, _):
                n = s.next()
                if 0 <= n.lo < B:
                    pe.wait_ge(zq_ready, n.i + 1)
                    if n.lo >= 1:
                        pe.wait_ge(zt_out, n.i)
                    nc.tensor.transpose(ZT[:, 0:T], S.zq[:, n.p, :], S.eye[:, :]).then_inc(zt_done, 1)
                    pe.wait_ge(zt_out, n.i + 1)
                    if n.lo >= 2:
                        pe.wait_ge(h_out, n.i - 1)
                    nc.tensor.matmul(H1[n.p][:, :], S.zT[:, n.p, :], S.w1q[:, :], start=True, stop=True).then_inc(h_done, 1)
                if 0 <= s.lo < B:
                    pe.wait_ge(gq_ready, s.i + 1)
                    if s.lo >= 1:
                        pe.wait_ge(gt_out, s.i)
                    for c in range(F // D):
                        mm = nc.tensor.transpose(GT[:, c * T:(c + 1) * T], S.gq[:, s.p, c * D:(c + 1) * D], S.eye[:, :])
                    mm.then_inc(gt_done, 1)
                    pe.wait_ge(gt_out, s.i + 1)
                    if s.lo >= 1:
                        pe.wait_ge(y_out, s.i)
                    for c in range(F // D):
                        mm = nc.tensor.matmul(OUT[:, 0:D], S.gT[:, c * T:(c + 1) * T], S.w2q[:, c * D:(c + 1) * D],
                                              start=(c == 0), stop=(c == F // D - 1))
                    mm.then_inc(y_done, 1)
            run_steps(pe, step, -2, last, 4, 3)


def dispatch(nc, S):
    last = B
    bank = S.bank
    XT, LG, CUM = bank[0], bank[1], bank[2]

    def sem(n):
        return S.sem(f"d_{n}")

    ln, ln_pow, xn_ready = sem("ln"), sem("ln_pow"), sem("xn_ready")
    xt_done, xt_out, lg_done, lg_out, ch, idx_ready, ex_done = (sem("xt_done"), sem("xt_out"), sem("lg_done"), sem("lg_out"), sem("choice"),
                                                                sem("idx_ready"), sem("ex_done"))
    oh_ready, count_ready, cum_done, place, slot_ready = sem("oh_ready"), sem("count_ready"), sem("cum_done"), sem("place"), sem("slot_ready")
    xg_ready = sem("xg_ready")
    scattered = [S.sem(f"scattered{p}") for p in range(2)]

    with nc.Block() as block:
        @block.gpsimd
        def _(g):
            def step(s, _):
                n2, b = s.next(2), s.next(-1)
                if n2.lo < B:
                    g.wait_ge(ln, n2.i * 3 + 3)
                    nc.gpsimd.tensor_tensor(S.rstd[:, n2.p, 0:1], S.varx[:, n2.p, 0:1], S.minus_half[:, 0:1], ALU.pow).then_inc(ln_pow, 1)
                if b.lo >= 0:
                    pool_fence(nc, S, g, b, 'd', slot_ready, b.i + 1)
                    nc.gpsimd.indirect_dma_start(out=S.dispatch[:, :], out_offset=bass.IndirectOffsetOnAxis(ap=S.row_to[:, b.p:b.p + 1], axis=0),
                                                 in_=S.xg[:, b.p, :], in_offset=None).then_inc(scattered[b.p], 16)
            run_steps(g, step, -2, last, 4, 3)
            for p in range(2):
                g.wait_ge(scattered[p], 16 * B // 2)

        @block.vector
        def _(v):
            def statistics(n):
                nc.vector.bn_stats(S.stats[:, n.p, 0, :], tile_at(S.x, n.i, D)).then_inc(ln, 1)
                v.wait_ge(ln, n.i * 3 + 1)
                nc.vector.memset(S.fence[:, :], 0.0)
                nc.vector.bn_aggr(S.meanvar[:, n.p, 0, :], S.stats[:, n.p, 0, :]).then_inc(ln, 1)
                v.wait_ge(ln, n.i * 3 + 2)
                nc.vector.tensor_scalar(S.varx[:, n.p, 0:1], S.meanvar[:, n.p, 0, 1:2], EPS, None, ALU.add).then_inc(ln, 1)

            def normalise(n):
                if n.lo >= 2:
                    v.wait_ge(xg_ready, n.i - 1)
                v.wait_ge(ln_pow, n.i + 1)
                nc.vector.tensor_scalar(S.xn[:, n.p, :], tile_at(S.x, n.i, D), S.meanvar[:, n.p, 0, 0:1], S.rstd[:, n.p, 0:1],
                                        ALU.subtract, ALU.mult).then_inc(xn_ready, 1)

            def choose(s):
                i, p = s.i, s.p
                v.wait_ge(lg_done, i + 1)
                nc.vector.tensor_copy(S.logits[:, p, :], LG[:, 0:E]).then_inc(lg_out, 1)
                v.wait_ge(lg_out, i + 1)
                nc.vector.memset(S.fence[:, :], 0.0)
                nc.vector.max(S.top8[:, :], S.logits[:, p, :]).then_inc(ch, 1)
                v.wait_ge(ch, i * 3 + 1)
                nc.vector.memset(S.fence[:, :], 0.0)
                nc.vector.max_index(S.idx8[:, :], S.top8[:, :], S.logits[:, p, :]).then_inc(ch, 1)
                nc.vector.tensor_scalar(S.minus_top[:, p:p + 1], S.top8[:, 0:1], -1.0, None, ALU.mult).then_inc(idx_ready, 1)
                v.wait_ge(ch, i * 3 + 2)
                nc.vector.tensor_copy(S.expert[:, p:p + 1], S.idx8[:, 0:1]).then_inc(ch, 1)
                v.wait_ge(ch, i * 3 + 3)
                nc.vector.tensor_scalar(S.onehot[:, p, :], S.experts[:, :], S.expert[:, p:p + 1], None, ALU.is_equal).then_inc(oh_ready, 1)
                v.wait_ge(oh_ready, i + 1)
                if s.lo >= 1:
                    v.wait_ge(cum_done, i)
                nc.vector.tensor_tensor(S.count[:, p, :], S.count[:, 1 - p, :], S.onehot[:, p, :], ALU.add).then_inc(count_ready, 1)
                if s.lo >= 2:
                    v.wait_ge(scattered[p], i * 8 - 8 * p)
                nc.vector.tensor_copy(S.xg[:, p, :], S.xn[:, p, :]).then_inc(xg_ready, 1)

            def places(b):
                i, p = b.i, b.p
                v.wait_ge(cum_done, i + 1)
                nc.vector.tensor_tensor_reduce(out=S.picked[:, :], in0=CUM[:, 0:E], in1=S.onehot[:, p, :], scale=1.0, scalar=0.0,
                                               op0=ALU.mult, op1=ALU.add, accum_out=S.pos[:, :]).then_inc(place, 1)
                v.wait_ge(place, i * 6 + 1)
                nc.vector.tensor_scalar(S.keep[:, :], S.pos[:, :], float(CAP), None, ALU.is_le).then_inc(place, 1)
                v.wait_ge(place, i * 6 + 2)
                nc.vector.tensor_scalar(S.pos[:, :], S.pos[:, :], -1.0, S.keep[:, :], ALU.add, ALU.mult).then_inc(place, 1)
                v.wait_ge(place, i * 6 + 3)
                nc.vector.tensor_scalar(S.row_f[:, :], S.expert[:, p:p + 1], float(CAP), S.pos[:, :], ALU.mult, ALU.add).then_inc(place, 1)
                v.wait_ge(place, i * 6 + 4)
                nc.vector.tensor_copy(S.row_from[:, bass.ds(i, 1)], S.row_f[:, :])
                nc.vector.tensor_tensor(S.row_g[:, :], S.row_f[:, :], S.dropped_row[:, bass.ds(i, 1)], ALU.subtract).then_inc(place, 1)
                v.wait_ge(place, i * 6 + 5)
                if b.lo >= 2:
                    v.wait_ge(scattered[p], i * 8 - 8 * p)
                nc.vector.scalar_tensor_tensor(S.row_to[:, p:p + 1], S.row_g[:, :], S.keep[:, :], S.dropped_row[:, bass.ds(i, 1)],
                                               ALU.mult, ALU.add).then_inc(slot_ready, 1)
                v.wait_ge(ex_done, i + 1)
                nc.vector.reciprocal(S.top_prob[:, :], S.sumexp[:, p:p + 1]).then_inc(place, 1)
                v.wait_ge(place, i * 6 + 6)
                nc.vector.tensor_tensor(S.weight[:, bass.ds(i, 1)], S.top_prob[:, :], S.keep[:, :], ALU.mult)

            def step(s, _):
                n, n2, b = s.next(), s.next(2), s.next(-1)
                if n2.lo < B:
                    statistics(n2)
                if b.lo >= 0:
                    places(b)
                if 0 <= s.lo < B:
                    choose(s)
                if n2.lo < B:
                    normalise(n2)
            run_steps(v, step, -2, last, 4, 3)

        @block.scalar
        def _(act):
            def step(s, _):
                n = s.next()
                if 0 <= n.lo < B:
                    act.wait_ge(xt_done, n.i + 1)
                    nc.scalar.copy(S.xT[:, n.p, :], XT[:, 0:D]).then_inc(xt_out, 1)
                if 0 <= s.lo < B:
                    act.wait_ge(idx_ready, s.i + 1)
                    nc.scalar.activation(S.exps[:, :], S.logits[:, s.p, :], ACT.Exp, bias=S.minus_top[:, s.p:s.p + 1],
                                         accum_out=S.sumexp[:, s.p:s.p + 1]).then_inc(ex_done, 1)
            run_steps(act, step, -2, last, 4, 3)

        @block.tensor
        def _(pe):
            def step(s, _):
                n = s.next()
                if 0 <= n.lo < B:
                    pe.wait_ge(xn_ready, n.i + 1)
                    if n.lo >= 1:
                        pe.wait_ge(xt_out, n.i)
                    nc.tensor.transpose(XT[:, 0:D], S.xn[:, n.p, :], S.eye[:, :]).then_inc(xt_done, 1)
                    pe.wait_ge(xt_out, n.i + 1)
                    if n.lo >= 1:
                        pe.wait_ge(lg_out, n.i)
                    nc.tensor.matmul(LG[:, 0:E], S.ones_row[:, :], S.gate_b[:, :], start=True, stop=False)
                    nc.tensor.matmul(LG[:, 0:E], S.xT[:, n.p, :], S.gate_t[:, :], start=False, stop=True).then_inc(lg_done, 1)
                if 0 <= s.lo < B:
                    pe.wait_ge(oh_ready, s.i + 1)
                    if s.lo >= 1:
                        pe.wait_ge(place, s.i * 6 - 5)
                        pe.wait_ge(count_ready, s.i)
                    nc.tensor.matmul(CUM[:, 0:E], S.upto[:, :], S.onehot[:, s.p, :], start=True, stop=False)
                    nc.tensor.matmul(CUM[:, 0:E], S.ones_bf[:, :], S.count[:, 1 - s.p, :], start=False, stop=True).then_inc(cum_done, 1)
            run_steps(pe, step, -2, last, 4, 3)


def experts(nc, S, A):
    last = E - 1
    bank = S.bank
    XT, HID, Y = bank[0], bank[1:5], bank[5:7]
    CHUNKS = F // D
    RT = [(r, min(T, CAP - r)) for r in range(0, CAP, T)]

    def sem(n):
        return S.sem(f"e_{n}")

    rows_in = [sem(f"rows_in{p}") for p in range(2)]
    w_in = [sem(f"w_in{p}") for p in range(2)]
    stored = [sem(f"stored{p}") for p in range(2)]
    W_LOADS = 4 * 16
    R_LOADS = 2 * 16
    xt_done, xt_out, h_done, h_act, h_dve, y_done, y_out = (sem("xt_done"), sem("xt_out"), sem("h_done"), sem("h_act"), sem("h_dve"),
                                                            sem("y_done"), sem("y_out"))
    full = RT[-1][0]

    with nc.Block() as block:
        @block.sync
        def _(sp):
            def load(n, _):
                e, p = n.i, n.p
                if n.lo >= 2:
                    sp.wait_ge(xt_done, e - 1)
                sp.dma_start(S.erows[:, p, 0:full // T, :], S.dispatch[bass.ds(e * CAP, full), :].rearrange("(r t) d -> t r d", t=T)
                             ).then_inc(rows_in[p], 16)
                sp.dma_start(S.erows[0:CAP - full, p, full // T, :], S.dispatch[bass.ds(e * CAP + full, CAP - full), :]).then_inc(rows_in[p], 16)
                if n.lo >= 2:
                    sp.wait_ge(y_done, e - 1)
                    sp.wait_ge(h_act, e * 2 - 2)
                    sp.wait_ge(h_dve, e * 2 - 2)
                sp.dma_start(S.ew1[:, p, :], A["L1_ffn_w1"][bass.ds(e, 1)].rearrange("e d f -> d (e f)")).then_inc(w_in[p], 16)
                sp.dma_start(S.eb1[:, p, :], A["L1_ffn_b1"][bass.ds(e, 1)].rearrange("e (c f) -> f (e c)", f=D), allow_slow_non_contiguous=True).then_inc(w_in[p], 16)
                sp.dma_start(S.ew2[:, p, :, :], A["L1_ffn_w2"][bass.ds(e, 1)].rearrange("e (c f) d -> f (e c) d", f=D)).then_inc(w_in[p], 16)
                sp.dma_start(S.eb2[:, p, :], A["L1_ffn_b2"][bass.ds(e, 1), :]).then_inc(w_in[p], 16)
            run_steps(sp, load, 0, last, 2, 0)

        @block.gpsimd
        def _(g):
            def store(n, _):
                e, p = n.i, n.p
                pool_fence(nc, S, g, n, 'e', y_out, e + 1)
                g.dma_start(S.results[bass.ds(e * CAP, full), :].rearrange("(r t) d -> t r d", t=T), S.eout[:, p, 0:full // T, :]
                            ).then_inc(stored[p], 16)
                g.dma_start(S.results[bass.ds(e * CAP + full, CAP - full), :], S.eout[0:CAP - full, p, full // T, :]).then_inc(stored[p], 16)
            run_steps(g, store, 0, last, 2, 0)
            for p in range(2):
                g.wait_ge(stored[p], 32 * E // 2)

        @block.tensor
        def _(pe):
            def step(s, _):
                n = s.next()
                if n.lo <= last:
                    pe.wait_ge(rows_in[n.p], n.i * 16 + (32 - 16 * n.p))
                    if n.lo >= 1:
                        pe.wait_ge(xt_out, n.i)
                    for r, (r0, rows) in enumerate(RT):
                        mm = nc.tensor.transpose(XT[:, r0:r0 + rows], S.erows[0:rows, n.p, r, :], S.eye[0:rows, 0:rows])
                    mm.then_inc(xt_done, 1)
                if s.lo >= 0:
                    e, p = s.i, s.p
                    pe.wait_ge(xt_out, e + 1)
                    pe.wait_ge(w_in[p], e * 32 + (64 - 32 * p))
                    if s.lo >= 1:
                        pe.wait_ge(h_act, e * 2)
                        pe.wait_ge(h_dve, e * 2)
                    for c in range(CHUNKS):
                        nc.tensor.matmul(HID[c][:, 0:CAP], S.ew1[:, p, c * D:(c + 1) * D], S.eXT[:, p, :], start=True, stop=True).then_inc(h_done, 1)
                    pe.wait_ge(h_act, e * 2 + 2)
                    pe.wait_ge(h_dve, e * 2 + 2)
                    if s.lo >= 2:
                        pe.wait_ge(y_out, e - 1)
                    for r, (r0, rows) in enumerate(RT):
                        out = Y[p][0:rows, r * D:(r + 1) * D]
                        nc.tensor.matmul(out, S.ones_row[:, 0:rows], S.eb2[:, p, :], start=True, stop=False)
                        for c in range(CHUNKS):
                            mm = nc.tensor.matmul(out, S.ehid[:, c, r0:r0 + rows], S.ew2[:, p, c, :], start=False, stop=(c == CHUNKS - 1))
                    mm.then_inc(y_done, 1)
            run_steps(pe, step, -1, last, 3, 2)

        @block.scalar
        def _(act):
            def step(s, _):
                n = s.next()
                if n.lo <= last:
                    act.wait_ge(xt_done, n.i + 1)
                    nc.scalar.copy(S.eXT[:, n.p, :], XT[:, 0:CAP]).then_inc(xt_out, 1)
                if s.lo >= 0:
                    for c in (0, 2):
                        act.wait_ge(h_done, s.i * 4 + (c + 1))
                        if c == 0 and s.lo >= 1:
                            act.wait_ge(y_done, s.i)
                        nc.scalar.activation(S.ehid[:, c, :], HID[c][:, 0:CAP], ACT.Relu, bias=S.eb1[:, s.p, c:c + 1]).then_inc(h_act, 1)
            run_steps(act, step, -1, last, 3, 2)

        @block.vector
        def _(v):
            def step(s, _):
                if s.lo < 0:
                    return
                for c in (1, 3):
                    v.wait_ge(h_done, s.i * 4 + (c + 1))
                    if c == 1 and s.lo >= 1:
                        v.wait_ge(y_done, s.i)
                    nc.vector.tensor_scalar(S.ehid[:, c, :], HID[c][:, 0:CAP], S.eb1[:, s.p, c:c + 1], 0.0, ALU.add, ALU.max).then_inc(h_dve, 1)
                v.wait_ge(y_done, s.i + 1)
                if s.lo >= 2:
                    v.wait_ge(stored[s.p], s.i * 16 - 16 * s.p)
                nc.vector.tensor_copy(S.eout[:, s.p, 0:full // T, :].rearrange("t r d -> t (r d)"), Y[s.p][:, 0:full])
                nc.vector.tensor_copy(S.eout[0:CAP - full, s.p, full // T, :], Y[s.p][0:CAP - full, full:full + D]).then_inc(y_out, 1)
            run_steps(v, step, -1, last, 3, 2)


def combine(nc, S, out):
    def sem(n):
        return S.sem(f"c_{n}")
    gathered = [sem(f"gathered{p}") for p in range(2)]
    row_ready, x_ready, written = sem("row_ready"), sem("x_ready"), sem("written")

    with nc.Block() as block:
        @block.vector
        def _(v):
            def step(s, _):
                n = s.next()
                if n.lo < B:
                    if n.lo >= 2:
                        v.wait_ge(gathered[n.p], n.i * 8 - 8 * n.p)
                    nc.vector.tensor_copy(S.row_now[:, n.p:n.p + 1], S.row_from[:, bass.ds(n.i, 1)]).then_inc(row_ready, 1)
                if s.lo >= 0:
                    v.wait_ge(gathered[s.p], s.i * 8 + (16 - 8 * s.p))
                    nc.vector.scalar_tensor_tensor(tile_at(S.x, s.i, D), S.xg[:, s.p, :], S.weight[:, bass.ds(s.i, 1)], tile_at(S.x, s.i, D),
                                                   ALU.mult, ALU.add).then_inc(x_ready, 1)
            run_steps(v, step, -1, B - 1, 3, 2)

        @block.gpsimd
        def _(g):
            def step(n, _):
                if n.lo >= 2:
                    g.wait_ge(x_ready, n.i - 1)
                pool_fence(nc, S, g, n, 'c', row_ready, n.i + 1)
                nc.gpsimd.indirect_dma_start(out=S.xg[:, n.p, :], out_offset=None, in_=S.results[:, :],
                                             in_offset=bass.IndirectOffsetOnAxis(ap=S.row_now[:, n.p:n.p + 1], axis=0)
                                             ).then_inc(gathered[n.p], 16)
            run_steps(g, step, 0, B - 1, 2, 0)

        @block.sync
        def _(sp):
            def step(n, _):
                sp.wait_ge(x_ready, n.i + 1)
                sp.dma_start(out[bass.ds(n.i, 1)].rearrange("b t d -> t (b d)"), tile_at(S.x, n.i, D)).then_inc(written, 16)
            run_steps(sp, step, 0, B - 1, 2, 0)
            sp.wait_ge(written, 16 * B)


def program(nc, A, out):
    with ExitStack() as ctx:
        S = Store(nc, ctx)
        sb = S.sb
        S.bank = [ctx.enter_context(nc.psum_tensor(f"bank{b}", [D, 512], F32)) for b in range(8)]
        S.bank_bf = [b[:, :].bitcast(BF16) for b in S.bank]
        S.dispatch = nc.dram_tensor("dispatch", (ROWS + B * T, D), F32, kind="Internal").ap()
        S.results = nc.dram_tensor("results", (ROWS, D), F32, kind="Internal").ap()
        S.eye = sb("eye", [D, D])
        S.eye_bf = sb("eye_bf", [D, D], BF16)
        S.x = sb("x", [T, B * D])
        S.cols = sb("cols", [D, 5])
        S.bvcol = sb("bvcol", [D, 8])
        S.wq0, S.wk0, S.wv0, S.wo0 = (sb(w, [D, D]) for w in ("wq0", "wk0", "wv0", "wo0"))
        S.row_o = sb("row_o", [1, 2, D])
        S.slotmask = sb("slotmask", [D, 4])
        S.negsel = sb("negsel", [D, 2, H * KEYS], BF16)
        S.len_i = sb("len_i", [D, B], I32)
        S.len_f = sb("len_f", [D, B])
        S.w1n = sb("w1n", [D, 4, D])
        S.w2n = sb("w2n", [D, F])
        S.w1t = sb("w1t", [D, F], BF16)
        S.w2t = sb("w2t", [D, F], BF16)
        S.w1q = sb("w1q", [D, F], BF16)
        S.w2q = sb("w2q", [D, F], BF16)
        S.b1bc = sb("b1bc", [D, F])
        S.b2bc = sb("b2bc", [D, D])
        S.bias8 = sb("bias8", [D, 3, 8])
        S.parts = sb("parts", [D, 3, 3, 8], BF16)
        S.bias3 = sb("bias3", [3, 3, H * DH1], BF16)
        S.kpos = sb("kpos", [D, 1])
        S.krow = sb("krow", [1, KEYS])
        S.maskrow32 = sb("maskrow32", [1, B, KEYS])
        S.maskrow = sb("maskrow", [1, B * 4 * KEYS], BF16)
        S.maskcol = sb("maskcol", [D, B])
        S.mcol = sb("mcol", [KEYS, 2])
        S.wq1, S.wk1, S.wk1r, S.wv1 = (sb(w, [D, H * DH1]) for w in ("wq1", "wk1", "wk1r", "wv1"))
        S.wo1 = sb("wo1", [D, 8, D])
        S.cosq = sb("cosq", [T, DH1])
        S.sinq = sb("sinq", [T, DH1])
        S.cosk = sb("cosk", [D, KEYS])
        S.sink = sb("sink", [D, KEYS])
        S.gate_w = sb("gate_w", [E, D])
        S.gate_b = sb("gate_b", [1, E])
        S.gate_t = sb("gate_t", [D, E])
        S.upto32 = sb("upto32", [D, D])
        S.upto = sb("upto", [D, D], BF16)
        S.experts = sb("experts", [D, E])
        S.dropped_row = sb("dropped_row", [D, B])
        S.ones_row = sb("ones_row", [1, D])
        S.ones_bf = sb("ones_bf", [D, D], BF16)
        S.ones_mean = sb("ones_mean", [D, D])
        S.wabs = sb("wabs", [D, 2])
        S.wmean = sb("wmean", [D, 2])
        S.wscale = sb("wscale", [D, 2])
        S.wmean127 = sb("wmean127", [D, 2])
        S.minus_half = sb("minus_half", [D, 2])
        S.minus_magic = sb("minus_magic", [D, 1])
        S.fence = sb("fence", [D, 1])
        S.fence_g = sb("fence_g", [D, 1])
        S.stats = sb("stats", [D, 2, 2, 6])
        S.meanvar = sb("meanvar", [D, 2, 2, 2])
        S.varx = sb("varx", [D, 2, 2])
        S.rstd = sb("rstd", [D, 2, 2])
        S.xn = sb("xn", [T, 2, D])
        S.ctx_in = sb("ctx_in", [KEYS, 2, D])
        S.cn = sb("cn", [KEYS, 2, D])
        S.xT = sb("xT", [D, 2, T])
        S.cT = sb("cT", [D, 2, KEYS])
        S.qT = [sb("qT0", [D, 2, T]), sb("qT1", [D, 2, 8, T])]
        S.kT = [sb("kT0", [D, 2, KEYS]), sb("kT1", [D, 2, 8, KEYS])]
        S.vaug = [sb("vaug0", [KEYS, 2, H, DH0 + 1]), sb("vaug1", [KEYS, 2, H, DH1 + 1])]
        S.kmask = sb("kmask", [D, 2, 4, KEYS])
        S.rowmax = [sb("rowmax0", [T, 2, D], BF16), sb("rowmax1", [T, 2, D], BF16)]
        S.maxT = sb("maxT", [D, 2, T], BF16)
        S.probs = sb("probs", [KEYS, 2, 2, 4 * T])
        S.attn = [sb("attn0", [T, 2, H * DH0]), sb("attn1", [T, 2, H * DH1])]
        S.attnT = sb("attnT", [D, 8, T])
        S.recip = sb("recip", [T, 2, 4])
        S.qcos = sb("qcos", [T, 2, 512])
        S.qsin = sb("qsin", [T, 2, 512])
        S.qrot = sb("qrot", [T, 2, 512])
        S.kcos = sb("kcos", [D, 2, 4, KEYS])
        S.ksin = sb("ksin", [D, 2, 4, KEYS])
        S.z = sb("z", [T, D])
        S.zmax = sb("zmax", [T, 2, 1])
        S.zinv = sb("zinv", [T, 1])
        S.zout = sb("zout", [T, 2, 1])
        S.zq = sb("zq", [T, 2, D])
        S.zT = sb("zT", [D, 2, T], BF16)
        S.hid = sb("hid", [T, 2, F])
        S.gel = sb("gel", [T, 2, F])
        S.gsq = sb("gsq", [T, F])
        S.sumsq = sb("sumsq", [T, 1])
        S.meansq = sb("meansq", [T, 1])
        S.rms = sb("rms", [T, 1])
        S.gmax = sb("gmax", [T, 1])
        S.ginv = sb("ginv", [T, 1])
        S.gout = sb("gout", [T, 2, 1])
        S.gq = sb("gq", [T, 2, F])
        S.gT = sb("gT", [D, F], BF16)
        S.logits = sb("logits", [T, 2, E])
        S.top8 = sb("top8", [T, 8])
        S.idx8 = sb("idx8", [T, 8], U32)
        S.minus_top = sb("minus_top", [T, 2])
        S.expert = sb("expert", [T, 2])
        S.onehot = sb("onehot", [T, 2, E], BF16)
        S.count = sb("count", [T, 2, E], BF16)
        S.exps = sb("exps", [T, E])
        S.sumexp = sb("sumexp", [T, 2])
        S.picked = sb("picked", [T, E])
        S.pos = sb("pos", [T, 1])
        S.keep = sb("keep", [T, 1])
        S.row_f = sb("row_f", [T, 1])
        S.row_g = sb("row_g", [T, 1])
        S.top_prob = sb("top_prob", [T, 1])
        S.row_from = sb("row_from", [T, B], I32)
        S.row_to = sb("row_to", [T, 2], I32)
        S.weight = sb("weight", [T, B])
        S.row_now = sb("row_now", [T, 2], I32)
        S.xg = sb("xg", [T, 2, D])
        S.erows = sb("erows", [T, 2, 3, D])
        S.eXT = sb("eXT", [D, 2, CAP])
        S.ew1 = sb("ew1", [D, 2, F])
        S.ew2 = sb("ew2", [D, 2, 4, D])
        S.eb1 = sb("eb1", [D, 2, 4])
        S.eb2 = sb("eb2", [1, 2, D])
        S.ehid = sb("ehid", [D, 4, CAP])
        S.eout = sb("eout", [T, 2, 3, D])
        with nc.sbuf_tensor("zeros", [D, ROWS], F32) as z, nc.sbuf_tensor("negsel32", [D, 2, H * KEYS], F32) as n32:
            S.zeros, S.negsel32 = z, n32
            setup(nc, S, A)
        for k in STAGES:
            k(nc, S, A, out)


STAGES = [lambda nc, S, A, out: attention(nc, S, A, 0), lambda nc, S, A, out: ffn0(nc, S),
          lambda nc, S, A, out: attention(nc, S, A, 1), lambda nc, S, A, out: dispatch(nc, S),
          lambda nc, S, A, out: experts(nc, S, A), lambda nc, S, A, out: combine(nc, S, out)]


def shape_constants():
    f = np.float32
    d, h = np.arange(D), np.arange(H)
    t = np.arange(T, dtype=f)
    inv_freq = (f(1.0) / f(10000.0) ** (np.arange(0, DH1, 2, dtype=f) / f(DH1))).astype(f)
    angle = (t[:, None] * inv_freq[None, :]).astype(f)
    cos, sin = np.repeat(np.cos(angle), 2, 1).astype(f), np.repeat(np.sin(angle), 2, 1).astype(f)
    sign = np.where(np.arange(DH1) % 2 == 0, f(-1), f(1))
    return {
        "c_eye": np.eye(D, dtype=f),
        "c_slotmask": ((d[:, None] % 32) // DH0 == np.arange(4)[None, :]).astype(f),
        "c_negsel": np.stack([np.repeat(-(d[:, None] == place[None, :]).astype(f), KEYS, axis=1)
                              for place in (32 * (h // 4) + h % 4, 64 * (h % 2) + h // 2)], axis=1),
        "c_kpos": d.astype(f).reshape(D, 1),
        "c_krow": np.arange(KEYS, dtype=f).reshape(1, KEYS),
        "c_cosq": cos, "c_sinq": (sin * sign).astype(f),
        "c_cosk": np.tile(cos[:KEYS].T, (2, 1)).copy(), "c_sink": np.tile(sin[:KEYS].T, (2, 1)).copy(),
        "c_upto": (d[:, None] <= d[None, :]).astype(f),
        "c_experts": np.tile(np.arange(E, dtype=f), (D, 1)),
        "c_dropped": (ROWS + np.arange(B)[None, :] * T + d[:, None]).astype(f),
    }


_INS = ['x', 'ctx_1024', '_lenS2', 'L0_xattn_q_w', 'L0_xattn_q_b', 'L0_xattn_k_w', 'L0_xattn_k_b', 'L0_xattn_v_w', 'L0_xattn_v_b',
        'L0_xattn_o_w', 'L0_xattn_o_b', 'L0_ffn_w1', 'L0_ffn_b1', 'L0_ffn_w2', 'L0_ffn_b2', 'L1_xattn_ln_g', 'L1_xattn_ln_b',
        'L1_xattn_Wq', 'L1_xattn_bq', 'L1_xattn_Wk', 'L1_xattn_bk', 'L1_xattn_Wv', 'L1_xattn_bv', 'L1_xattn_Wo', 'L1_xattn_bo',
        'L1_ffn_gate_w', 'L1_ffn_gate_b', 'L1_ffn_w1', 'L1_ffn_b1', 'L1_ffn_w2', 'L1_ffn_b2']


def kernel(**inputs):
    import concourse.bacc as _bacc
    from concourse.bass_utils import run_bass_kernel_spmd as _run

    nc = _bacc.Bacc("TRN2", target_bir_lowering=False, num_devices=1)
    arrays = {name: np.ascontiguousarray(inputs[name]) for name in _INS}
    arrays.update(shape_constants())
    aps = {name: nc.dram_tensor("in_" + name, a.shape, mybir.dt.from_np(a.dtype), kind="ExternalInput").ap() for name, a in arrays.items()}
    out = nc.dram_tensor("out", (B, T, D), F32, kind="ExternalOutput").ap()
    program(nc, aps, out)
    r = _run(nc, [{"in_" + name: a for name, a in arrays.items()}], core_ids=[0])
    return r.results[0]["out"]
```

```python
from contextlib import ExitStack

import numpy as np

import concourse.bass as bass
from concourse import mybir

ALU = mybir.AluOpType
ACT = mybir.ActivationFunctionType
AX = mybir.AxisListType.X
F32 = mybir.dt.float32
BF16 = mybir.dt.bfloat16
I32 = mybir.dt.int32
U32 = mybir.dt.uint32

B = 16
T = 128
D = 128
KEYS = 77
KP = 78
H = 16
DH0, DH1 = 8, 64
F = 512
E = 8
CAP = 320
ROWS = E * CAP
EPS = 1e-5
MAGIC = 12582912.0
MASKED = -1e30


class Step:

    def __init__(self, i, p, lo):
        self.i, self.p, self.lo = i, p, lo

    def next(self, k=1):
        return Step(self.i + k, (self.p + k) % 2, self.lo + k)


def run_steps(eng, step, first, last, head, tail):
    start, stop = first + head, last + 1 - tail
    assert (stop - start) % 2 == 0
    for i in range(first, start):
        step(Step(i, i % 2, i), last)
    with eng.Fori(0, (stop - start) // 2) as r:
        step(Step(r * 2 + start, start % 2, start), last)
        step(Step(r * 2 + (start + 1), (start + 1) % 2, start + 1), last)
    for i in range(stop, last + 1):
        step(Step(i, i % 2, i), last)


def tile_at(t, i, width):
    return t[:, bass.ts(i, width)]


class Store:

    def __init__(self, nc, ctx):
        self.nc, self.ctx, self.sems = nc, ctx, {}

    def sb(self, name, shape, dt=F32):
        return self.ctx.enter_context(self.nc.sbuf_tensor(name, shape, dt))

    def sem(self, name):
        if name not in self.sems:
            self.sems[name] = self.ctx.enter_context(self.nc.semaphore(name))
        return self.sems[name]


def setup(nc, S, A):
    loads = [
        ("eye", S.eye[:, :], A["c_eye"]),
        ("x", S.x[:, :].rearrange("t (b d) -> t b d", d=D), A["x"].rearrange("b t d -> t b d")),
        ("w0", S.wq0[:, :], A["L0_xattn_q_w"]), ("w0", S.wk0[:, :], A["L0_xattn_k_w"]),
        ("w0", S.wv0[:, :], A["L0_xattn_v_w"]), ("w0", S.wo0[:, :], A["L0_xattn_o_w"]),
        ("bias0", S.bias_row[:, 0, :], A["L0_xattn_q_b"].rearrange("(a n) -> a n", a=1)),
        ("bias0", S.bias_row[:, 1, :], A["L0_xattn_k_b"].rearrange("(a n) -> a n", a=1)),
        ("cols", S.cols[:, 2:3], A["L0_xattn_v_b"].rearrange("(p a) -> p a", a=1)),
        ("cols", S.cols[:, 3:4], A["L1_xattn_ln_g"].rearrange("(p a) -> p a", a=1)),
        ("cols", S.cols[:, 4:5], A["L1_xattn_ln_b"].rearrange("(p a) -> p a", a=1)),
        ("cols", S.bvcol[:, :], A["L1_xattn_bv"].rearrange("(j p) -> p j", p=D)),
        ("rows", S.row_o[:, 0, :], A["L0_xattn_o_b"].rearrange("(a n) -> a n", a=1)),
        ("rows", S.row_o[:, 1, :], A["L1_xattn_bo"].rearrange("(a n) -> a n", a=1)),
        ("negsel32", S.negsel32[:, :], A["c_negsel"]),
        ("len", S.len_i[:, :], A["_lenS2"].rearrange("(a n) -> a n", a=1).to_broadcast([D, B])),
        ("w1n", S.w1n[:, :, :], A["L0_ffn_w1"].rearrange("(c p) d -> p c d", p=D)),
        ("w2n", S.w2n[:, :], A["L0_ffn_w2"]),
        ("b1bc", S.b1bc[:, :], A["L0_ffn_b1"].rearrange("(a n) -> a n", a=1).to_broadcast([D, F])),
        ("b2bc", S.b2bc[:, :], A["L0_ffn_b2"].rearrange("(a n) -> a n", a=1).to_broadcast([D, D])),
        ("bias8", S.bias8[:, 0, :], A["L1_xattn_bq"].rearrange("(p j) -> p j", p=D)),
        ("bias8", S.bias8[:, 1, :], A["L1_xattn_bk"].rearrange("(p j) -> p j", p=D)),
        ("kpos", S.kpos[:, :], A["c_kpos"]),
        ("krow", S.krow[:, :], A["c_krow"]),
        ("w1", S.wq1[:, :], A["L1_xattn_Wq"]), ("w1", S.wk1[:, :], A["L1_xattn_Wk"]),
        ("w1", S.wv1[:, :], A["L1_xattn_Wv"]),
        ("w1", S.wo1[:, :, :], A["L1_xattn_Wo"].rearrange("(j p) n -> p j n", p=D)),
        ("w1", S.cosq[:, :], A["c_cosq"]), ("w1", S.sinq[:, :], A["c_sinq"]),
        ("gate", S.gate_w[:, :], A["L1_ffn_gate_w"]),
        ("gate", S.gate_b[:, :], A["L1_ffn_gate_b"].rearrange("(a n) -> a n", a=1)),
        ("moec", S.upto32[:, :], A["c_upto"]), ("moec", S.experts[:, :], A["c_experts"]),
        ("moec", S.dropped_row[:, :], A["c_dropped"]),
    ]
    total = {}
    for name, _, _ in loads:
        total[name] = total.get(name, 0) + 16

    def loaded(eng, *names):
        for n in names:
            eng.wait_ge(S.sem("ld_" + n), total[n])

    for n in total:
        S.sem("ld_" + n)
    zero_done, cast, quant, ps, rotk, split = (S.sem(n) for n in ("zeros", "cast", "quant", "set_pe", "rotk", "split"))
    zero_rows, rows3, step_v, step_g, evac = (S.sem(n) for n in ("zero_rows", "rows3", "set_v", "set_g", "set_act"))
    bank = S.bank

    with nc.Block() as block:
        @block.sync
        def _(sp):
            for name, dst, src in loads:
                sp.dma_start(dst, src, allow_slow_non_contiguous=True).then_inc(S.sem("ld_" + name), 16)
            sp.wait_ge(zero_done, 1)
            for half in range(2):
                sp.dma_start(S.dispatch[half * ROWS // 2:(half + 1) * ROWS // 2, :].rearrange("(p n) d -> p (n d)", p=D), S.zeros[:, :]
                             ).then_inc(zero_rows, 16)
            sp.wait_ge(split, 10)
            for part in range(3):
                sp.dma_start(S.bias3_0[part:part + 1, :, :], S.parts_row[:, part, :, :]).then_inc(rows3, 16)
                for which in range(2):
                    sp.dma_start(S.bias3[part:part + 1, which, :], S.parts[:, part, which, :]).then_inc(rows3, 16)
            sp.wait_ge(rows3, 9 * 16)
            sp.wait_ge(zero_rows, 2 * 16)
            loaded(sp, *total)

        @block.gpsimd
        def _(g):
            nc.gpsimd.memset(S.minus_half[:, :], -0.5)
            nc.gpsimd.memset(S.zeros[:, :], 0.0).then_inc(zero_done, 1)
            g.wait_ge(step_v, 1)
            loaded(g, "krow")
            nc.gpsimd.tensor_tensor(S.maskrow32[:, :, :], S.len_f[0:1, :].unsqueeze(2).to_broadcast([1, B, KEYS]),
                                    S.krow[:, :].unsqueeze(1).to_broadcast([1, B, KEYS]), ALU.subtract).then_inc(step_g, 1)
            g.wait_ge(step_g, 1)
            for s in range(4):
                nc.gpsimd.tensor_scalar(S.maskrow[:, :].rearrange("a (b s k) -> a b s k", b=B, s=4)[:, :, s, :],
                                        S.maskrow32[:, :, :], 0.0, MASKED, ALU.is_le, ALU.mult)

        @block.vector
        def _(v):
            loaded(v, "len")
            nc.vector.tensor_copy(S.len_f[:, :], S.len_i[:, :]).then_inc(step_v, 1)
            for p in range(2):
                nc.vector.memset(S.vaug[0][:, p, :, :], 1.0)
                nc.vector.memset(S.vaug[1][:, p, :, :], 1.0)
            nc.vector.memset(S.kT[0][:, :, :, :], 0.0)
            for parts in (S.qparts, S.kparts):
                nc.vector.memset(parts[:, :], 0.0)
            nc.vector.memset(S.ones_row[:, :], 1.0).then_inc(cast, 1)
            nc.vector.memset(S.ones_bf[:, :], 1.0).then_inc(cast, 1)
            nc.vector.memset(S.ones_mean[:, :], 1.0 / (F * D)).then_inc(cast, 1)
            nc.vector.memset(S.count[:, :, :], 0.0)
            nc.vector.memset(S.varx[:, :, :], 1.0)
            nc.vector.memset(S.minus_magic[:, :], -MAGIC)
            loaded(v, "eye", "negsel32", "moec")
            nc.vector.tensor_copy(S.eye_bf[:, :], S.eye[:, :]).then_inc(cast, 1)
            nc.vector.tensor_copy(S.negsel[:, :], S.negsel32[:, :])
            nc.vector.memset(S.rowmax[:, :, :], 0.0)
            nc.vector.tensor_copy(S.upto[:, :], S.upto32[:, :])
            n = 0
            for ld, row, parts in (("bias0", S.bias_row, S.parts_row), ("bias8", S.bias8, S.parts)):
                loaded(v, ld)
                for part in range(3):
                    nc.vector.tensor_copy(parts[:, part, :, :], row[:, :, :]).then_inc(split, 1)
                    n += 1
                    v.wait_ge(split, n)
                    if part < 2:
                        nc.vector.tensor_tensor(row[:, :, :], row[:, :, :], parts[:, part, :, :], ALU.subtract).then_inc(split, 1)
                        n += 1
                        v.wait_ge(split, n)
            v.wait_ge(step_v, 1)
            loaded(v, "kpos")
            nc.vector.tensor_scalar(S.maskcol[:, :], S.len_f[:, :], S.kpos[:, 0:1], MASKED, ALU.is_le, ALU.mult)
            loaded(v, "w1n", "w2n")
            nc.vector.tensor_reduce(S.wabs[:, 0:1], S.w1n[:, :, :].rearrange("p c d -> p (c d)"), AX, ALU.add,
                                    apply_absolute_value=True).then_inc(quant, 1)
            nc.vector.tensor_reduce(S.wabs[:, 1:2], S.w2n[:, :], AX, ALU.add, apply_absolute_value=True).then_inc(quant, 1)
            v.wait_ge(ps, 1)
            nc.vector.tensor_scalar(S.wmean[:, :], bank[0][:, 0:2], EPS, None, ALU.max).then_inc(quant, 1)
            v.wait_ge(quant, 3)
            nc.vector.reciprocal(S.wscale[:, :], S.wmean[:, :]).then_inc(quant, 1)
            nc.vector.tensor_scalar(S.wmean127[:, :], S.wmean[:, :], 1.0 / 127.0, None, ALU.mult)
            v.wait_ge(quant, 4)
            w1f, w2f = S.w1n[:, :, :].rearrange("p c d -> p (c d)"), S.w2n[:, :]
            n = 4
            for k, (w, wb) in enumerate(((w1f, S.w1t), (w2f, S.w2t))):
                nc.vector.tensor_scalar(w, w, S.wscale[:, k:k + 1], MAGIC, ALU.mult, ALU.add).then_inc(quant, 1)
                n += 1
                v.wait_ge(quant, n)
                nc.vector.tensor_scalar(w, w, -MAGIC, 1.0, ALU.add, ALU.min).then_inc(quant, 1)
                n += 1
                v.wait_ge(quant, n)
                nc.vector.tensor_scalar(wb[:, :], w, -1.0, None, ALU.max).then_inc(quant, 1)
                n += 1
            v.wait_ge(ps, 4)
            loaded(v, "rows")
            nc.vector.tensor_tensor(S.row_o[:, 0, :], bank[1][0:1, 0:D], S.row_o[:, 0, :], ALU.add)
            nc.vector.tensor_tensor(S.row_o[:, 1, :], bank[1][0:1, D:2 * D], S.row_o[:, 1, :], ALU.add)

        @block.tensor
        def _(pe):
            pe.wait_ge(cast, 4)
            pe.wait_ge(quant, 2)
            nc.tensor.matmul(bank[0][:, 0:2], S.ones_mean[:, :], S.wabs[:, :], start=True, stop=True).then_inc(ps, 1)
            pe.wait_ge(quant, 10)
            for k, (wb, b) in enumerate(((S.w1t, 2), (S.w2t, 3))):
                for c in range(F // D):
                    mm = nc.tensor.transpose(S.bank_bf[b][:, c * D:(c + 1) * D], wb[:, c * D:(c + 1) * D], S.eye_bf[:, :])
                mm.then_inc(ps, 1)
            loaded(pe, "cols", "w0", "w1", "gate", "eye")
            nc.tensor.matmul(bank[1][0:1, 0:D], S.cols[:, 2:3], S.wo0[:, :], start=True, stop=True)
            for j in range(H * DH1 // D):
                mm = nc.tensor.matmul(bank[1][0:1, D:2 * D], S.bvcol[:, j:j + 1], S.wo1[:, j, :],
                                      start=(j == 0), stop=(j == 7))
            mm.then_inc(ps, 1)
            nc.tensor.transpose(bank[4][:, 0:E], S.gate_w[:, :], S.eye[0:E, 0:E]).then_inc(ps, 1)

        @block.scalar
        def _(act):
            act.wait_ge(ps, 2)
            nc.scalar.copy(S.w1q[:, :], S.bank_bf[2][:, 0:F])
            act.wait_ge(ps, 3)
            nc.scalar.copy(S.w2q[:, :], S.bank_bf[3][:, 0:F])
            act.wait_ge(ps, 5)
            nc.scalar.copy(S.gate_t[:, :], bank[4][:, 0:E]).then_inc(evac, 1)


def normalise_steps(nc, S, v, L, n):
    ln, ln_pow, xn_ready = S.sem(f"ln{L}"), S.sem(f"ln_pow{L}"), S.sem(f"xn_ready{L}")
    i, p = n.i, n.p
    parts = 2 if L == 1 else 1
    per = 3 * parts

    def statistics():
        if L == 1:
            v.wait_ge(S.sem(f"ctx_in{L}_{p}"), i * 8 + (16 - 8 * p))
            nc.vector.memset(S.fence[:, :], 0.0)
            nc.vector.bn_stats(S.stats[0:KEYS, p, 1, :], S.ctx_in[:, p, :]).then_inc(ln, 1)
        nc.vector.bn_stats(S.stats[:, p, 0, :], tile_at(S.x, i, D)).then_inc(ln, 1)
        v.wait_ge(ln, i * per + parts)
        nc.vector.memset(S.fence[:, :], 0.0)
        nc.vector.bn_aggr(S.meanvar[:, p, 0, :], S.stats[:, p, 0, :]).then_inc(ln, 1)
        if L == 1:
            nc.vector.bn_aggr(S.meanvar[0:KEYS, p, 1, :], S.stats[0:KEYS, p, 1, :]).then_inc(ln, 1)
        v.wait_ge(ln, i * per + 2 * parts)
        if L == 0:
            nc.vector.tensor_scalar(S.varx[:, p, 0:1], S.meanvar[:, p, 0, 1:2], EPS, None, ALU.add).then_inc(ln, 1)
        else:
            nc.vector.tensor_scalar(S.varx[0:KEYS, p, 1:2], S.meanvar[0:KEYS, p, 1, 1:2], EPS, None, ALU.add).then_inc(ln, 1)
            nc.vector.tensor_scalar(S.varx[:, p, 0:1], S.meanvar[:, p, 0, 1:2], 1.0 + EPS, EPS * EPS,
                                    ALU.mult, ALU.add).then_inc(ln, 1)

    def scale():
        v.wait_ge(ln_pow, i + 1)
        if L == 1:
            nc.vector.tensor_scalar(S.cn[:, p, :], S.ctx_in[:, p, :], S.meanvar[0:KEYS, p, 1, 0:1], S.rstd[0:KEYS, p, 1:2],
                                    ALU.subtract, ALU.mult)
        nc.vector.tensor_scalar(S.xn[:, p, :], tile_at(S.x, i, D), S.meanvar[:, p, 0, 0:1], S.rstd[:, p, 0:1],
                                ALU.subtract, ALU.mult).then_inc(xn_ready, 1)

    return statistics, scale


def attention(nc, S, A, L):
    dh = DH1 if L else DH0
    tiles = H * dh // D
    scale = float(dh) ** -0.5
    bank = S.bank
    ST, SM, PV, M0, M1 = (0, 1), (2, 3), (4, 5), bank[6], bank[7]
    qmax, kmax = (S.qT_bf, S.kT_bf) if L else (S.qT[0], S.kT[0])
    xT, cT, qT, vaug, attn, attnT = S.xT, S.cT, S.qT[L], S.vaug[L], S.attn[L], S.attnT
    kT = S.kT[L]
    last = B - 1

    def sem(n):
        return S.sem(f"{n}{L}")

    xn_ready, a1_done, a1_out = sem("xn_ready"), sem("a1_done"), sem("a1_out")
    m1_done, m1_out, sm_done, mx_out = sem("m1_done"), sem("m1_out"), sem("sm_done"), sem("mx_out")
    mt_done, mt_out, st_done, ex_out = sem("mt_done"), sem("mt_out"), sem("st_done"), sem("ex_out")
    pv_done, pve_out, pv_rec, ta_done, ta_out = sem("pv_done"), sem("pve_out"), sem("pv_rec"), sem("ta_done"), sem("ta_out")
    o_done, o_out, tq_done, tq_out, ln, ln_pow = sem("o_done"), sem("o_out"), sem("tq_done"), sem("tq_out"), sem("ln"), sem("ln_pow")
    ctx_in = [S.sem(f"ctx_in{L}_{p}") for p in range(2)]
    tk_done, tk_out = sem("tk_done"), sem("tk_out")
    if L:
        q_ready, k_ready, v_done, v_out, mcol_out, bf_out = (sem("q_ready"), sem("k_ready"), sem("v_done"), sem("v_out"),
                                                             sem("mcol_out"), sem("bf_out"))
    else:
        split = sem("split")
    M1_USES = 4 if L else 1
    CH = 1 + L
    M0_q = M0 if L else S.bank_bf[6]
    M0_max = S.bank_bf[6]
    KT = M0 if L else S.bank_bf[7]
    XT = bank[SM[1]]
    OUT = M1 if L else bank[PV[1]]
    PVW = dh + 1 if L else 8 * (dh + 1)

    def head(half, c, s):
        return 8 * half + 2 * s + c

    def rows_of(h):
        return slice(64 * (h % 2), 64 * (h % 2) + 64)

    def kq_of(h, k, q):
        if L:
            return k[rows_of(h), h // 2, :], q[rows_of(h), h // 2, :]
        return k[:, h, :], q[:, h // 2, :]

    def max_cols(t, half, c):
        return t[:, 64 * c + 4 * half:64 * c + 4 * half + 4]

    def head_cols(t, half, c):
        return t[:, 8 * half + c:8 * half + 8:2]

    with nc.Block() as block:
        @block.sync
        def _(sp):
            def load(n, _):
                if n.lo >= 2:
                    if L:
                        sp.wait_ge(xn_ready, n.i - 1)
                    else:
                        sp.wait_ge(a1_done, n.i - 1)
                sp.dma_start(S.ctx_in[:, n.p, :], A["ctx_1024"][bass.ds(n.i, 1)].rearrange("b k d -> k (b d)")
                             ).then_inc(ctx_in[n.p], 16)
            run_steps(sp, load, 0, last, 2, 0)

        @block.gpsimd
        def _(g):
            def step(s, _):
                n, n2 = s.next(), s.next(2)

                def rotated(x, c):
                    out, c1, c2 = ((S.qrot, S.qcos, S.qsin), (S.krot, S.kcos, S.ksin))[x]
                    g.wait_ge(m1_out, n.i * 4 + (2 * x + c + 1))
                    nc.gpsimd.tensor_tensor(out[:, c, :], c1[:, c, :], c2[:, c, :], ALU.add).then_inc((q_ready, k_ready)[x], 1)
                rotary = L and 0 <= n.lo <= last
                if rotary:
                    rotated(0, 0)
                if n2.lo <= last:
                    g.wait_ge(ln, n2.i * (3 + 3 * L) + (3 + 3 * L))
                    nc.gpsimd.tensor_tensor(S.rstd[:, n2.p, 0:1 + L], S.varx[:, n2.p, 0:1 + L], S.minus_half[:, 0:1 + L],
                                            ALU.pow).then_inc(ln_pow, 1)
                if rotary:
                    rotated(0, 1)
                    rotated(1, 0)
                    rotated(1, 1)
            run_steps(g, step, -2, last, 3, 3)

        @block.vector
        def _(v):
            def split_qkv(n):
                v.wait_ge(m1_done, n.i + 1)
                both = []
                for x, (ps, parts, rest, rows) in enumerate(((M1[:, 0:D], S.qparts, S.qrest, T), (M1[0:KEYS, D:2 * D], S.kparts, S.krest, KEYS))):
                    slots = parts[:, :].rearrange("t (h s d) -> t h s d", h=H, s=8)
                    both.append((ps.rearrange("t (h d) -> t h d", h=H), slots, rest[:, :].rearrange("t (h d) -> t h d", h=H), rows,
                                 (slice(0, 3), slice(3, 5), slice(6, 7)) if x == 0 else (slice(0, 7, 3), slice(1, 5, 3), slice(2, 3))))

                def wide(ap, rows, k):
                    return ap.unsqueeze(2).to_broadcast([rows, H, k, DH0])
                for ps, slots, rest, rows, (h, m, l) in both:
                    nc.vector.tensor_copy(slots[:, :, h, :], wide(ps, rows, 3)).then_inc(split, 1)
                for x, (ps, slots, rest, rows, (h, m, l)) in enumerate(both):
                    v.wait_ge(split, n.i * 8 + (1 + x))
                    nc.vector.tensor_tensor(rest, ps, slots[:, :, 0, :], ALU.subtract).then_inc(split, 1)
                nc.vector.tensor_copy(vaug[:, n.p, :, 0:dh], M1[0:KEYS, 256:256 + D].rearrange("k (h d) -> k h d", h=H)
                                      ).then_inc(m1_out, 1)
                for x, (ps, slots, rest, rows, (h, m, l)) in enumerate(both):
                    v.wait_ge(split, n.i * 8 + (3 + x))
                    nc.vector.tensor_copy(slots[:, :, m, :], wide(rest, rows, 2)).then_inc(split, 1)
                for x, (ps, slots, rest, rows, (h, m, l)) in enumerate(both):
                    v.wait_ge(split, n.i * 8 + (5 + x))
                    nc.vector.tensor_tensor(slots[:, :, l, :].rearrange("t h one d -> t h (one d)"), rest,
                                            slots[:, :, m.start, :], ALU.subtract).then_inc(split, 1)

            def rotate(n, x, c):
                rows, cosv, sinv = (T, S.qcos, S.qsin) if x == 0 else (KEYS, S.kcos, S.ksin)
                v.wait_ge(m1_done, n.i * 4 + (2 * x + c + 1))
                ps = M1[0:rows, 0:512].rearrange("t (h d) -> t h d", h=8)
                pair = M1[0:rows, 0:512].rearrange("t (h n two) -> t h n two", h=8, two=2)
                qs = sinv[:, c, :].rearrange("t (h n two) -> t h n two", h=8, two=2)
                sn = S.sinq[0:rows, :].rearrange("t (n two) -> t n two", two=2)
                nc.vector.tensor_tensor(cosv[:, c, :].rearrange("t (h d) -> t h d", h=8), ps,
                                        S.cosq[0:rows, :].unsqueeze(1).to_broadcast([rows, 8, DH1]), ALU.mult)
                nc.vector.tensor_tensor(qs[:, :, :, 0], pair[:, :, :, 1],
                                        sn[:, :, 0].unsqueeze(1).to_broadcast([rows, 8, DH1 // 2]), ALU.mult)
                nc.vector.tensor_tensor(qs[:, :, :, 1], pair[:, :, :, 0],
                                        sn[:, :, 1].unsqueeze(1).to_broadcast([rows, 8, DH1 // 2]), ALU.mult).then_inc(m1_out, 1)

            def divide(s, half):
                for c in range(2):
                    v.wait_ge(pv_done, s.i * 4 + (2 * half + c + 1))
                    off, step = (0, dh + 1) if L else (c * (dh + 1), PVW + 2 * (dh + 1))
                    pvb = bank[PV[c]][:, off:off + 4 * step].rearrange("t (s x) -> t s x", s=4)[:, :, 0:dh + 1]
                    nc.vector.reciprocal(S.recip[:, c, :], pvb[:, :, dh]).then_inc(pv_rec, 1)
                    v.wait_ge(pv_rec, s.i * 4 + (2 * half + c + 1))
                    nc.vector.tensor_tensor(head_cols(attn[:, s.p, :].rearrange("t (h d) -> t h d", h=H), half, c), pvb[:, :, 0:dh],
                                            S.recip[:, c, :].unsqueeze(2).to_broadcast([T, 4, dh]), ALU.mult).then_inc(pve_out, 1)

            def residual(s):
                v.wait_ge(o_done, s.i + 1)
                nc.vector.tensor_tensor(tile_at(S.x, s.i, D), OUT[:, 0:D], tile_at(S.x, s.i, D), ALU.add).then_inc(o_out, 1)

            def maximum(n, half):
                for c in range(2):
                    v.wait_ge(sm_done, n.i * 4 + (2 * half + c + 1))
                    nc.vector.tensor_reduce(max_cols(S.rowmax[:, n.p, :], half, c),
                                            bank[(SM, ST)[half][c]][:, 0:4 * KEYS].rearrange("t (s k) -> t s k", s=4), AX, ALU.max
                                            ).then_inc(mx_out, 1)

            def copy_bf(n, x, c):
                v.wait_ge((tq_out, tk_out)[x], n.i * 2 + (c + 1))
                out, src = ((S.qT_bf, qT), (S.kT_bf, kT))[x]
                nc.vector.tensor_copy(out[:, 4 * c:4 * c + 4, :], src[:, n.p, 4 * c:4 * c + 4, :]).then_inc(bf_out, 1)

            def step(s, _):
                n, n2 = s.next(), s.next(2)
                cur, nxt, nxt2 = s.lo >= 0, 0 <= n.lo <= last, n2.lo <= last
                statistics, normalise = normalise_steps(nc, S, v, L, n2)
                if nxt and L:
                    rotate(n, 0, 0)
                if nxt2:
                    statistics()
                if nxt and L:
                    nc.vector.tensor_copy(S.mcol[:, n.p:n.p + 1], S.maskcol[0:KEYS, bass.ds(n.i, 1)]).then_inc(mcol_out, 1)
                    rotate(n, 0, 1)
                if nxt and L == 0:
                    split_qkv(n)
                if nxt2 and L == 0:
                    normalise()
                if s.lo >= 1 and L == 0:
                    residual(s.next(-1))
                if cur:
                    divide(s, 0)
                if nxt and L:
                    rotate(n, 1, 0)
                if nxt2 and L:
                    normalise()
                if nxt and L:
                    copy_bf(n, 0, 0)
                if cur:
                    divide(s, 1)
                if nxt and L:
                    copy_bf(n, 0, 1)
                    rotate(n, 1, 1)
                    copy_bf(n, 1, 0)
                    copy_bf(n, 1, 1)
                if cur and (L or not nxt):
                    residual(s)
                if nxt:
                    maximum(n, 0)
                    maximum(n, 1)
            run_steps(v, step, -2, last, 3, 3)

        @block.scalar
        def _(act):
            def exponent(s, half):
                for c in range(2):
                    act.wait_ge(st_done, s.i * 4 + (2 * half + c + 1))
                    if L == 0:
                        nc.scalar.activation(S.probs[:, half, c, :], bank[(ST, SM)[half][c]][0:KEYS, :], ACT.Exp, scale=scale).then_inc(ex_out, 1)
                    else:
                        if half == 0 and c == 0:
                            act.wait_ge(mcol_out, s.i + 1)
                        nc.scalar.activation(S.probs[:, half, c, :], bank[(ST, SM)[half][c]][0:KEYS, :], ACT.Exp, scale=scale,
                                             bias=S.mcol[:, s.p:s.p + 1]).then_inc(ex_out, 1)

            def copy_v(n, c):
                act.wait_ge(v_done, n.i * 2 + (c + 1))
                nc.scalar.copy(vaug[:, n.p, 8 * c:8 * c + 8, 0:dh], bank[SM[c]][0:KEYS, :].rearrange("k (h d) -> k h d", h=8)
                               ).then_inc(v_out, 1)

            def copy_q(n, c):
                w = 8 // CH
                act.wait_ge(tq_done, n.i * CH + (c + 1))
                nc.scalar.copy(qT[:, n.p, w * c:w * c + w, :].rearrange("d j t -> d (j t)"), M0_q[:, 0:w * T]).then_inc(tq_out, 1)

            def copy_k(n, c):
                w = 8 // CH
                act.wait_ge(tk_done, n.i * CH + (c + 1))
                tiles_k = KT[:, 0:w * KP].rearrange("d (j k) -> d j k", k=KP)[:, :, 0:KEYS]
                if L:
                    nc.scalar.copy(kT[:, n.p, w * c:w * c + w, :], tiles_k).then_inc(tk_out, 1)
                else:
                    nc.scalar.copy(kT[0:64, n.p, 0:H:2, :], tiles_k[0:64])
                    nc.scalar.copy(kT[64:D, n.p, 1:H:2, :], tiles_k[64:D]).then_inc(tk_out, 1)

            def copy_out(s, c):
                w = min(tiles, 4)
                act.wait_ge(ta_done, s.i * CH + (c + 1))
                nc.scalar.copy(attnT[:, 4 * c:4 * c + w, :].rearrange("d j t -> d (j t)"), bank[PV[c]][:, 0:w * T]).then_inc(ta_out, 1)

            def copy_rows(n):
                act.wait_ge(a1_done, n.i + 1)
                if L == 0:
                    nc.scalar.copy(xT[:, n.p, :], XT[:, 0:D])
                    nc.scalar.copy(cT[:, n.p, :], XT[:, D:D + KEYS]).then_inc(a1_out, 1)
                else:
                    nc.scalar.activation(xT[:, n.p, :], XT[:, 0:D], ACT.Identity, bias=S.cols[:, 4:5], scale=S.cols[:, 3:4])
                    nc.scalar.activation(cT[:, n.p, :], XT[:, D:D + KEYS], ACT.Identity, bias=S.cols[:, 4:5],
                                         scale=S.cols[:, 3:4]).then_inc(a1_out, 1)

            def step(s, _):
                n, n2 = s.next(), s.next(2)
                cur, nxt, nxt2 = s.lo >= 0, 0 <= n.lo <= last, n2.lo <= last
                if nxt and L:
                    copy_v(n, 0)
                if cur:
                    act.wait_ge(mt_done, s.i + 1)
                    nc.scalar.copy(S.maxT[:, s.p, :], M0_max[:, 0:T]).then_inc(mt_out, 1)
                if nxt and L:
                    copy_v(n, 1)
                if cur:
                    exponent(s, 0)
                    exponent(s, 1)
                if nxt:
                    copy_q(n, 0)
                    if L:
                        copy_q(n, 1)
                if cur and L:
                    copy_out(s, 0)
                if nxt:
                    copy_k(n, 0)
                if cur and L:
                    copy_out(s, 1)
                if nxt2:
                    copy_rows(n2)
                if cur and L == 0:
                    copy_out(s, 0)
                if nxt and L:
                    copy_k(n, 1)
            run_steps(act, step, -2, last, 3, 3)

        @block.tensor
        def _(pe):
            def transpose_rows(n):
                pe.wait_ge(xn_ready, n.i + 1)
                if L == 0:
                    pe.wait_ge(ctx_in[n.p], n.i * 8 + (16 - 8 * n.p))
                nc.tensor.transpose(XT[:, 0:D], S.xn[:, n.p, :], S.eye[:, :])
                c = S.cn if L else S.ctx_in
                nc.tensor.transpose(XT[:, D:D + KEYS], c[:, n.p, :], S.eye[0:KEYS, 0:KEYS]).then_inc(a1_done, 1)

            def m1_free(n):
                if L == 0:
                    if n.lo >= 1:
                        pe.wait_ge(tk_out, n.i)
                elif n.lo >= 2:
                    pe.wait_ge(o_out, n.i - 1)
                elif n.lo == 1:
                    pe.wait_ge(m1_out, M1_USES)

            def project_qkv(n):
                pe.wait_ge(a1_out, n.i + 1)
                m1_free(n)
                nc.tensor.matmul(M1[:, 0:D], S.ones_bf[0:3, :], S.bias3_0[:, 0, :], start=True, stop=False)
                nc.tensor.matmul(M1[:, 0:D], xT[:, n.p, :], S.wq0[:, :], start=False, stop=True)
                nc.tensor.matmul(M1[0:KEYS, D:2 * D], S.ones_bf[0:3, 0:KEYS], S.bias3_0[:, 1, :], start=True, stop=False)
                nc.tensor.matmul(M1[0:KEYS, D:2 * D], cT[:, n.p, :], S.wk0[:, :], start=False, stop=True)
                nc.tensor.matmul(M1[0:KEYS, 256:256 + D], cT[:, n.p, :], S.wv0[:, :], start=True, stop=True).then_inc(m1_done, 1)

            def project(n, x, c):
                if x == 0 and c == 0:
                    pe.wait_ge(a1_out, n.i + 1)
                    m1_free(n)
                else:
                    pe.wait_ge(m1_out, n.i * 4 + (2 * x + c))
                rows, src, w = ((T, xT, S.wq1), (KEYS, cT, S.wk1))[x]
                nc.tensor.matmul(M1[0:rows, :], S.ones_bf[0:3, 0:rows], S.bias3[:, x, 512 * c:512 * c + 512], start=True, stop=False)
                nc.tensor.matmul(M1[0:rows, :], src[:, n.p, :], w[:, 512 * c:512 * c + 512], start=False, stop=True).then_inc(m1_done, 1)

            def project_v(n, c):
                if n.lo >= 1 and c == 0:
                    pe.wait_ge(mx_out, n.i * 4 - 2)
                nc.tensor.matmul(bank[SM[c]][0:KEYS, :], cT[:, n.p, :], S.wv1[:, 512 * c:512 * c + 512], start=True, stop=True).then_inc(v_done, 1)

            def transpose_q(n, c):
                if L:
                    pe.wait_ge(q_ready, n.i * 2 + (c + 1))
                else:
                    pe.wait_ge(split, n.i * 8 + 7)
                if c:
                    pe.wait_ge(tq_out, n.i * 2 + 1)
                for j in range(8 // CH):
                    src = S.qrot[:, c, j * D:(j + 1) * D] if L else S.qparts[:, j * D:(j + 1) * D]
                    mm = nc.tensor.transpose(M0_q[:, j * T:(j + 1) * T], src, S.eye[:, :] if L else S.eye_bf[:, :])
                mm.then_inc(tq_done, 1)

            def transpose_k(n, c):
                if L:
                    pe.wait_ge(k_ready, n.i * 2 + (c + 1))
                else:
                    pe.wait_ge(split, n.i * 8 + 8)
                    pe.wait_ge(m1_out, n.i + 1)
                if c:
                    pe.wait_ge(tk_out, n.i * 2 + 1)
                elif L:
                    pe.wait_ge(tq_out, n.i * CH + CH)
                for j in range(8 // CH):
                    src = S.krot[:, c, j * D:(j + 1) * D] if L else S.kparts[:, j * D:(j + 1) * D]
                    mm = nc.tensor.transpose(KT[:, KP * j:KP * j + KEYS], src,
                                             S.eye[0:KEYS, 0:KEYS] if L else S.eye_bf[0:KEYS, 0:KEYS])
                mm.then_inc(tk_done, 1)

            def scores_for_max(n, half, cur, nxt2):
                banks = (SM, ST)[half]
                if half == 0:
                    if L:
                        pe.wait_ge(bf_out, n.i * 4 + 4)
                        if not cur:
                            pe.wait_ge(v_out, n.i * 2 + 2)
                    else:
                        pe.wait_ge(tk_out, n.i + 1)
                    if nxt2:
                        pe.wait_ge(a1_out, n.i + 2)
                for s4 in range(4):
                    for c in range(2):
                        h = head(half, c, s4)
                        k, q = kq_of(h, kmax[:, :, :] if L else kmax[:, n.p, :, :], qmax[:, :, :] if L else qmax[:, n.p, :, :])
                        mm = nc.tensor.matmul(bank[banks[c]][:, s4 * KEYS:(s4 + 1) * KEYS], q, k, start=(s4 == 0), stop=(L == 0),
                                              skip_group_check=True)
                        if L == 0 and s4 == 3:
                            mm.then_inc(sm_done, 1)
                if L:
                    for c in range(2):
                        nc.tensor.matmul(bank[banks[c]][:, 0:4 * KEYS], S.ones_bf[0:1, :], tile_at(S.maskrow, n.i, 4 * KEYS),
                                         start=False, stop=True, skip_group_check=True).then_inc(sm_done, 1)

            def transpose_max(n):
                if L:
                    pe.wait_ge(tk_out, n.i * CH + CH)
                else:
                    pe.wait_ge(tq_out, n.i + 1)
                pe.wait_ge(mx_out, n.i * 4 + 4)
                nc.tensor.transpose(M0_max[:, 0:T], S.rowmax[:, n.p, :], S.eye_bf[:, :]).then_inc(mt_done, 1)

            def scores(s, half, nxt):
                if half == 0:
                    pe.wait_ge(mt_out, s.i + 1)
                elif L and nxt:
                    pe.wait_ge(v_out, s.i * 2 + 4)
                for s4 in range(4):
                    for c in range(2):
                        h = head(half, c, s4)
                        out = bank[(ST, SM)[half][c]][0:KEYS, s4 * T:(s4 + 1) * T]
                        rows = rows_of(h) if L else slice(0, D)
                        k, q = kq_of(h, kT[:, s.p, :, :], qT[:, s.p, :, :])
                        nc.tensor.matmul(out, S.negsel[rows, h * KEYS:(h + 1) * KEYS], S.maxT[rows, s.p, :], start=True, stop=False)
                        mm = nc.tensor.matmul(out, k, q, start=False, stop=True)
                        if s4 == 3:
                            mm.then_inc(st_done, 1)

            def times_v(s, half):
                for c in range(2):
                    pe.wait_ge(ex_out, s.i * 4 + (2 * half + c + 1))
                    if half:
                        pe.wait_ge(pve_out, s.i * 4 + (c + 1))
                    elif L == 0 and c and s.lo >= 1:
                        pe.wait_ge(o_out, s.i)
                    if L and half == 0 and c == 0:
                        pe.wait_ge(v_out, s.i * 2 + 2)
                    for s4 in range(4):
                        out = bank[PV[c]][:, s4 * PVW:(s4 + 1) * PVW]
                        v = vaug[:, s.p, head(half, c, s4), :] if L else vaug[:, s.p, 8 * half:8 * half + 8, :].rearrange("k h d -> k (h d)")
                        mm = nc.tensor.matmul(out, S.probs[:, half, c, s4 * T:(s4 + 1) * T], v, start=True, stop=True)
                    mm.then_inc(pv_done, 1)

            def transpose_out(s, c):
                pe.wait_ge(pve_out, s.i * 4 + 4)
                for j in range(min(tiles, 4)):
                    mm = nc.tensor.transpose(bank[PV[c]][:, j * T:(j + 1) * T], attn[:, s.p, (4 * c + j) * D:(4 * c + j + 1) * D], S.eye[:, :])
                mm.then_inc(ta_done, 1)

            def project_out(s, part, nxt):
                pe.wait_ge(ta_out, s.i * CH + (part + 1))
                if part == 0:
                    if L == 0:
                        pass
                    elif nxt:
                        pe.wait_ge(m1_out, s.i * M1_USES + 2 * M1_USES)
                    elif s.lo >= 1:
                        pe.wait_ge(o_out, s.i)
                    nc.tensor.matmul(OUT[:, 0:D], S.ones_row[:, :], S.row_o[:, L, :], start=True, stop=False)
                for j in range(4 * part, min(4 * part + 4, tiles)):
                    w = S.wo1[:, j, :] if L else S.wo0[:, :]
                    mm = nc.tensor.matmul(OUT[:, 0:D], attnT[:, j, :], w, start=False, stop=(j == tiles - 1))
                if part == CH - 1:
                    mm.then_inc(o_done, 1)

            def step0(s, _):
                n, n2 = s.next(), s.next(2)
                cur, nxt, nxt2 = s.lo >= 0, 0 <= n.lo <= last, n2.lo <= last
                if nxt:
                    project_qkv(n)
                if cur:
                    transpose_max(s)
                    if s.lo >= 1:
                        project_out(s.next(-1), 0, nxt)
                    scores(s, 0, nxt)
                    scores(s, 1, nxt)
                if nxt:
                    transpose_q(n, 0)
                    transpose_k(n, 0)
                if cur:
                    times_v(s, 0)
                    pe.wait_ge(ex_out, s.i * 4 + 4)
                if nxt2:
                    transpose_rows(n2)
                if cur:
                    times_v(s, 1)
                if nxt:
                    scores_for_max(n, 0, cur, nxt2)
                if cur:
                    transpose_out(s, 0)
                if nxt:
                    scores_for_max(n, 1, cur, nxt2)
                elif cur:
                    project_out(s, 0, nxt)

            def step1(s, _):
                n, n2 = s.next(), s.next(2)
                cur, nxt, nxt2 = s.lo >= 0, 0 <= n.lo <= last, n2.lo <= last
                if nxt:
                    project(n, 0, 0)
                    project_v(n, 0)
                if cur:
                    transpose_max(s)
                if nxt:
                    project_v(n, 1)
                if cur:
                    scores(s, 0, nxt)
                if nxt:
                    project(n, 0, 1)
                if cur:
                    times_v(s, 0)
                    scores(s, 1, nxt)
                if nxt:
                    project(n, 1, 0)
                    transpose_q(n, 0)
                if cur:
                    times_v(s, 1)
                if nxt:
                    transpose_q(n, 1)
                    project(n, 1, 1)
                if cur:
                    transpose_out(s, 0)
                if nxt:
                    transpose_k(n, 0)
                if cur:
                    transpose_out(s, 1)
                if nxt2:
                    transpose_rows(n2)
                if cur:
                    project_out(s, 0, nxt)
                if nxt:
                    transpose_k(n, 1)
                if cur:
                    project_out(s, 1, nxt)
                if nxt:
                    scores_for_max(n, 0, cur, nxt2)
                    scores_for_max(n, 1, cur, nxt2)
            run_steps(pe, step1 if L else step0, -2, last, 3, 3)


def pool_fence(nc, S, g, n, phase, sem, value):
    done = S.sem(phase + "_fence")
    own = S.fence_g[:, "fdecqk".index(phase):][:, 0:1]
    if n.lo >= 1:
        g.wait_ge(done, n.i)
    g.wait_ge(sem, value)
    nc.gpsimd.tensor_tensor(own, S.minus_half[:, 0:1], S.minus_half[:, 0:1], ALU.add).then_inc(done, 1)


def ffn0(nc, S):
    last = B
    bank, bank_bf = S.bank, S.bank_bf
    ZT, H1, GT, OUT = bank[0], (bank[1], bank[2]), bank[3], bank[4]

    def sem(n):
        return S.sem(f"f_{n}")

    ln, ln_pow, zq_ready, rec = sem("ln"), sem("ln_pow"), sem("zq_ready"), sem("rec")
    zt_done, zt_out, h_done, h_out, g_ready, sq_ready = sem("zt_done"), sem("zt_out"), sem("h_done"), sem("h_out"), sem("g_ready"), sem("sq_ready")
    rms_in, rms_pow, gq_ready, gt_done, gt_out, y_done, y_out = (sem("rms_in"), sem("rms_pow"), sem("gq_ready"), sem("gt_done"),
                                                                  sem("gt_out"), sem("y_done"), sem("y_out"))
    z_done, xb_done, rec2 = sem("z_done"), sem("xb_done"), sem("rec2")

    with nc.Block() as block:
        @block.gpsimd
        def _(g):
            def step(s, _):
                n, n2 = s.next(), s.next(2)
                if n2.lo < B:
                    g.wait_ge(ln, n2.i * 3 + 3)
                    nc.gpsimd.tensor_tensor(S.rstd[:, n2.p, 0:1], S.varx[:, n2.p, 0:1], S.minus_half[:, 0:1], ALU.pow).then_inc(ln_pow, 1)
                if 0 <= n.lo < B:
                    pool_fence(nc, S, g, n, 'f', z_done, n.i + 1)
                    nc.gpsimd.tensor_tensor(tile_at(S.x, n.i, D), tile_at(S.x, n.i, D), S.b2bc[:, :], ALU.add).then_inc(xb_done, 1)
                if 0 <= s.lo < B:
                    g.wait_ge(rms_in, s.i + 1)
                    nc.gpsimd.tensor_tensor(S.rms[:, :], S.meansq[:, :], S.minus_half[:, 0:1], ALU.pow).then_inc(rms_pow, 1)
            run_steps(g, step, -2, last, 4, 3)

        @block.vector
        def _(v):
            def statistics(n):
                nc.vector.bn_stats(S.stats[:, n.p, 0, :], tile_at(S.x, n.i, D)).then_inc(ln, 1)
                v.wait_ge(ln, n.i * 3 + 1)
                nc.vector.memset(S.fence[:, :], 0.0)
                nc.vector.bn_aggr(S.meanvar[:, n.p, 0, :], S.stats[:, n.p, 0, :]).then_inc(ln, 1)
                v.wait_ge(ln, n.i * 3 + 2)
                nc.vector.tensor_scalar(S.varx[:, n.p, 0:1], S.meanvar[:, n.p, 0, 1:2], 1.0 + EPS, EPS * EPS,
                                        ALU.mult, ALU.add).then_inc(ln, 1)

            def quantise_z(n):
                p = n.p
                v.wait_ge(ln_pow, n.i + 1)
                nc.vector.tensor_scalar(S.z[:, :], tile_at(S.x, n.i, D), S.meanvar[:, p, 0, 0:1], S.rstd[:, p, 0:1],
                                        ALU.subtract, ALU.mult).then_inc(z_done, 1)
                v.wait_ge(z_done, n.i + 1)
                nc.vector.tensor_reduce(S.zmax[:, p, :], S.z[:, :], AX, ALU.max, apply_absolute_value=True).then_inc(rec, 1)
                v.wait_ge(rec, n.i * 4 + 1)
                nc.vector.tensor_scalar(S.zmax[:, p, :], S.zmax[:, p, :], EPS, None, ALU.max).then_inc(rec, 1)
                v.wait_ge(rec, n.i * 4 + 2)
                nc.vector.reciprocal(S.zinv[:, :], S.zmax[:, p, :]).then_inc(rec, 1)
                v.wait_ge(rec, n.i * 4 + 3)
                nc.vector.tensor_scalar(S.zinv[:, :], S.zinv[:, :], 127.0, None, ALU.mult).then_inc(rec, 1)
                nc.vector.tensor_scalar(S.zout[:, p, :], S.zmax[:, p, :], S.wmean127[:, 0:1], None, ALU.mult)
                v.wait_ge(rec, n.i * 4 + 4)
                nc.vector.tensor_scalar(S.zq[:, p, :], S.z[:, :], S.zinv[:, :], MAGIC, ALU.mult, ALU.add).then_inc(zq_ready, 1)

            def hidden(s):
                v.wait_ge(h_done, s.i + 1)
                nc.vector.scalar_tensor_tensor(S.hid[:, s.p, :], H1[s.p][:, :], S.zout[:, s.p, :], S.b1bc[:, :],
                                               ALU.mult, ALU.add).then_inc(h_out, 1)

            def quantise_g(s):
                v.wait_ge(sq_ready, s.i + 1)
                nc.vector.tensor_scalar(S.meansq[:, :], S.sumsq[:, :], 1.0 / F, EPS, ALU.mult, ALU.add).then_inc(rms_in, 1)
                nc.vector.tensor_reduce(S.gmax[:, :], S.gel[:, s.p, :], AX, ALU.max, apply_absolute_value=True).then_inc(rec2, 1)
                v.wait_ge(rec2, s.i * 5 + 1)
                v.wait_ge(rms_pow, s.i + 1)
                nc.vector.tensor_scalar(S.gmax[:, :], S.gmax[:, :], S.rms[:, :], EPS, ALU.mult, ALU.max).then_inc(rec2, 1)
                v.wait_ge(rec2, s.i * 5 + 2)
                nc.vector.reciprocal(S.ginv[:, :], S.gmax[:, :]).then_inc(rec2, 1)
                nc.vector.tensor_scalar(S.gout[:, s.p, :], S.gmax[:, :], S.wmean127[:, 1:2], None, ALU.mult).then_inc(rec2, 1)
                v.wait_ge(rec2, s.i * 5 + 4)
                nc.vector.tensor_scalar(S.ginv[:, :], S.ginv[:, :], S.rms[:, :], 127.0, ALU.mult, ALU.mult).then_inc(rec2, 1)
                v.wait_ge(rec2, s.i * 5 + 5)
                nc.vector.tensor_scalar(S.gq[:, s.p, :], S.gel[:, s.p, :], S.ginv[:, :], MAGIC, ALU.mult, ALU.add).then_inc(gq_ready, 1)

            def residual(b):
                v.wait_ge(xb_done, b.i + 1)
                v.wait_ge(y_done, b.i + 1)
                nc.vector.scalar_tensor_tensor(tile_at(S.x, b.i, D), OUT[:, 0:D], S.gout[:, b.p, :], tile_at(S.x, b.i, D),
                                               ALU.mult, ALU.add).then_inc(y_out, 1)

            def step(s, _):
                n, n2, b = s.next(), s.next(2), s.next(-1)
                if n2.lo < B:
                    statistics(n2)
                if 0 <= s.lo < B:
                    hidden(s)
                if b.lo >= 0:
                    residual(b)
                if 0 <= n.lo < B:
                    quantise_z(n)
                if 0 <= s.lo < B:
                    quantise_g(s)
            run_steps(v, step, -2, last, 4, 3)

        @block.scalar
        def _(act):
            def step(s, _):
                n = s.next()
                if 0 <= s.lo < B:
                    act.wait_ge(h_out, s.i + 1)
                    nc.scalar.activation(S.gel[:, s.p, :], S.hid[:, s.p, :], ACT.Gelu).then_inc(g_ready, 1)
                    act.wait_ge(g_ready, s.i + 1)
                    nc.scalar.activation(S.gsq[:, :], S.gel[:, s.p, :], ACT.Square, accum_out=S.sumsq[:, :]).then_inc(sq_ready, 1)
                if 0 <= n.lo < B:
                    act.wait_ge(zt_done, n.i + 1)
                    nc.scalar.activation(S.zT[:, n.p, :], ZT[:, 0:T], ACT.Identity, bias=S.minus_magic[:, :]).then_inc(zt_out, 1)
                if 0 <= s.lo < B:
                    act.wait_ge(gt_done, s.i + 1)
                    nc.scalar.activation(S.gT[:, :], GT[:, :], ACT.Identity, bias=S.minus_magic[:, :]).then_inc(gt_out, 1)
            run_steps(act, step, -2, last, 4, 3)

        @block.tensor
        def _(pe):
            def step(s, _):
                n = s.next()
                if 0 <= n.lo < B:
                    pe.wait_ge(zq_ready, n.i + 1)
                    if n.lo >= 1:
                        pe.wait_ge(zt_out, n.i)
                    nc.tensor.transpose(ZT[:, 0:T], S.zq[:, n.p, :], S.eye[:, :]).then_inc(zt_done, 1)
                    pe.wait_ge(zt_out, n.i + 1)
                    if n.lo >= 2:
                        pe.wait_ge(h_out, n.i - 1)
                    nc.tensor.matmul(H1[n.p][:, :], S.zT[:, n.p, :], S.w1q[:, :], start=True, stop=True).then_inc(h_done, 1)
                if 0 <= s.lo < B:
                    pe.wait_ge(gq_ready, s.i + 1)
                    if s.lo >= 1:
                        pe.wait_ge(gt_out, s.i)
                    for c in range(F // D):
                        mm = nc.tensor.transpose(GT[:, c * T:(c + 1) * T], S.gq[:, s.p, c * D:(c + 1) * D], S.eye[:, :])
                    mm.then_inc(gt_done, 1)
                    pe.wait_ge(gt_out, s.i + 1)
                    if s.lo >= 1:
                        pe.wait_ge(y_out, s.i)
                    for c in range(F // D):
                        mm = nc.tensor.matmul(OUT[:, 0:D], S.gT[:, c * T:(c + 1) * T], S.w2q[:, c * D:(c + 1) * D],
                                              start=(c == 0), stop=(c == F // D - 1))
                    mm.then_inc(y_done, 1)
            run_steps(pe, step, -2, last, 4, 3)


def dispatch(nc, S):
    last = B
    bank = S.bank
    XT, LG, CUM = bank[0], bank[1], bank[2]

    def sem(n):
        return S.sem(f"d_{n}")

    ln, ln_pow, xn_ready = sem("ln"), sem("ln_pow"), sem("xn_ready")
    xt_done, xt_out, lg_done, lg_out, ch, idx_ready, ex_done = (sem("xt_done"), sem("xt_out"), sem("lg_done"), sem("lg_out"), sem("choice"),
                                                                sem("idx_ready"), sem("ex_done"))
    oh_ready, count_ready, cum_done, place, slot_ready = sem("oh_ready"), sem("count_ready"), sem("cum_done"), sem("place"), sem("slot_ready")
    xg_ready = sem("xg_ready")
    scattered = [S.sem(f"scattered{p}") for p in range(2)]

    with nc.Block() as block:
        @block.gpsimd
        def _(g):
            def step(s, _):
                n2, b = s.next(2), s.next(-1)
                if n2.lo < B:
                    g.wait_ge(ln, n2.i * 3 + 3)
                    nc.gpsimd.tensor_tensor(S.rstd[:, n2.p, 0:1], S.varx[:, n2.p, 0:1], S.minus_half[:, 0:1], ALU.pow).then_inc(ln_pow, 1)
                if b.lo >= 0:
                    pool_fence(nc, S, g, b, 'd', slot_ready, b.i + 1)
                    nc.gpsimd.indirect_dma_start(out=S.dispatch[:, :], out_offset=bass.IndirectOffsetOnAxis(ap=S.row_to[:, b.p:b.p + 1], axis=0),
                                                 in_=S.xg[:, b.p, :], in_offset=None).then_inc(scattered[b.p], 16)
            run_steps(g, step, -2, last, 4, 3)
            for p in range(2):
                g.wait_ge(scattered[p], 16 * B // 2)

        @block.vector
        def _(v):
            def statistics(n):
                nc.vector.bn_stats(S.stats[:, n.p, 0, :], tile_at(S.x, n.i, D)).then_inc(ln, 1)
                v.wait_ge(ln, n.i * 3 + 1)
                nc.vector.memset(S.fence[:, :], 0.0)
                nc.vector.bn_aggr(S.meanvar[:, n.p, 0, :], S.stats[:, n.p, 0, :]).then_inc(ln, 1)
                v.wait_ge(ln, n.i * 3 + 2)
                nc.vector.tensor_scalar(S.varx[:, n.p, 0:1], S.meanvar[:, n.p, 0, 1:2], EPS, None, ALU.add).then_inc(ln, 1)

            def normalise(n):
                if n.lo >= 2:
                    v.wait_ge(xg_ready, n.i - 1)
                v.wait_ge(ln_pow, n.i + 1)
                nc.vector.tensor_scalar(S.xn[:, n.p, :], tile_at(S.x, n.i, D), S.meanvar[:, n.p, 0, 0:1], S.rstd[:, n.p, 0:1],
                                        ALU.subtract, ALU.mult).then_inc(xn_ready, 1)

            def choose(s):
                i, p = s.i, s.p
                v.wait_ge(lg_done, i + 1)
                nc.vector.tensor_copy(S.logits[:, p, :], LG[:, 0:E]).then_inc(lg_out, 1)
                v.wait_ge(lg_out, i + 1)
                nc.vector.memset(S.fence[:, :], 0.0)
                nc.vector.max(S.top8[:, :], S.logits[:, p, :]).then_inc(ch, 1)
                v.wait_ge(ch, i * 3 + 1)
                nc.vector.memset(S.fence[:, :], 0.0)
                nc.vector.max_index(S.idx8[:, :], S.top8[:, :], S.logits[:, p, :]).then_inc(ch, 1)
                nc.vector.tensor_scalar(S.minus_top[:, p:p + 1], S.top8[:, 0:1], -1.0, None, ALU.mult).then_inc(idx_ready, 1)
                v.wait_ge(ch, i * 3 + 2)
                nc.vector.tensor_copy(S.expert[:, p:p + 1], S.idx8[:, 0:1]).then_inc(ch, 1)
                v.wait_ge(ch, i * 3 + 3)
                nc.vector.tensor_scalar(S.onehot[:, p, :], S.experts[:, :], S.expert[:, p:p + 1], None, ALU.is_equal).then_inc(oh_ready, 1)
                v.wait_ge(oh_ready, i + 1)
                if s.lo >= 1:
                    v.wait_ge(cum_done, i)
                nc.vector.tensor_tensor(S.count[:, p, :], S.count[:, 1 - p, :], S.onehot[:, p, :], ALU.add).then_inc(count_ready, 1)
                if s.lo >= 2:
                    v.wait_ge(scattered[p], i * 8 - 8 * p)
                nc.vector.tensor_copy(S.xg[:, p, :], S.xn[:, p, :]).then_inc(xg_ready, 1)

            def places(b):
                i, p = b.i, b.p
                v.wait_ge(cum_done, i + 1)
                nc.vector.tensor_tensor_reduce(out=S.picked[:, :], in0=CUM[:, 0:E], in1=S.onehot[:, p, :], scale=1.0, scalar=0.0,
                                               op0=ALU.mult, op1=ALU.add, accum_out=S.pos[:, :]).then_inc(place, 1)
                v.wait_ge(place, i * 6 + 1)
                nc.vector.tensor_scalar(S.keep[:, :], S.pos[:, :], float(CAP), None, ALU.is_le).then_inc(place, 1)
                v.wait_ge(place, i * 6 + 2)
                nc.vector.tensor_scalar(S.pos[:, :], S.pos[:, :], -1.0, S.keep[:, :], ALU.add, ALU.mult).then_inc(place, 1)
                v.wait_ge(place, i * 6 + 3)
                nc.vector.tensor_scalar(S.row_f[:, :], S.expert[:, p:p + 1], float(CAP), S.pos[:, :], ALU.mult, ALU.add).then_inc(place, 1)
                v.wait_ge(place, i * 6 + 4)
                nc.vector.tensor_copy(S.row_from[:, bass.ds(i, 1)], S.row_f[:, :])
                nc.vector.tensor_tensor(S.row_g[:, :], S.row_f[:, :], S.dropped_row[:, bass.ds(i, 1)], ALU.subtract).then_inc(place, 1)
                v.wait_ge(place, i * 6 + 5)
                if b.lo >= 2:
                    v.wait_ge(scattered[p], i * 8 - 8 * p)
                nc.vector.scalar_tensor_tensor(S.row_to[:, p:p + 1], S.row_g[:, :], S.keep[:, :], S.dropped_row[:, bass.ds(i, 1)],
                                               ALU.mult, ALU.add).then_inc(slot_ready, 1)
                v.wait_ge(ex_done, i + 1)
                nc.vector.reciprocal(S.top_prob[:, :], S.sumexp[:, p:p + 1]).then_inc(place, 1)
                v.wait_ge(place, i * 6 + 6)
                nc.vector.tensor_tensor(S.weight[:, bass.ds(i, 1)], S.top_prob[:, :], S.keep[:, :], ALU.mult)

            def step(s, _):
                n, n2, b = s.next(), s.next(2), s.next(-1)
                if n2.lo < B:
                    statistics(n2)
                if b.lo >= 0:
                    places(b)
                if 0 <= s.lo < B:
                    choose(s)
                if n2.lo < B:
                    normalise(n2)
            run_steps(v, step, -2, last, 4, 3)

        @block.scalar
        def _(act):
            def step(s, _):
                n = s.next()
                if 0 <= n.lo < B:
                    act.wait_ge(xt_done, n.i + 1)
                    nc.scalar.copy(S.xT[:, n.p, :], XT[:, 0:D]).then_inc(xt_out, 1)
                if 0 <= s.lo < B:
                    act.wait_ge(idx_ready, s.i + 1)
                    nc.scalar.activation(S.exps[:, :], S.logits[:, s.p, :], ACT.Exp, bias=S.minus_top[:, s.p:s.p + 1],
                                         accum_out=S.sumexp[:, s.p:s.p + 1]).then_inc(ex_done, 1)
            run_steps(act, step, -2, last, 4, 3)

        @block.tensor
        def _(pe):
            def step(s, _):
                n = s.next()
                if 0 <= n.lo < B:
                    pe.wait_ge(xn_ready, n.i + 1)
                    if n.lo >= 1:
                        pe.wait_ge(xt_out, n.i)
                    nc.tensor.transpose(XT[:, 0:D], S.xn[:, n.p, :], S.eye[:, :]).then_inc(xt_done, 1)
                    pe.wait_ge(xt_out, n.i + 1)
                    if n.lo >= 1:
                        pe.wait_ge(lg_out, n.i)
                    nc.tensor.matmul(LG[:, 0:E], S.ones_row[:, :], S.gate_b[:, :], start=True, stop=False)
                    nc.tensor.matmul(LG[:, 0:E], S.xT[:, n.p, :], S.gate_t[:, :], start=False, stop=True).then_inc(lg_done, 1)
                if 0 <= s.lo < B:
                    pe.wait_ge(oh_ready, s.i + 1)
                    if s.lo >= 1:
                        pe.wait_ge(place, s.i * 6 - 5)
                        pe.wait_ge(count_ready, s.i)
                    nc.tensor.matmul(CUM[:, 0:E], S.upto[:, :], S.onehot[:, s.p, :], start=True, stop=False)
                    nc.tensor.matmul(CUM[:, 0:E], S.ones_bf[:, :], S.count[:, 1 - s.p, :], start=False, stop=True).then_inc(cum_done, 1)
            run_steps(pe, step, -2, last, 4, 3)


def experts(nc, S, A):
    last = E - 1
    bank = S.bank
    XT, HID, Y = bank[0], bank[1:5], bank[5:7]
    CHUNKS = F // D
    RT = [(r, min(T, CAP - r)) for r in range(0, CAP, T)]

    def sem(n):
        return S.sem(f"e_{n}")

    rows_in = [sem(f"rows_in{p}") for p in range(2)]
    w_in = [sem(f"w_in{p}") for p in range(2)]
    stored = [sem(f"stored{p}") for p in range(2)]
    W_LOADS = 4 * 16
    R_LOADS = 2 * 16
    xt_done, xt_out, h_done, h_act, h_dve, y_done, y_out = (sem("xt_done"), sem("xt_out"), sem("h_done"), sem("h_act"), sem("h_dve"),
                                                            sem("y_done"), sem("y_out"))
    full = RT[-1][0]

    with nc.Block() as block:
        @block.sync
        def _(sp):
            def load(n, _):
                e, p = n.i, n.p
                if n.lo >= 2:
                    sp.wait_ge(xt_done, e - 1)
                sp.dma_start(S.erows[:, p, 0:full // T, :], S.dispatch[bass.ds(e * CAP, full), :].rearrange("(r t) d -> t r d", t=T)
                             ).then_inc(rows_in[p], 16)
                sp.dma_start(S.erows[0:CAP - full, p, full // T, :], S.dispatch[bass.ds(e * CAP + full, CAP - full), :]).then_inc(rows_in[p], 16)
                if n.lo >= 2:
                    sp.wait_ge(y_done, e - 1)
                    sp.wait_ge(h_act, e * 2 - 2)
                    sp.wait_ge(h_dve, e * 2 - 2)
                sp.dma_start(S.ew1[:, p, :], A["L1_ffn_w1"][bass.ds(e, 1)].rearrange("e d f -> d (e f)")).then_inc(w_in[p], 16)
                sp.dma_start(S.eb1[:, p, :], A["L1_ffn_b1"][bass.ds(e, 1)].rearrange("e (c f) -> f (e c)", f=D), allow_slow_non_contiguous=True).then_inc(w_in[p], 16)
                sp.dma_start(S.ew2[:, p, :, :], A["L1_ffn_w2"][bass.ds(e, 1)].rearrange("e (c f) d -> f (e c) d", f=D)).then_inc(w_in[p], 16)
                sp.dma_start(S.eb2[:, p, :], A["L1_ffn_b2"][bass.ds(e, 1), :]).then_inc(w_in[p], 16)
            run_steps(sp, load, 0, last, 2, 0)

        @block.gpsimd
        def _(g):
            def store(n, _):
                e, p = n.i, n.p
                pool_fence(nc, S, g, n, 'e', y_out, e + 1)
                g.dma_start(S.results[bass.ds(e * CAP, full), :].rearrange("(r t) d -> t r d", t=T), S.eout[:, p, 0:full // T, :]
                            ).then_inc(stored[p], 16)
                g.dma_start(S.results[bass.ds(e * CAP + full, CAP - full), :], S.eout[0:CAP - full, p, full // T, :]).then_inc(stored[p], 16)
            run_steps(g, store, 0, last, 2, 0)
            for p in range(2):
                g.wait_ge(stored[p], 32 * E // 2)

        @block.tensor
        def _(pe):
            def step(s, _):
                n = s.next()
                if n.lo <= last:
                    pe.wait_ge(rows_in[n.p], n.i * 16 + (32 - 16 * n.p))
                    if n.lo >= 1:
                        pe.wait_ge(xt_out, n.i)
                    for r, (r0, rows) in enumerate(RT):
                        mm = nc.tensor.transpose(XT[:, r0:r0 + rows], S.erows[0:rows, n.p, r, :], S.eye[0:rows, 0:rows])
                    mm.then_inc(xt_done, 1)
                if s.lo >= 0:
                    e, p = s.i, s.p
                    pe.wait_ge(xt_out, e + 1)
                    pe.wait_ge(w_in[p], e * 32 + (64 - 32 * p))
                    if s.lo >= 1:
                        pe.wait_ge(h_act, e * 2)
                        pe.wait_ge(h_dve, e * 2)
                    for c in range(CHUNKS):
                        nc.tensor.matmul(HID[c][:, 0:CAP], S.ew1[:, p, c * D:(c + 1) * D], S.eXT[:, p, :], start=True, stop=True).then_inc(h_done, 1)
                    pe.wait_ge(h_act, e * 2 + 2)
                    pe.wait_ge(h_dve, e * 2 + 2)
                    if s.lo >= 2:
                        pe.wait_ge(y_out, e - 1)
                    for r, (r0, rows) in enumerate(RT):
                        out = Y[p][0:rows, r * D:(r + 1) * D]
                        nc.tensor.matmul(out, S.ones_row[:, 0:rows], S.eb2[:, p, :], start=True, stop=False)
                        for c in range(CHUNKS):
                            mm = nc.tensor.matmul(out, S.ehid[:, c, r0:r0 + rows], S.ew2[:, p, c, :], start=False, stop=(c == CHUNKS - 1))
                    mm.then_inc(y_done, 1)
            run_steps(pe, step, -1, last, 3, 2)

        @block.scalar
        def _(act):
            def step(s, _):
                n = s.next()
                if n.lo <= last:
                    act.wait_ge(xt_done, n.i + 1)
                    nc.scalar.copy(S.eXT[:, n.p, :], XT[:, 0:CAP]).then_inc(xt_out, 1)
                if s.lo >= 0:
                    for c in (0, 2):
                        act.wait_ge(h_done, s.i * 4 + (c + 1))
                        if c == 0 and s.lo >= 1:
                            act.wait_ge(y_done, s.i)
                        nc.scalar.activation(S.ehid[:, c, :], HID[c][:, 0:CAP], ACT.Relu, bias=S.eb1[:, s.p, c:c + 1]).then_inc(h_act, 1)
            run_steps(act, step, -1, last, 3, 2)

        @block.vector
        def _(v):
            def step(s, _):
                if s.lo < 0:
                    return
                for c in (1, 3):
                    v.wait_ge(h_done, s.i * 4 + (c + 1))
                    if c == 1 and s.lo >= 1:
                        v.wait_ge(y_done, s.i)
                    nc.vector.tensor_scalar(S.ehid[:, c, :], HID[c][:, 0:CAP], S.eb1[:, s.p, c:c + 1], 0.0, ALU.add, ALU.max).then_inc(h_dve, 1)
                v.wait_ge(y_done, s.i + 1)
                if s.lo >= 2:
                    v.wait_ge(stored[s.p], s.i * 16 - 16 * s.p)
                nc.vector.tensor_copy(S.eout[:, s.p, 0:full // T, :].rearrange("t r d -> t (r d)"), Y[s.p][:, 0:full])
                nc.vector.tensor_copy(S.eout[0:CAP - full, s.p, full // T, :], Y[s.p][0:CAP - full, full:full + D]).then_inc(y_out, 1)
            run_steps(v, step, -1, last, 3, 2)


def combine(nc, S, out):
    def sem(n):
        return S.sem(f"c_{n}")
    gathered = [sem(f"gathered{p}") for p in range(2)]
    row_ready, x_ready, written = sem("row_ready"), sem("x_ready"), sem("written")

    with nc.Block() as block:
        @block.vector
        def _(v):
            def step(s, _):
                n = s.next()
                if n.lo < B:
                    if n.lo >= 2:
                        v.wait_ge(gathered[n.p], n.i * 8 - 8 * n.p)
                    nc.vector.tensor_copy(S.row_now[:, n.p:n.p + 1], S.row_from[:, bass.ds(n.i, 1)]).then_inc(row_ready, 1)
                if s.lo >= 0:
                    v.wait_ge(gathered[s.p], s.i * 8 + (16 - 8 * s.p))
                    nc.vector.scalar_tensor_tensor(tile_at(S.x, s.i, D), S.xg[:, s.p, :], S.weight[:, bass.ds(s.i, 1)], tile_at(S.x, s.i, D),
                                                   ALU.mult, ALU.add).then_inc(x_ready, 1)
            run_steps(v, step, -1, B - 1, 3, 2)

        @block.gpsimd
        def _(g):
            def step(n, _):
                if n.lo >= 2:
                    g.wait_ge(x_ready, n.i - 1)
                pool_fence(nc, S, g, n, 'c', row_ready, n.i + 1)
                nc.gpsimd.indirect_dma_start(out=S.xg[:, n.p, :], out_offset=None, in_=S.results[:, :],
                                             in_offset=bass.IndirectOffsetOnAxis(ap=S.row_now[:, n.p:n.p + 1], axis=0)
                                             ).then_inc(gathered[n.p], 16)
            run_steps(g, step, 0, B - 1, 2, 0)

        @block.sync
        def _(sp):
            def step(n, _):
                sp.wait_ge(x_ready, n.i + 1)
                sp.dma_start(out[bass.ds(n.i, 1)].rearrange("b t d -> t (b d)"), tile_at(S.x, n.i, D)).then_inc(written, 16)
            run_steps(sp, step, 0, B - 1, 2, 0)
            sp.wait_ge(written, 16 * B)


def program(nc, A, out):
    with ExitStack() as ctx:
        S = Store(nc, ctx)
        sb = S.sb
        S.bank = [ctx.enter_context(nc.psum_tensor(f"bank{b}", [D, 512], F32)) for b in range(8)]
        S.bank_bf = [b[:, :].bitcast(BF16) for b in S.bank]
        S.dispatch = nc.dram_tensor("dispatch", (ROWS + B * T, D), F32, kind="Internal").ap()
        S.results = nc.dram_tensor("results", (ROWS, D), F32, kind="Internal").ap()
        S.eye = sb("eye", [D, D])
        S.eye_bf = sb("eye_bf", [D, D], BF16)
        S.x = sb("x", [T, B * D])
        S.cols = sb("cols", [D, 5])
        S.bvcol = sb("bvcol", [D, 8])
        S.wq0, S.wk0, S.wv0, S.wo0 = (sb(w, [D, D]) for w in ("wq0", "wk0", "wv0", "wo0"))
        S.row_o = sb("row_o", [1, 2, D])
        S.negsel = sb("negsel", [D, H * KEYS], BF16)
        S.len_i = sb("len_i", [D, B], I32)
        S.len_f = sb("len_f", [D, B])
        S.w1n = sb("w1n", [D, 4, D])
        S.w2n = sb("w2n", [D, F])
        S.w1t = sb("w1t", [D, F], BF16)
        S.w2t = sb("w2t", [D, F], BF16)
        S.w1q = sb("w1q", [D, F], BF16)
        S.w2q = sb("w2q", [D, F], BF16)
        S.b1bc = sb("b1bc", [D, F])
        S.b2bc = sb("b2bc", [D, D])
        S.bias8 = sb("bias8", [D, 2, 8])
        S.bias_row = sb("bias_row", [1, 2, D])
        S.parts_row = sb("parts_row", [1, 3, 2, D], BF16)
        S.bias3_0 = sb("bias3_0", [3, 2, D], BF16)
        S.parts = sb("parts", [D, 3, 2, 8], BF16)
        S.bias3 = sb("bias3", [3, 2, H * DH1], BF16)
        S.kpos = sb("kpos", [D, 1])
        S.krow = sb("krow", [1, KEYS])
        S.maskrow32 = sb("maskrow32", [1, B, KEYS])
        S.maskrow = sb("maskrow", [1, B * 4 * KEYS], BF16)
        S.maskcol = sb("maskcol", [D, B])
        S.mcol = sb("mcol", [KEYS, 2])
        S.wq1, S.wk1, S.wv1 = (sb(w, [D, H * DH1]) for w in ("wq1", "wk1", "wv1"))
        S.wo1 = sb("wo1", [D, 8, D])
        S.cosq = sb("cosq", [T, DH1])
        S.sinq = sb("sinq", [T, DH1])
        S.gate_w = sb("gate_w", [E, D])
        S.gate_b = sb("gate_b", [1, E])
        S.gate_t = sb("gate_t", [D, E])
        S.upto32 = sb("upto32", [D, D])
        S.upto = sb("upto", [D, D], BF16)
        S.experts = sb("experts", [D, E])
        S.dropped_row = sb("dropped_row", [D, B])
        S.ones_row = sb("ones_row", [1, D])
        S.ones_bf = sb("ones_bf", [D, D], BF16)
        S.ones_mean = sb("ones_mean", [D, D])
        S.wabs = sb("wabs", [D, 2])
        S.wmean = sb("wmean", [D, 2])
        S.wscale = sb("wscale", [D, 2])
        S.wmean127 = sb("wmean127", [D, 2])
        S.minus_half = sb("minus_half", [D, 2])
        S.minus_magic = sb("minus_magic", [D, 1])
        S.fence = sb("fence", [D, 1])
        S.fence_g = sb("fence_g", [D, 6])
        S.stats = sb("stats", [D, 2, 2, 6])
        S.meanvar = sb("meanvar", [D, 2, 2, 2])
        S.varx = sb("varx", [D, 2, 2])
        S.rstd = sb("rstd", [D, 2, 2])
        S.xn = sb("xn", [T, 2, D])
        S.ctx_in = sb("ctx_in", [KEYS, 2, D])
        S.cn = sb("cn", [KEYS, 2, D])
        S.xT = sb("xT", [D, 2, T])
        S.cT = sb("cT", [D, 2, KEYS])
        S.qT = [sb("qT0", [D, 2, 8, T], BF16), sb("qT1", [D, 2, 8, T])]
        S.kT = [sb("kT0", [D, 2, H, KEYS], BF16), sb("kT1", [D, 2, 8, KEYS])]
        S.qT_bf, S.kT_bf = sb("qT_bf", [D, 8, T], BF16), sb("kT_bf", [D, 8, KEYS], BF16)
        S.qparts, S.kparts = sb("qparts", [T, 8 * D], BF16), sb("kparts", [KEYS, 8 * D], BF16)
        S.qrest, S.krest = sb("qrest", [T, D]), sb("krest", [KEYS, D])
        S.vaug = [sb("vaug0", [KEYS, 2, H, DH0 + 1]), sb("vaug1", [KEYS, 2, H, DH1 + 1])]
        S.rowmax = sb("rowmax", [T, 2, D], BF16)
        S.maxT = sb("maxT", [D, 2, T], BF16)
        S.probs = sb("probs", [KEYS, 2, 2, 4 * T])
        S.attn = [sb("attn0", [T, 2, H * DH0]), sb("attn1", [T, 2, H * DH1])]
        S.attnT = sb("attnT", [D, 8, T])
        S.recip = sb("recip", [T, 2, 4])
        S.qcos = sb("qcos", [T, 2, 512])
        S.qsin = sb("qsin", [T, 2, 512])
        S.qrot = sb("qrot", [T, 2, 512])
        S.kcos = sb("kcos", [KEYS, 2, 512])
        S.ksin = sb("ksin", [KEYS, 2, 512])
        S.krot = sb("krot", [KEYS, 2, 512])
        S.z = sb("z", [T, D])
        S.zmax = sb("zmax", [T, 2, 1])
        S.zinv = sb("zinv", [T, 1])
        S.zout = sb("zout", [T, 2, 1])
        S.zq = sb("zq", [T, 2, D])
        S.zT = sb("zT", [D, 2, T], BF16)
        S.hid = sb("hid", [T, 2, F])
        S.gel = sb("gel", [T, 2, F])
        S.gsq = sb("gsq", [T, F])
        S.sumsq = sb("sumsq", [T, 1])
        S.meansq = sb("meansq", [T, 1])
        S.rms = sb("rms", [T, 1])
        S.gmax = sb("gmax", [T, 1])
        S.ginv = sb("ginv", [T, 1])
        S.gout = sb("gout", [T, 2, 1])
        S.gq = sb("gq", [T, 2, F])
        S.gT = sb("gT", [D, F], BF16)
        S.logits = sb("logits", [T, 2, E])
        S.top8 = sb("top8", [T, 8])
        S.idx8 = sb("idx8", [T, 8], U32)
        S.minus_top = sb("minus_top", [T, 2])
        S.expert = sb("expert", [T, 2])
        S.onehot = sb("onehot", [T, 2, E], BF16)
        S.count = sb("count", [T, 2, E], BF16)
        S.exps = sb("exps", [T, E])
        S.sumexp = sb("sumexp", [T, 2])
        S.picked = sb("picked", [T, E])
        S.pos = sb("pos", [T, 1])
        S.keep = sb("keep", [T, 1])
        S.row_f = sb("row_f", [T, 1])
        S.row_g = sb("row_g", [T, 1])
        S.top_prob = sb("top_prob", [T, 1])
        S.row_from = sb("row_from", [T, B], I32)
        S.row_to = sb("row_to", [T, 2], I32)
        S.weight = sb("weight", [T, B])
        S.row_now = sb("row_now", [T, 2], I32)
        S.xg = sb("xg", [T, 2, D])
        S.erows = sb("erows", [T, 2, 3, D])
        S.eXT = sb("eXT", [D, 2, CAP])
        S.ew1 = sb("ew1", [D, 2, F])
        S.ew2 = sb("ew2", [D, 2, 4, D])
        S.eb1 = sb("eb1", [D, 2, 4])
        S.eb2 = sb("eb2", [1, 2, D])
        S.ehid = sb("ehid", [D, 4, CAP])
        S.eout = sb("eout", [T, 2, 3, D])
        with nc.sbuf_tensor("zeros", [D, ROWS // 2], F32) as z, nc.sbuf_tensor("negsel32", [D, H * KEYS], F32) as n32:
            S.zeros, S.negsel32 = z, n32
            setup(nc, S, A)
        for k in STAGES:
            k(nc, S, A, out)


STAGES = [lambda nc, S, A, out: attention(nc, S, A, 0), lambda nc, S, A, out: ffn0(nc, S),
          lambda nc, S, A, out: attention(nc, S, A, 1), lambda nc, S, A, out: dispatch(nc, S),
          lambda nc, S, A, out: experts(nc, S, A), lambda nc, S, A, out: combine(nc, S, out)]


def shape_constants():
    f = np.float32
    d, h = np.arange(D), np.arange(H)
    t = np.arange(T, dtype=f)
    inv_freq = (f(1.0) / f(10000.0) ** (np.arange(0, DH1, 2, dtype=f) / f(DH1))).astype(f)
    angle = (t[:, None] * inv_freq[None, :]).astype(f)
    cos, sin = np.repeat(np.cos(angle), 2, 1).astype(f), np.repeat(np.sin(angle), 2, 1).astype(f)
    sign = np.where(np.arange(DH1) % 2 == 0, f(-1), f(1))
    return {
        "c_eye": np.eye(D, dtype=f),
        "c_negsel": np.repeat(-(d[:, None] == (64 * (h % 2) + h // 2)[None, :]).astype(f), KEYS, axis=1),
        "c_kpos": d.astype(f).reshape(D, 1),
        "c_krow": np.arange(KEYS, dtype=f).reshape(1, KEYS),
        "c_cosq": cos, "c_sinq": (sin * sign).astype(f),
        "c_upto": (d[:, None] <= d[None, :]).astype(f),
        "c_experts": np.tile(np.arange(E, dtype=f), (D, 1)),
        "c_dropped": (ROWS + np.arange(B)[None, :] * T + d[:, None]).astype(f),
    }


_INS = ['x', 'ctx_1024', '_lenS2', 'L0_xattn_q_w', 'L0_xattn_q_b', 'L0_xattn_k_w', 'L0_xattn_k_b', 'L0_xattn_v_w', 'L0_xattn_v_b',
        'L0_xattn_o_w', 'L0_xattn_o_b', 'L0_ffn_w1', 'L0_ffn_b1', 'L0_ffn_w2', 'L0_ffn_b2', 'L1_xattn_ln_g', 'L1_xattn_ln_b',
        'L1_xattn_Wq', 'L1_xattn_bq', 'L1_xattn_Wk', 'L1_xattn_bk', 'L1_xattn_Wv', 'L1_xattn_bv', 'L1_xattn_Wo', 'L1_xattn_bo',
        'L1_ffn_gate_w', 'L1_ffn_gate_b', 'L1_ffn_w1', 'L1_ffn_b1', 'L1_ffn_w2', 'L1_ffn_b2']


def kernel(**inputs):
    import concourse.bacc as _bacc
    from concourse.bass_utils import run_bass_kernel_spmd as _run

    nc = _bacc.Bacc("TRN2", target_bir_lowering=False, num_devices=1)
    arrays = {name: np.ascontiguousarray(inputs[name]) for name in _INS}
    arrays.update(shape_constants())
    aps = {name: nc.dram_tensor("in_" + name, a.shape, mybir.dt.from_np(a.dtype), kind="ExternalInput").ap() for name, a in arrays.items()}
    out = nc.dram_tensor("out", (B, T, D), F32, kind="ExternalOutput").ap()
    program(nc, aps, out)
    r = _run(nc, [{"in_" + name: a for name, a in arrays.items()}], core_ids=[0])
    return r.results[0]["out"]
```

```python
from contextlib import ExitStack

import numpy as np

import concourse.bass as bass
from concourse import mybir

ALU = mybir.AluOpType
ACT = mybir.ActivationFunctionType
AX = mybir.AxisListType.X
F32 = mybir.dt.float32
BF16 = mybir.dt.bfloat16
I32 = mybir.dt.int32

B = 16
T = 128
D = 128
KEYS = 77
KP = 78
H = 16
DH0, DH1 = 8, 64
F = 512
E = 8
CAP = 320
ROWS = E * CAP
EPS = 1e-5
MAGIC = 12582912.0
MASKED = -1e30
WARM = 8


class Step:

    def __init__(self, i, p, lo):
        self.i, self.p, self.lo = i, p, lo

    def next(self, k=1):
        return Step(self.i + k, (self.p + k) % 2, self.lo + k)


def run_steps(eng, step, first, last, head, tail):
    start, stop = first + head, last + 1 - tail
    assert (stop - start) % 2 == 0
    for i in range(first, start):
        step(Step(i, i % 2, i), last)
    with eng.Fori(0, (stop - start) // 2) as r:
        step(Step(r * 2 + start, start % 2, start), last)
        step(Step(r * 2 + (start + 1), (start + 1) % 2, start + 1), last)
    for i in range(stop, last + 1):
        step(Step(i, i % 2, i), last)


def tile_at(t, i, width):
    return t[:, bass.ts(i, width)]


class Store:

    def __init__(self, nc, ctx):
        self.nc, self.ctx, self.sems = nc, ctx, {}

    def sb(self, name, shape, dt=F32):
        return self.ctx.enter_context(self.nc.sbuf_tensor(name, shape, dt))

    def sem(self, name):
        if name not in self.sems:
            self.sems[name] = self.ctx.enter_context(self.nc.semaphore(name))
        return self.sems[name]


def loads_of(S, A):
    def row(name):
        return A[name].rearrange("(a n) -> a n", a=1)

    return [
        ("len", S.len_i[:, :], row("_lenS2").to_broadcast([D, B])), ("len", S.krow[:, :], A["c_krow"]), ("len", S.kpos[:, :], A["c_kpos"]),
        ("bias0", S.bias_row[:, 0, :], row("L0_xattn_q_b")), ("bias0", S.bias_row[:, 1, :], row("L0_xattn_k_b")),
        ("eye", S.eye[:, :], A["c_eye"]),
        ("negsel32", S.negsel32[:, :], A["c_negsel"]),
        ("x", S.x[:, :].rearrange("t (b d) -> t b d", d=D), A["x"].rearrange("b t d -> t b d")),
        ("w0", S.wq0[:, :], A["L0_xattn_q_w"]), ("w0", S.wk0[:, :], A["L0_xattn_k_w"]),
        ("w0", S.wv0[:, :], A["L0_xattn_v_w"]), ("w0", S.wo0[:, :], A["L0_xattn_o_w"]),
        ("rows", S.cols[:, 2:3], A["L0_xattn_v_b"].rearrange("(p a) -> p a", a=1)),
        ("rows", S.row_o[:, 0, :], row("L0_xattn_o_b")),
        ("ternary", S.w1n[:, :, :], A["L0_ffn_w1"].rearrange("(c p) d -> p c d", p=D)), ("ternary", S.w2n[:, :], A["L0_ffn_w2"]),
        ("bias8", S.bias8[:, 0, :], A["L1_xattn_bq"].rearrange("(p j) -> p j", p=D)),
        ("bias8", S.bias8[:, 1, :], A["L1_xattn_bk"].rearrange("(p j) -> p j", p=D)),
        ("later", S.cols[:, 3:4], A["L1_xattn_ln_g"].rearrange("(p a) -> p a", a=1)),
        ("later", S.cols[:, 4:5], A["L1_xattn_ln_b"].rearrange("(p a) -> p a", a=1)),
        ("later", S.bvcol[:, :], A["L1_xattn_bv"].rearrange("(j p) -> p j", p=D)),
        ("later", S.row_o[:, 1, :], row("L1_xattn_bo")),
        ("later", S.b1bc[:, :], row("L0_ffn_b1").to_broadcast([D, F])), ("later", S.b2bc[:, :], row("L0_ffn_b2").to_broadcast([D, D])),
        ("later", S.wq1[:, :], A["L1_xattn_Wq"]), ("later", S.wk1[:, :], A["L1_xattn_Wk"]), ("later", S.wv1[:, :], A["L1_xattn_Wv"]),
        ("later", S.wo1[:, :, :], A["L1_xattn_Wo"].rearrange("(j p) n -> p j n", p=D)),
        ("later", S.cosq[:, :], A["c_cosq"]), ("later", S.sinq[:, :], A["c_sinq"]),
        ("later", S.gate_w[:, :], A["L1_ffn_gate_w"]), ("later", S.gate_b[:, :], row("L1_ffn_gate_b")),
        ("later", S.upto32[:, :], A["c_upto"]), ("later", S.expert_ids[:, :], A["c_expert_ids"]),
        ("later", S.dropped_row[:, :], A["c_dropped"]),
    ]


def load_context(sp, S, A, L, n):
    ctx = A["ctx_1024"][n.i:n.i + 1] if isinstance(n.i, int) else A["ctx_1024"][bass.ds(n.i, 1)]
    sp.dma_start(S.ctx_in[:, n.p, :], ctx.rearrange("b k d -> k (b d)")).then_inc(S.sem(f"ctx_in{L}_{n.p}"), 16)


def setup(nc, S, A):
    loads = loads_of(S, A)
    S.load_total = {}
    for name, _, _ in loads:
        S.load_total[name] = S.load_total.get(name, 0) + 16

    def loaded(eng, *names):
        for n in names:
            eng.wait_ge(S.sem("ld_" + n), S.load_total[n])

    for n in S.load_total:
        S.sem("ld_" + n)
    zero_done, cast, quant, ps, split = (S.sem(n) for n in ("zeros", "cast", "quant", "set_pe", "split"))
    zero_rows, rows3, rows3_1, step_v, step_g = (S.sem(n) for n in ("zero_rows", "rows3", "rows3_1", "set_v", "set_g"))
    bank = S.bank

    with nc.Block() as block:
        @block.sync
        def _(sp):
            for name, dst, src in loads:
                if name == "later":
                    break
                sp.dma_start(dst, src, allow_slow_non_contiguous=True).then_inc(S.sem("ld_" + name), 16)
                if name == "negsel32":
                    for p in range(2):
                        load_context(sp, S, A, 0, Step(p, p, p))
                    sp.wait_ge(split, 5)
                    for part in range(3):
                        sp.dma_start(S.bias3_0[part:part + 1, :, :], S.parts_row[:, part, :, :]).then_inc(rows3, 16)
            sp.wait_ge(split, 10)
            for part in range(3):
                for which in range(2):
                    sp.dma_start(S.bias3[part:part + 1, which, :], S.parts[:, part, which, :]).then_inc(rows3_1, 16)
            sp.wait_ge(zero_done, 1)
            for half in range(2):
                sp.dma_start(S.dispatch[half * ROWS // 2:(half + 1) * ROWS // 2, :].rearrange("(p n) d -> p (n d)", p=D), S.zeros[:, :]
                             ).then_inc(zero_rows, 16)
            sp.wait_ge(rows3, 3 * 16)
            loaded(sp, "x", "w0", "rows")

        @block.gpsimd
        def _(g):
            nc.gpsimd.memset(S.minus_half[:, :], -0.5)
            nc.gpsimd.memset(S.zeros[:, :], 0.0).then_inc(zero_done, 1)
            nc.gpsimd.memset(S.vaug[1][:, :, :, :], 1.0)
            nc.gpsimd.memset(S.kT[0][:, :, :, :], 0.0)
            g.wait_ge(step_v, 1)
            loaded(g, "len")
            nc.gpsimd.tensor_tensor(S.maskrow32[:, :, :], S.len_f[0:1, :].unsqueeze(2).to_broadcast([1, B, KEYS]),
                                    S.krow[:, :].unsqueeze(1).to_broadcast([1, B, KEYS]), ALU.subtract).then_inc(step_g, 1)
            g.wait_ge(step_g, 1)
            nc.gpsimd.tensor_scalar(S.maskrow[:, :], S.maskrow32[:, :, :].rearrange("a b k -> a (b k)"), 0.0, MASKED, ALU.is_le, ALU.mult)

        @block.vector
        def _(v):
            nc.vector.memset(S.vaug[0][:, :, :, :], 1.0)
            for parts in (S.qparts, S.kparts):
                nc.vector.memset(parts[:, :], 0.0)
            nc.vector.memset(S.ones_row[:, :], 1.0)
            nc.vector.memset(S.ones_bf[:, :], 1.0)
            nc.vector.memset(S.ones_mean[:, :], 1.0 / (F * D)).then_inc(cast, 1)
            nc.vector.memset(S.onehot[:, 0:(B - 1) * E], 0.0)
            nc.vector.memset(S.varx[:, :, :], 1.0)
            nc.vector.memset(S.minus_magic[:, :], -MAGIC)
            nc.vector.memset(S.rowmax[:, :, :], 0.0)
            loaded(v, "len")
            nc.vector.tensor_copy(S.len_f[:, :], S.len_i[:, :]).then_inc(step_v, 1)
            n = 0
            for ld, row, parts in (("bias0", S.bias_row, S.parts_row), ("bias8", S.bias8, S.parts)):
                loaded(v, ld)
                for part in range(3):
                    nc.vector.tensor_copy(parts[:, part, :, :], row[:, :, :]).then_inc(split, 1)
                    n += 1
                    v.wait_ge(split, n)
                    if part < 2:
                        nc.vector.tensor_tensor(row[:, :, :], row[:, :, :], parts[:, part, :, :], ALU.subtract).then_inc(split, 1)
                        n += 1
                        v.wait_ge(split, n)
                if ld == "bias0":
                    loaded(v, "eye", "negsel32")
                    nc.vector.tensor_copy(S.eye_bf[:, :], S.eye[:, :])
                    nc.vector.tensor_copy(S.negsel[:, :], S.negsel32[:, :])
                    v.wait_ge(step_v, 1)
                    nc.vector.tensor_scalar(S.maskcol[:, :], S.len_f[:, :], S.kpos[:, 0:1], MASKED, ALU.is_le, ALU.mult)
            v.wait_ge(ps, 1)
            nc.vector.tensor_tensor(S.row_o[:, 0, :], bank[1][0:1, 0:D], S.row_o[:, 0, :], ALU.add)
            loaded(v, "ternary")
            nc.vector.tensor_reduce(S.wabs[:, 0:1], S.w1n[:, :, :].rearrange("p c d -> p (c d)"), AX, ALU.add,
                                    apply_absolute_value=True).then_inc(quant, 1)
            nc.vector.tensor_reduce(S.wabs[:, 1:2], S.w2n[:, :], AX, ALU.add, apply_absolute_value=True).then_inc(quant, 1)
            v.wait_ge(ps, 2)
            nc.vector.tensor_scalar(S.wmean[:, :], bank[0][:, 0:2], EPS, None, ALU.max).then_inc(quant, 1)
            v.wait_ge(quant, 3)
            nc.vector.reciprocal(S.wscale[:, :], S.wmean[:, :])
            nc.vector.tensor_scalar(S.wmean127[:, :], S.wmean[:, :], 1.0 / 127.0, None, ALU.mult)

        @block.tensor
        def _(pe):
            loaded(pe, "rows", "w0")
            nc.tensor.matmul(bank[1][0:1, 0:D], S.cols[:, 2:3], S.wo0[:, :], start=True, stop=True).then_inc(ps, 1)
            pe.wait_ge(cast, 1)
            pe.wait_ge(quant, 2)
            nc.tensor.matmul(bank[0][:, 0:2], S.ones_mean[:, :], S.wabs[:, :], start=True, stop=True).then_inc(ps, 1)


def normalise_steps(nc, S, v, L, n):
    ln, ln_pow, xn_ready = S.sem(f"ln{L}"), S.sem(f"ln_pow{L}"), S.sem(f"xn_ready{L}")
    i, p = n.i, n.p
    parts = 2 if L == 1 else 1
    per = 3 * parts

    def statistics():
        if L == 1:
            v.wait_ge(S.sem(f"ctx_in{L}_{p}"), i * 8 + (16 - 8 * p))
            nc.vector.memset(S.fence[:, :], 0.0)
            nc.vector.bn_stats(S.stats[0:KEYS, p, 1, :], S.ctx_in[:, p, :]).then_inc(ln, 1)
        nc.vector.bn_stats(S.stats[:, p, 0, :], tile_at(S.x, i, D)).then_inc(ln, 1)
        v.wait_ge(ln, i * per + parts)
        nc.vector.memset(S.fence[:, :], 0.0)
        nc.vector.bn_aggr(S.meanvar[:, p, 0, :], S.stats[:, p, 0, :]).then_inc(ln, 1)
        if L == 1:
            nc.vector.bn_aggr(S.meanvar[0:KEYS, p, 1, :], S.stats[0:KEYS, p, 1, :]).then_inc(ln, 1)
        v.wait_ge(ln, i * per + 2 * parts)
        if L == 0:
            nc.vector.tensor_scalar(S.varx[:, p, 0:1], S.meanvar[:, p, 0, 1:2], EPS, None, ALU.add).then_inc(ln, 1)
        else:
            nc.vector.tensor_scalar(S.varx[0:KEYS, p, 1:2], S.meanvar[0:KEYS, p, 1, 1:2], EPS, None, ALU.add).then_inc(ln, 1)
            nc.vector.tensor_scalar(S.varx[:, p, 0:1], S.meanvar[:, p, 0, 1:2], 1.0 + EPS, EPS * EPS,
                                    ALU.mult, ALU.add).then_inc(ln, 1)

    def scale():
        v.wait_ge(ln_pow, i + 1)
        if L == 1:
            nc.vector.tensor_scalar(S.cn[:, p, :], S.ctx_in[:, p, :], S.meanvar[0:KEYS, p, 1, 0:1], S.rstd[0:KEYS, p, 1:2],
                                    ALU.subtract, ALU.mult)
        nc.vector.tensor_scalar(S.xn[:, p, :], tile_at(S.x, i, D), S.meanvar[:, p, 0, 0:1], S.rstd[:, p, 0:1],
                                ALU.subtract, ALU.mult).then_inc(xn_ready, 1)

    return statistics, scale


def keep_clock(nc, S, bank, k):
    for _ in range(k):
        nc.tensor.matmul(bank[:, :], S.eye_bf[:, :], S.negsel[:, 0:512], start=True, stop=True)


def quantise_weights(nc, S, g):
    done = S.sem("ternary")
    w1f, w2f = S.w1n[:, :, :].rearrange("p c d -> p (c d)"), S.w2n[:, :]
    n = 0
    for k, w in enumerate((w1f, w2f)):
        nc.gpsimd.tensor_scalar(w, w, S.wscale[:, k:k + 1], MAGIC, ALU.mult, ALU.add).then_inc(done, 1)
        n += 1
        g.wait_ge(done, n)
        nc.gpsimd.tensor_scalar(w, w, -MAGIC, 1.0, ALU.add, ALU.min).then_inc(done, 1)
        n += 1
        g.wait_ge(done, n)
        nc.gpsimd.tensor_scalar((S.w1t, S.w2t)[k][:, :], w, -1.0, None, ALU.max).then_inc(done, 1)
        n += 1


def attention(nc, S, A, L):
    dh = DH1 if L else DH0
    tiles = H * dh // D
    scale = float(dh) ** -0.5
    bank = S.bank
    ST, SM, PV, M0, M1 = (0, 1), (2, 3), (4, 5), bank[6], bank[7]
    qmax, kmax = (S.qT_bf, S.kT_bf) if L else (S.qT[0], S.kT[0])
    xT, cT, qT, vaug, attn, attnT = S.xT, S.cT, S.qT[L], S.vaug[L], S.attn[L], S.attnT
    kT = S.kT[L]
    last = B - 1

    def sem(n):
        return S.sem(f"{n}{L}")

    xn_ready, a1_done, a1_out = sem("xn_ready"), sem("a1_done"), sem("a1_out")
    m1_done, m1_out, sm_done, mx_out = sem("m1_done"), sem("m1_out"), sem("sm_done"), sem("mx_out")
    mt_done, mt_out, st_done, ex_out = sem("mt_done"), sem("mt_out"), sem("st_done"), sem("ex_out")
    pv_done, pve_out, pv_rec, ta_done, ta_out = sem("pv_done"), sem("pve_out"), sem("pv_rec"), sem("ta_done"), sem("ta_out")
    o_done, o_out, tq_done, tq_out, ln, ln_pow = sem("o_done"), sem("o_out"), sem("tq_done"), sem("tq_out"), sem("ln"), sem("ln_pow")
    ctx_in = [S.sem(f"ctx_in{L}_{p}") for p in range(2)]
    tk_done, tk_out, st_ready = sem("tk_done"), sem("tk_out"), S.sem(("f_st_ready", "d_st_ready")[L])
    if L:
        q_ready, k_ready, k_ready_v, v_done, v_out, mcol_out, bf_out = (sem("q_ready"), sem("k_ready"), sem("k_ready_v"), sem("v_done"), sem("v_out"),
                                                             sem("mcol_out"), sem("bf_out"))
    else:
        split = sem("split")
    M1_USES = 4 if L else 1
    CH = 1 + L
    M0_q = M0 if L else S.bank_bf[6]
    M0_max = S.bank_bf[6]
    KT = M0 if L else S.bank_bf[7]
    XT = bank[SM[1]]
    OUT = M1 if L else bank[PV[1]]
    PVW = dh + 1 if L else 8 * (dh + 1)

    def head(half, c, s):
        return 8 * half + 2 * s + c

    def rows_of(h):
        return slice(64 * (h % 2), 64 * (h % 2) + 64)

    def kq_of(h, k, q):
        if L:
            return k[rows_of(h), h // 2, :], q[rows_of(h), h // 2, :]
        return k[:, h, :], q[:, h // 2, :]

    def max_cols(t, half, c):
        return t[:, 64 * c + 4 * half:64 * c + 4 * half + 4]

    def head_cols(t, half, c):
        return t[:, 8 * half + c:8 * half + 8:2]

    with nc.Block() as block:
        @block.sync
        def _(sp):
            if L == 0:
                for name, dst, src in loads_of(S, A):
                    if name == "later":
                        sp.dma_start(dst, src, allow_slow_non_contiguous=True).then_inc(S.sem("ld_later"), 16)

            def load(n, _):
                sp.wait_ge(xn_ready if L else a1_done, n.i - 1)
                load_context(sp, S, A, L, n)
            run_steps(sp, load, 2, last, 0, 0)

        @block.gpsimd
        def _(g):
            def step(s, _):
                n, n2 = s.next(), s.next(2)

                def rotated(x, c):
                    out, c1, c2 = ((S.qrot, S.qcos, S.qsin), (S.krot, S.kcos, S.ksin))[x]
                    g.wait_ge(m1_out, n.i * 4 + (2 * x + c + 1))
                    nc.gpsimd.tensor_tensor(out[:, c, :], c1[:, c, :], c2[:, c, :], ALU.add).then_inc((q_ready, k_ready)[x], 1)
                rotary = L and 0 <= n.lo <= last
                if rotary:
                    rotated(0, 0)
                if n2.lo <= last:
                    g.wait_ge(ln, n2.i * (3 + 3 * L) + (3 + 3 * L))
                    nc.gpsimd.tensor_tensor(S.rstd[:, n2.p, 0:1 + L], S.varx[:, n2.p, 0:1 + L], S.minus_half[:, 0:1 + L],
                                            ALU.pow).then_inc(ln_pow, 1)
                if rotary:
                    rotated(0, 1)
                    rotated(1, 0)
            run_steps(g, step, -2, last, 3, 3)
            if L == 0:
                quantise_weights(nc, S, g)

        @block.vector
        def _(v):
            def split_qkv(n):
                v.wait_ge(m1_done, n.i + 1)
                both = []
                for x, (ps, parts, rest, rows) in enumerate(((M1[:, 0:D], S.qparts, S.qrest, T), (M1[0:KEYS, D:2 * D], S.kparts, S.krest, KEYS))):
                    slots = parts[:, :].rearrange("t (h s d) -> t h s d", h=H, s=8)
                    both.append((ps.rearrange("t (h d) -> t h d", h=H), slots, rest[:, :].rearrange("t (h d) -> t h d", h=H), rows,
                                 (slice(0, 3), slice(3, 5), slice(6, 7)) if x == 0 else (slice(0, 7, 3), slice(1, 5, 3), slice(2, 3))))

                def wide(ap, rows, k):
                    return ap.unsqueeze(2).to_broadcast([rows, H, k, DH0])
                for ps, slots, rest, rows, (h, m, l) in both:
                    nc.vector.tensor_copy(slots[:, :, h, :], wide(ps, rows, 3)).then_inc(split, 1)
                for x, (ps, slots, rest, rows, (h, m, l)) in enumerate(both):
                    v.wait_ge(split, n.i * 8 + (1 + x))
                    nc.vector.tensor_tensor(rest, ps, slots[:, :, 0, :], ALU.subtract).then_inc(split, 1)
                nc.vector.tensor_copy(vaug[:, n.p, :, 0:dh], M1[0:KEYS, 256:256 + D].rearrange("k (h d) -> k h d", h=H)
                                      ).then_inc(m1_out, 1)
                for x, (ps, slots, rest, rows, (h, m, l)) in enumerate(both):
                    v.wait_ge(split, n.i * 8 + (3 + x))
                    nc.vector.tensor_copy(slots[:, :, m, :], wide(rest, rows, 2)).then_inc(split, 1)
                for x, (ps, slots, rest, rows, (h, m, l)) in enumerate(both):
                    v.wait_ge(split, n.i * 8 + (5 + x))
                    nc.vector.tensor_tensor(slots[:, :, l, :].rearrange("t h one d -> t h (one d)"), rest,
                                            slots[:, :, m.start, :], ALU.subtract).then_inc(split, 1)

            def rotate(n, x, c):
                rows, cosv, sinv = (T, S.qcos, S.qsin) if x == 0 else (KEYS, S.kcos, S.ksin)
                v.wait_ge(m1_done, n.i * 4 + (2 * x + c + 1))
                ps = M1[0:rows, 0:512].rearrange("t (h d) -> t h d", h=8)
                pair = M1[0:rows, 0:512].rearrange("t (h n two) -> t h n two", h=8, two=2)
                qs = sinv[:, c, :].rearrange("t (h n two) -> t h n two", h=8, two=2)
                sn = S.sinq[0:rows, :].rearrange("t (n two) -> t n two", two=2)
                nc.vector.tensor_tensor(cosv[:, c, :].rearrange("t (h d) -> t h d", h=8), ps,
                                        S.cosq[0:rows, :].unsqueeze(1).to_broadcast([rows, 8, DH1]), ALU.mult)
                nc.vector.tensor_tensor(qs[:, :, :, 0], pair[:, :, :, 1],
                                        sn[:, :, 0].unsqueeze(1).to_broadcast([rows, 8, DH1 // 2]), ALU.mult)
                nc.vector.tensor_tensor(qs[:, :, :, 1], pair[:, :, :, 0],
                                        sn[:, :, 1].unsqueeze(1).to_broadcast([rows, 8, DH1 // 2]), ALU.mult).then_inc(m1_out, 1)

            def divide(s, half):
                for c in range(2):
                    v.wait_ge(pv_done, s.i * 4 + (2 * half + c + 1))
                    off, step = (0, dh + 1) if L else (c * (dh + 1), PVW + 2 * (dh + 1))
                    pvb = bank[PV[c]][:, off:off + 4 * step].rearrange("t (s x) -> t s x", s=4)[:, :, 0:dh + 1]
                    nc.vector.reciprocal(S.recip[:, c, :], pvb[:, :, dh]).then_inc(pv_rec, 1)
                    v.wait_ge(pv_rec, s.i * 4 + (2 * half + c + 1))
                    nc.vector.tensor_tensor(head_cols(attn[:, s.p, :].rearrange("t (h d) -> t h d", h=H), half, c), pvb[:, :, 0:dh],
                                            S.recip[:, c, :].unsqueeze(2).to_broadcast([T, 4, dh]), ALU.mult).then_inc(pve_out, 1)

            def row_statistics(s):
                v.wait_ge(o_out, s.i + 1)
                nc.vector.memset(S.fence_x[:, :], 0.0)
                nc.vector.bn_stats(S.stats_all[:, bass.ds(s.i, 1), :].rearrange("t one n -> t (one n)"), tile_at(S.x, s.i, D)).then_inc(st_ready, 1)

            def residual(s):
                v.wait_ge(o_done, s.i + 1)
                nc.vector.tensor_tensor(tile_at(S.x, s.i, D), OUT[:, 0:D], tile_at(S.x, s.i, D), ALU.add).then_inc(o_out, 1)
                if s.lo >= 1:
                    row_statistics(s.next(-1))
                if s.lo == last:
                    v.wait_ge(st_ready, last)
                    row_statistics(s)

            def maximum(n, half):
                for c in range(2):
                    v.wait_ge(sm_done, n.i * 4 + (2 * half + c + 1))
                    nc.vector.tensor_reduce(max_cols(S.rowmax[:, n.p, :], half, c),
                                            bank[(SM, ST)[half][c]][:, 0:4 * KEYS].rearrange("t (s k) -> t s k", s=4), AX, ALU.max
                                            ).then_inc(mx_out, 1)

            def copy_bf(n, x, c):
                v.wait_ge((tq_out, tk_out)[x], n.i * 2 + (c + 1))
                out, src = ((S.qT_bf, qT), (S.kT_bf, kT))[x]
                nc.vector.tensor_copy(out[:, 4 * c:4 * c + 4, :], src[:, n.p, 4 * c:4 * c + 4, :]).then_inc(bf_out, 1)

            def step(s, _):
                n, n2 = s.next(), s.next(2)
                cur, nxt, nxt2 = s.lo >= 0, 0 <= n.lo <= last, n2.lo <= last
                statistics, normalise = normalise_steps(nc, S, v, L, n2)
                if nxt and L:
                    rotate(n, 0, 0)
                if nxt2 and L:
                    statistics()
                if nxt and L:
                    nc.vector.tensor_copy(S.mcol[:, n.p:n.p + 1], S.maskcol[0:KEYS, bass.ds(n.i, 1)]).then_inc(mcol_out, 1)
                    rotate(n, 0, 1)
                if nxt and L == 0:
                    split_qkv(n)
                if nxt2 and L == 0:
                    statistics()
                if s.lo >= 1 and L == 0:
                    residual(s.next(-1))
                if nxt2 and L == 0:
                    normalise()
                if cur:
                    divide(s, 0)
                if nxt and L:
                    rotate(n, 1, 0)
                if nxt2 and L:
                    normalise()
                if cur:
                    divide(s, 1)
                if nxt and L:
                    rotate(n, 1, 1)
                    v.wait_ge(m1_out, n.i * 4 + 4)
                    nc.vector.tensor_tensor(S.krot[:, 1, :], S.kcos[:, 1, :], S.ksin[:, 1, :], ALU.add).then_inc(k_ready_v, 1)
                    copy_bf(n, 0, 0)
                    copy_bf(n, 0, 1)
                    copy_bf(n, 1, 0)
                    copy_bf(n, 1, 1)
                if cur and (L or not nxt):
                    residual(s)
                if nxt:
                    maximum(n, 0)
                    maximum(n, 1)
            run_steps(v, step, -2, last, 4, 2)

        @block.scalar
        def _(act):
            def exponent(s, half):
                for c in range(2):
                    act.wait_ge(st_done, s.i * 4 + (2 * half + c + 1))
                    if L == 0:
                        nc.scalar.activation(S.probs[:, half, c, :], bank[(ST, SM)[half][c]][0:KEYS, :], ACT.Exp, scale=scale).then_inc(ex_out, 1)
                    else:
                        if half == 0 and c == 0:
                            act.wait_ge(mcol_out, s.i + 1)
                        nc.scalar.activation(S.probs[:, half, c, :], bank[(ST, SM)[half][c]][0:KEYS, :], ACT.Exp, scale=scale,
                                             bias=S.mcol[:, s.p:s.p + 1]).then_inc(ex_out, 1)

            def copy_v(n, c):
                act.wait_ge(v_done, n.i * 2 + (c + 1))
                nc.scalar.copy(vaug[:, n.p, 8 * c:8 * c + 8, 0:dh], bank[SM[c]][0:KEYS, :].rearrange("k (h d) -> k h d", h=8)
                               ).then_inc(v_out, 1)

            def copy_q(n, c):
                w = 8 // CH
                act.wait_ge(tq_done, n.i * CH + (c + 1))
                nc.scalar.copy(qT[:, n.p, w * c:w * c + w, :].rearrange("d j t -> d (j t)"), M0_q[:, 0:w * T]).then_inc(tq_out, 1)

            def copy_k(n, c):
                w = 8 // CH
                act.wait_ge(tk_done, n.i * CH + (c + 1))
                tiles_k = KT[:, 0:w * KP].rearrange("d (j k) -> d j k", k=KP)[:, :, 0:KEYS]
                if L:
                    nc.scalar.copy(kT[:, n.p, w * c:w * c + w, :], tiles_k).then_inc(tk_out, 1)
                else:
                    nc.scalar.copy(kT[0:64, n.p, 0:H:2, :], tiles_k[0:64])
                    nc.scalar.copy(kT[64:D, n.p, 1:H:2, :], tiles_k[64:D]).then_inc(tk_out, 1)

            def copy_out(s, c):
                w = min(tiles, 4)
                act.wait_ge(ta_done, s.i * CH + (c + 1))
                nc.scalar.copy(attnT[:, 4 * c:4 * c + w, :].rearrange("d j t -> d (j t)"), bank[PV[c]][:, 0:w * T]).then_inc(ta_out, 1)

            def copy_rows(n):
                act.wait_ge(a1_done, n.i + 1)
                if L == 0:
                    nc.scalar.copy(xT[:, n.p, :], XT[:, 0:D])
                    nc.scalar.copy(cT[:, n.p, :], XT[:, D:D + KEYS]).then_inc(a1_out, 1)
                else:
                    nc.scalar.activation(xT[:, n.p, :], XT[:, 0:D], ACT.Identity, bias=S.cols[:, 4:5], scale=S.cols[:, 3:4])
                    nc.scalar.activation(cT[:, n.p, :], XT[:, D:D + KEYS], ACT.Identity, bias=S.cols[:, 4:5],
                                         scale=S.cols[:, 3:4]).then_inc(a1_out, 1)

            def step(s, _):
                n, n2 = s.next(), s.next(2)
                cur, nxt, nxt2 = s.lo >= 0, 0 <= n.lo <= last, n2.lo <= last
                if nxt and L:
                    copy_v(n, 0)
                if cur:
                    act.wait_ge(mt_done, s.i + 1)
                    nc.scalar.copy(S.maxT[:, s.p, :], M0_max[:, 0:T]).then_inc(mt_out, 1)
                if nxt and L:
                    copy_v(n, 1)
                if cur:
                    exponent(s, 0)
                    exponent(s, 1)
                if nxt:
                    copy_q(n, 0)
                    if L:
                        copy_q(n, 1)
                if cur and L:
                    copy_out(s, 0)
                    copy_out(s, 1)
                if nxt and L:
                    copy_k(n, 0)
                if nxt2:
                    copy_rows(n2)
                if nxt and L == 0:
                    copy_k(n, 0)
                if cur and L == 0:
                    copy_out(s, 0)
                if nxt and L:
                    copy_k(n, 1)
            run_steps(act, step, -2, last, 3, 3)

        @block.tensor
        def _(pe):
            def transpose_rows(n):
                pe.wait_ge(xn_ready, n.i + 1)
                if L == 0:
                    pe.wait_ge(ctx_in[n.p], n.i * 8 + (16 - 8 * n.p))
                nc.tensor.transpose(XT[:, 0:D], S.xn[:, n.p, :], S.eye[:, :])
                c = S.cn if L else S.ctx_in
                nc.tensor.transpose(XT[:, D:D + KEYS], c[:, n.p, :], S.eye[0:KEYS, 0:KEYS]).then_inc(a1_done, 1)

            def m1_free(n):
                if L == 0:
                    if n.lo >= 1:
                        pe.wait_ge(tk_out, n.i)
                elif n.lo >= 2:
                    pe.wait_ge(o_out, n.i - 1)
                elif n.lo == 1:
                    pe.wait_ge(m1_out, M1_USES)

            def project_qkv(n):
                pe.wait_ge(a1_out, n.i + 1)
                m1_free(n)
                nc.tensor.matmul(M1[:, 0:D], S.ones_bf[0:3, :], S.bias3_0[:, 0, :], start=True, stop=False)
                nc.tensor.matmul(M1[:, 0:D], xT[:, n.p, :], S.wq0[:, :], start=False, stop=True)
                nc.tensor.matmul(M1[0:KEYS, D:2 * D], S.ones_bf[0:3, 0:KEYS], S.bias3_0[:, 1, :], start=True, stop=False)
                nc.tensor.matmul(M1[0:KEYS, D:2 * D], cT[:, n.p, :], S.wk0[:, :], start=False, stop=True)
                nc.tensor.matmul(M1[0:KEYS, 256:256 + D], cT[:, n.p, :], S.wv0[:, :], start=True, stop=True).then_inc(m1_done, 1)

            def project(n, x, c):
                if x == 0 and c == 0:
                    pe.wait_ge(a1_out, n.i + 1)
                    m1_free(n)
                else:
                    pe.wait_ge(m1_out, n.i * 4 + (2 * x + c))
                rows, src, w = ((T, xT, S.wq1), (KEYS, cT, S.wk1))[x]
                nc.tensor.matmul(M1[0:rows, :], S.ones_bf[0:3, 0:rows], S.bias3[:, x, 512 * c:512 * c + 512], start=True, stop=False)
                nc.tensor.matmul(M1[0:rows, :], src[:, n.p, :], w[:, 512 * c:512 * c + 512], start=False, stop=True).then_inc(m1_done, 1)

            def project_v(n, c):
                if n.lo >= 1 and c == 0:
                    pe.wait_ge(mx_out, n.i * 4 - 2)
                nc.tensor.matmul(bank[SM[c]][0:KEYS, :], cT[:, n.p, :], S.wv1[:, 512 * c:512 * c + 512], start=True, stop=True).then_inc(v_done, 1)

            def transpose_q(n, c):
                if L:
                    pe.wait_ge(q_ready, n.i * 2 + (c + 1))
                else:
                    pe.wait_ge(split, n.i * 8 + 7)
                if c:
                    pe.wait_ge(tq_out, n.i * 2 + 1)
                for j in range(8 // CH):
                    src = S.qrot[:, c, j * D:(j + 1) * D] if L else S.qparts[:, j * D:(j + 1) * D]
                    mm = nc.tensor.transpose(M0_q[:, j * T:(j + 1) * T], src, S.eye[:, :] if L else S.eye_bf[:, :])
                mm.then_inc(tq_done, 1)

            def transpose_k(n, c):
                if L:
                    pe.wait_ge((k_ready, k_ready_v)[c], n.i + 1)
                else:
                    pe.wait_ge(split, n.i * 8 + 8)
                    pe.wait_ge(m1_out, n.i + 1)
                if c:
                    pe.wait_ge(tk_out, n.i * 2 + 1)
                elif L:
                    pe.wait_ge(tq_out, n.i * CH + CH)
                for j in range(8 // CH):
                    src = S.krot[:, c, j * D:(j + 1) * D] if L else S.kparts[:, j * D:(j + 1) * D]
                    mm = nc.tensor.transpose(KT[:, KP * j:KP * j + KEYS], src,
                                             S.eye[0:KEYS, 0:KEYS] if L else S.eye_bf[0:KEYS, 0:KEYS])
                mm.then_inc(tk_done, 1)

            def scores_for_max(n, half, cur, nxt2):
                banks = (SM, ST)[half]
                if half == 0:
                    if L:
                        pe.wait_ge(bf_out, n.i * 4 + 4)
                        if not cur:
                            pe.wait_ge(v_out, n.i * 2 + 2)
                    else:
                        pe.wait_ge(tk_out, n.i + 1)
                    if nxt2:
                        pe.wait_ge(a1_out, n.i + 2)
                for s4 in range(4):
                    for c in range(2):
                        h = head(half, c, s4)
                        k, q = kq_of(h, kmax[:, :, :] if L else kmax[:, n.p, :, :], qmax[:, :, :] if L else qmax[:, n.p, :, :])
                        mm = nc.tensor.matmul(bank[banks[c]][:, s4 * KEYS:(s4 + 1) * KEYS], q, k, start=(s4 == 0), stop=(L == 0),
                                              skip_group_check=True)
                        if L == 0 and s4 == 3:
                            mm.then_inc(sm_done, 1)
                if L:
                    for c in range(2):
                        nc.tensor.matmul(bank[banks[c]][:, 0:4 * KEYS], S.ones_bf[0:1, :],
                                         tile_at(S.maskrow, n.i, KEYS).unsqueeze(1).to_broadcast([1, 4, KEYS]),
                                         start=False, stop=True, skip_group_check=True).then_inc(sm_done, 1)

            def transpose_max(n):
                if L:
                    pe.wait_ge(tk_out, n.i * CH + CH)
                else:
                    pe.wait_ge(tq_out, n.i + 1)
                    keep_clock(nc, S, M0, 2)
                pe.wait_ge(mx_out, n.i * 4 + 4)
                nc.tensor.transpose(M0_max[:, 0:T], S.rowmax[:, n.p, :], S.eye_bf[:, :]).then_inc(mt_done, 1)

            def scores(s, half, nxt):
                if half == 0:
                    pe.wait_ge(mt_out, s.i + 1)
                elif L and nxt:
                    pe.wait_ge(v_out, s.i * 2 + 4)
                for s4 in range(4):
                    for c in range(2):
                        h = head(half, c, s4)
                        out = bank[(ST, SM)[half][c]][0:KEYS, s4 * T:(s4 + 1) * T]
                        rows = rows_of(h) if L else slice(0, D)
                        k, q = kq_of(h, kT[:, s.p, :, :], qT[:, s.p, :, :])
                        nc.tensor.matmul(out, S.negsel[rows, h * KEYS:(h + 1) * KEYS], S.maxT[rows, s.p, :], start=True, stop=False)
                        mm = nc.tensor.matmul(out, k, q, start=False, stop=True)
                        if s4 == 3:
                            mm.then_inc(st_done, 1)

            def times_v(s, half):
                for c in range(2):
                    pe.wait_ge(ex_out, s.i * 4 + (2 * half + c + 1))
                    if half:
                        pe.wait_ge(pve_out, s.i * 4 + (c + 1))
                    elif L == 0 and c and s.lo >= 1:
                        pe.wait_ge(o_out, s.i)
                    if L and half == 0 and c == 0:
                        pe.wait_ge(v_out, s.i * 2 + 2)
                    for s4 in range(4):
                        out = bank[PV[c]][:, s4 * PVW:(s4 + 1) * PVW]
                        v = vaug[:, s.p, head(half, c, s4), :] if L else vaug[:, s.p, 8 * half:8 * half + 8, :].rearrange("k h d -> k (h d)")
                        mm = nc.tensor.matmul(out, S.probs[:, half, c, s4 * T:(s4 + 1) * T], v, start=True, stop=True)
                    mm.then_inc(pv_done, 1)

            def transpose_out(s, c):
                pe.wait_ge(pve_out, s.i * 4 + 4)
                for j in range(min(tiles, 4)):
                    mm = nc.tensor.transpose(bank[PV[c]][:, j * T:(j + 1) * T], attn[:, s.p, (4 * c + j) * D:(4 * c + j + 1) * D], S.eye[:, :])
                mm.then_inc(ta_done, 1)

            def project_out(s, part, nxt):
                pe.wait_ge(ta_out, s.i * CH + (part + 1))
                if part == 0:
                    if L == 0:
                        pass
                    elif nxt:
                        pe.wait_ge(m1_out, s.i * M1_USES + 2 * M1_USES)
                    elif s.lo >= 1:
                        pe.wait_ge(o_out, s.i)
                    nc.tensor.matmul(OUT[:, 0:D], S.ones_row[:, :], S.row_o[:, L, :], start=True, stop=False)
                for j in range(4 * part, min(4 * part + 4, tiles)):
                    w = S.wo1[:, j, :] if L else S.wo0[:, :]
                    mm = nc.tensor.matmul(OUT[:, 0:D], attnT[:, j, :], w, start=False, stop=(j == tiles - 1))
                if part == CH - 1:
                    mm.then_inc(o_done, 1)

            def step0(s, _):
                n, n2 = s.next(), s.next(2)
                cur, nxt, nxt2 = s.lo >= 0, 0 <= n.lo <= last, n2.lo <= last
                if nxt:
                    project_qkv(n)
                if cur:
                    transpose_max(s)
                    if s.lo >= 1:
                        project_out(s.next(-1), 0, nxt)
                    scores(s, 0, nxt)
                    scores(s, 1, nxt)
                if nxt:
                    transpose_q(n, 0)
                    transpose_k(n, 0)
                if cur:
                    times_v(s, 0)
                    pe.wait_ge(ex_out, s.i * 4 + 4)
                if nxt2:
                    transpose_rows(n2)
                if cur:
                    times_v(s, 1)
                if nxt:
                    scores_for_max(n, 0, cur, nxt2)
                    scores_for_max(n, 1, cur, nxt2)
                if cur:
                    transpose_out(s, 0)
                    if not nxt:
                        project_out(s, 0, nxt)

            def step1(s, _):
                n, n2 = s.next(), s.next(2)
                cur, nxt, nxt2 = s.lo >= 0, 0 <= n.lo <= last, n2.lo <= last
                if nxt:
                    project(n, 0, 0)
                    project_v(n, 0)
                if cur:
                    transpose_max(s)
                if nxt:
                    project_v(n, 1)
                if cur:
                    scores(s, 0, nxt)
                if nxt:
                    project(n, 0, 1)
                if cur:
                    if not nxt:
                        scores(s, 1, nxt)
                    times_v(s, 0)
                    if nxt:
                        scores(s, 1, nxt)
                if nxt:
                    project(n, 1, 0)
                    transpose_q(n, 0)
                if cur:
                    times_v(s, 1)
                if nxt:
                    project(n, 1, 1)
                    transpose_q(n, 1)
                if cur:
                    transpose_out(s, 0)
                    transpose_out(s, 1)
                if nxt2:
                    transpose_rows(n2)
                if nxt:
                    transpose_k(n, 0)
                if cur:
                    project_out(s, 0, nxt)
                if nxt:
                    transpose_k(n, 1)
                if cur:
                    project_out(s, 1, nxt)
                if nxt:
                    scores_for_max(n, 0, cur, nxt2)
                    scores_for_max(n, 1, cur, nxt2)
            if L:
                keep_clock(nc, S, M0, WARM)
            run_steps(pe, step1 if L else step0, -2, last, 3, 3)


def pool_fence(nc, S, g, n, sem, value):
    done = S.sem("pool_fence")
    if n.lo >= 1:
        g.wait_ge(done, n.i)
    g.wait_ge(sem, value)
    nc.gpsimd.tensor_tensor(S.fence_g[:, 1:2], S.minus_half[:, 0:1], S.minus_half[:, 0:1], ALU.add).then_inc(done, 1)


def ffn0(nc, S, A):
    PAIRS = B // 2
    last = PAIRS
    bank = S.bank
    ZT, H1, GT, OUT = bank[0], bank[1:5], bank[5:7], bank[7]
    z_all = S.attn[1][:, :, :].rearrange("t p (b d) -> t (p b) d", d=D)
    x_all = S.x[:, :].rearrange("t (b d) -> t b d", d=D)
    gel = (S.qcos, S.qsin)

    def sem(n):
        return S.sem(f"f_{n}")

    st_ready, ln, ln_pow, centred, z_ready, zsc, zq_ready = (sem("st_ready"), sem("ln"), sem("ln_pow"), sem("centred"),
                                                              sem("z_ready"), sem("zsc"), sem("zq_ready"))
    zt_done, zt_out, h_done, h_out, g_ready, sq_ready = sem("zt_done"), sem("zt_out"), sem("h_done"), sem("h_out"), sem("g_ready"), sem("sq_ready")
    rms_in, rms_pow, gq_ready, gt_done, gt_out, y_done, y_out = (sem("rms_in"), sem("rms_pow"), sem("gq_ready"), sem("gt_done"),
                                                                  sem("gt_out"), sem("y_done"), sem("y_out"))
    xb_done, gsc, folded = sem("xb_done"), sem("gsc"), sem("folded")

    with nc.Block() as block:
        @block.sync
        def _(sp):
            sp.wait_ge(S.sem("rows3_1"), 6 * 16)
            sp.wait_ge(S.sem("zero_rows"), 2 * 16)
            sp.wait_ge(S.sem("ld_later"), S.load_total["later"])
            for p in range(2):
                load_context(sp, S, A, 1, Step(p, p, p))

        @block.gpsimd
        def _(g):
            g.wait_ge(ln, 1)
            nc.gpsimd.tensor_tensor(S.rstd_all[:, :], S.var_all[:, :], S.minus_half[:, 0:1].to_broadcast([T, B]), ALU.pow).then_inc(ln_pow, 1)
            g.wait_ge(S.sem("ld_later"), S.load_total["later"])
            g.wait_ge(centred, 1)
            nc.gpsimd.tensor_tensor(x_all, x_all, S.b2bc[:, :].unsqueeze(1).to_broadcast([T, B, D]), ALU.add).then_inc(xb_done, 1)

            def step(s, _):
                g.wait_ge(rms_in, s.i + 1)
                nc.gpsimd.tensor_tensor(S.rms[:, :], S.meansq[:, :], S.minus_half[:, 0:1].to_broadcast([T, 2]), ALU.pow).then_inc(rms_pow, 1)
            run_steps(g, step, 0, PAIRS - 1, 0, 0)

        @block.vector
        def _(v):
            v.wait_ge(st_ready, B)
            for b in range(B):
                nc.vector.bn_aggr(S.mv_all[:, b, :], S.stats_all[:, b, :]).then_inc(st_ready, 1)
            v.wait_ge(st_ready, 2 * B)
            nc.vector.tensor_scalar(S.var_all[:, :], S.mv_all[:, :, 1], 1.0 + EPS, EPS * EPS, ALU.mult, ALU.add).then_inc(ln, 1)
            nc.vector.tensor_tensor(z_all, x_all, S.mv_all[:, :, 0:1].to_broadcast([T, B, D]), ALU.subtract).then_inc(centred, 1)
            v.wait_ge(centred, 1)
            nc.vector.tensor_reduce(S.zmax[:, :], z_all, AX, ALU.max, apply_absolute_value=True).then_inc(zsc, 1)
            v.wait_ge(ln_pow, 1)
            v.wait_ge(zsc, 1)
            nc.vector.tensor_tensor(S.zmax[:, :], S.zmax[:, :], S.rstd_all[:, :], ALU.mult).then_inc(zsc, 1)
            nc.vector.tensor_tensor(z_all, z_all, S.rstd_all[:, :].unsqueeze(2).to_broadcast([T, B, D]), ALU.mult).then_inc(z_ready, 1)
            v.wait_ge(zsc, 2)
            nc.vector.tensor_scalar(S.zmax[:, :], S.zmax[:, :], EPS, None, ALU.max).then_inc(zsc, 1)
            v.wait_ge(zsc, 3)
            nc.vector.reciprocal(S.zinv[:, :], S.zmax[:, :]).then_inc(zsc, 1)
            nc.vector.tensor_scalar(S.zout[:, :], S.zmax[:, :], S.wmean127[:, 0:1], None, ALU.mult)
            v.wait_ge(zsc, 4)
            nc.vector.tensor_scalar(S.zinv[:, :], S.zinv[:, :], 127.0, None, ALU.mult).then_inc(zsc, 1)
            v.wait_ge(zsc, 5)
            v.wait_ge(z_ready, 1)
            v.wait_ge(folded, 1)
            v.wait_ge(S.sem("ld_later"), S.load_total["later"])
            nc.vector.tensor_tensor(S.row_o[:, 1, :], OUT[0:1, 0:D], S.row_o[:, 1, :], ALU.add).then_inc(folded, 1)
            nc.vector.tensor_copy(S.upto[:, :], S.upto32[:, :])

            def quantise_z(n, j):
                b = n.i * 2 + j
                nc.vector.tensor_scalar(S.zq[:, n.p, j, :], tile_at(S.attn[1][:, :, :].rearrange("t p n -> t (p n)"), b, D),
                                        S.zinv[:, bass.ds(b, 1)], MAGIC, ALU.mult, ALU.add).then_inc(zq_ready, 1)

            def hidden(n, j):
                b = n.i * 2 + j
                v.wait_ge(h_done, b + 1)
                nc.vector.scalar_tensor_tensor(S.hid[:, j, :], H1[2 * n.p + j][:, :], S.zout[:, bass.ds(b, 1)], S.b1bc[:, :],
                                               ALU.mult, ALU.add).then_inc(h_out, 1)

            def residual(b, j):
                v.wait_ge(y_done, b.i * 2 + 2)
                xb = tile_at(S.x, b.i * 2 + j, D)
                nc.vector.scalar_tensor_tensor(xb, OUT[:, j * D:(j + 1) * D], S.gout[:, b.p, j:j + 1], xb,
                                               ALU.mult, ALU.add).then_inc(y_out, 1)

            def step(s, _):
                n, n2, b = s.next(), s.next(2), s.next(-1)
                cur, nxt, nxt2, prev = 0 <= s.lo < PAIRS, 0 <= n.lo < PAIRS, n2.lo < PAIRS, b.lo >= 0
                if cur:
                    v.wait_ge(sq_ready, s.i * 2 + 2)
                    nc.vector.tensor_scalar(S.meansq[:, :], S.sumsq[:, :], 1.0 / F, EPS, ALU.mult, ALU.add).then_inc(rms_in, 1)
                    nc.vector.tensor_reduce(S.gmax[:, :], gel[s.p][:, :, :], AX, ALU.max, apply_absolute_value=True).then_inc(gsc, 1)
                if nxt2:
                    quantise_z(n2, 0)
                    quantise_z(n2, 1)
                if cur:
                    v.wait_ge(gsc, s.i * 5 + 1)
                    v.wait_ge(rms_pow, s.i + 1)
                    nc.vector.tensor_tensor(S.gmax[:, :], S.gmax[:, :], S.rms[:, :], ALU.mult).then_inc(gsc, 1)
                if nxt:
                    hidden(n, 0)
                if cur:
                    v.wait_ge(gsc, s.i * 5 + 2)
                    nc.vector.tensor_scalar(S.gmax[:, :], S.gmax[:, :], EPS, None, ALU.max).then_inc(gsc, 1)
                if nxt:
                    hidden(n, 1)
                if cur:
                    v.wait_ge(gsc, s.i * 5 + 3)
                    nc.vector.reciprocal(S.ginv[:, :], S.gmax[:, :]).then_inc(gsc, 1)
                    nc.vector.tensor_scalar(S.gout[:, s.p, :], S.gmax[:, :], S.wmean127[:, 1:2], None, ALU.mult)
                if prev:
                    if b.lo == 0:
                        v.wait_ge(xb_done, 1)
                    residual(b, 0)
                if cur:
                    v.wait_ge(gsc, s.i * 5 + 4)
                    nc.vector.scalar_tensor_tensor(S.ginv[:, :], S.ginv[:, :], 127.0, S.rms[:, :], ALU.mult, ALU.mult).then_inc(gsc, 1)
                if prev:
                    residual(b, 1)
                if cur:
                    v.wait_ge(gsc, s.i * 5 + 5)
                    if s.lo >= 1:
                        v.wait_ge(gt_done, s.i * 2)
                    for j in range(2):
                        nc.vector.tensor_scalar(S.gq[:, j, :], gel[s.p][:, j, :], S.ginv[:, j:j + 1], MAGIC, ALU.mult, ALU.add).then_inc(gq_ready, 1)
            run_steps(v, step, -2, last, 4, 3)

        @block.scalar
        def _(act):
            act.wait_ge(folded, 1)
            nc.scalar.copy(S.w1q[:, :], S.bank_bf[5][:, 0:F])
            nc.scalar.copy(S.w2q[:, :], S.bank_bf[6][:, 0:F])
            nc.scalar.copy(S.gate_t[:, :], bank[4][:, 0:E]).then_inc(folded, 1)

            def step(s, _):
                n, n2 = s.next(), s.next(2)
                if n2.lo < PAIRS:
                    act.wait_ge(zt_done, n2.i + 1)
                    nc.scalar.activation(S.zT[:, n2.p, :], ZT[:, 0:2 * T], ACT.Identity, bias=S.minus_magic[:, :]).then_inc(zt_out, 1)
                if 0 <= n.lo < PAIRS:
                    for j in range(2):
                        act.wait_ge(h_out, n.i * 2 + (j + 1))
                        nc.scalar.activation(gel[n.p][:, j, :], S.hid[:, j, :], ACT.Gelu).then_inc(g_ready, 1)
                        act.wait_ge(g_ready, n.i * 2 + (j + 1))
                        if j == 0 and n.lo >= 1:
                            act.wait_ge(rms_in, n.i)
                        nc.scalar.activation(S.gsq[:, :], gel[n.p][:, j, :], ACT.Square, accum_out=S.sumsq[:, j:j + 1]).then_inc(sq_ready, 1)
                if 0 <= s.lo < PAIRS:
                    for j in range(2):
                        act.wait_ge(gt_done, s.i * 2 + (j + 1))
                        nc.scalar.activation(S.gT[:, j, :], GT[j][:, :], ACT.Identity, bias=S.minus_magic[:, :]).then_inc(gt_out, 1)
            run_steps(act, step, -2, last, 4, 3)

        @block.tensor
        def _(pe):
            for wb, b in ((S.w1t, 5), (S.w2t, 6)):
                for c in range(F // D):
                    nc.tensor.transpose(S.bank_bf[b][:, c * D:(c + 1) * D], wb[:, c * D:(c + 1) * D], S.eye_bf[:, :])
            pe.wait_ge(S.sem("ld_later"), S.load_total["later"])
            for j in range(H * DH1 // D):
                nc.tensor.matmul(OUT[0:1, 0:D], S.bvcol[:, j:j + 1], S.wo1[:, j, :], start=(j == 0), stop=(j == H * DH1 // D - 1))
            nc.tensor.transpose(bank[4][:, 0:E], S.gate_w[:, :], S.eye[0:E, 0:E]).then_inc(folded, 1)
            pe.wait_ge(folded, 3)

            def step(s, _):
                n2 = s.next(2)
                if n2.lo < PAIRS:
                    pe.wait_ge(zq_ready, n2.i * 2 + 2)
                    for j in range(2):
                        mm = nc.tensor.transpose(ZT[:, j * T:(j + 1) * T], S.zq[:, n2.p, j, :], S.eye[:, :])
                    mm.then_inc(zt_done, 1)
                    pe.wait_ge(zt_out, n2.i + 1)
                    if n2.lo >= 2:
                        pe.wait_ge(h_out, n2.i * 2 - 2)
                    for j in range(2):
                        nc.tensor.matmul(H1[2 * n2.p + j][:, :], S.zT[:, n2.p, j * T:(j + 1) * T], S.w1q[:, :], start=True, stop=True).then_inc(h_done, 1)
                if 0 <= s.lo < PAIRS:
                    for j in range(2):
                        pe.wait_ge(gq_ready, s.i * 2 + (j + 1))
                        for c in range(F // D):
                            mm = nc.tensor.transpose(GT[j][:, c * T:(c + 1) * T], S.gq[:, j, c * D:(c + 1) * D], S.eye[:, :])
                        mm.then_inc(gt_done, 1)
                    if s.lo >= 1:
                        pe.wait_ge(y_out, s.i * 2)
                    for j in range(2):
                        pe.wait_ge(gt_out, s.i * 2 + (j + 1))
                        for c in range(F // D):
                            mm = nc.tensor.matmul(OUT[:, j * D:(j + 1) * D], S.gT[:, j, c * T:(c + 1) * T], S.w2q[:, c * D:(c + 1) * D],
                                                  start=(c == 0), stop=(c == F // D - 1))
                        mm.then_inc(y_done, 1)
            run_steps(pe, step, -2, last, 4, 3)


def dispatch(nc, S, A):
    bank = S.bank
    XT, LG, CUM = bank[0:2], bank[2:4], bank[4:6]
    HB = B // 2
    GROUPS, PER = 4, B // 4
    z_all = S.attn[1][:, :, :].rearrange("t p (b d) -> t (p b) d", d=D)
    x_all = S.x[:, :].rearrange("t (b d) -> t b d", d=D)
    xT = S.gq

    def sem(n):
        return S.sem(f"d_{n}")

    st_ready, ln, ln_pow, centred, z_ready = sem("st_ready"), sem("ln"), sem("ln_pow"), sem("centred"), sem("z_ready")
    xt_done, xt_out, lg_done, ch, shifted, ex_done, oh_ready, cum_done, place = (
        sem("xt_done"), sem("xt_out"), sem("lg_done"), sem("choice"), sem("shifted"), sem("ex_done"), sem("oh_ready"), sem("cum_done"),
        sem("place"))
    rows_ready, scattered = sem("rows_ready"), sem("scattered")

    with nc.Block() as block:
        @block.sync
        def _(sp):
            for e in range(2):
                load_expert(sp, S, A, Step(e, e, e))

        @block.gpsimd
        def _(g):
            g.wait_ge(ln, 1)
            nc.gpsimd.tensor_tensor(S.rstd_all[:, :], S.var_all[:, :], S.minus_half[:, 0:1].to_broadcast([T, B]), ALU.pow).then_inc(ln_pow, 1)
            for b in range(B):
                if b % HB == 0:
                    g.wait_ge(rows_ready, b // HB + 1)
                    nc.gpsimd.tensor_tensor(S.fence_g[:, b // HB:b // HB + 1], S.minus_half[:, 0:1], S.minus_half[:, 0:1], ALU.add)
                nc.gpsimd.indirect_dma_start(out=S.dispatch[:, :], out_offset=bass.IndirectOffsetOnAxis(ap=S.row_to[:, b:b + 1], axis=0),
                                             in_=z_all[:, b, :], in_offset=None).then_inc(scattered, 16)
            g.wait_ge(scattered, 16 * B)

        @block.vector
        def _(v):
            ids = S.expert_ids[:, :].unsqueeze(1).to_broadcast([T, HB, E])

            def half_of(h):
                bs = slice(h * HB, (h + 1) * HB)
                return bs, S.onehot[:, (B - 1 + h * HB) * E:(B - 1 + (h + 1) * HB) * E].rearrange("t (b e) -> t b e", e=E)

            def choose(h):
                bs, onehot = half_of(h)
                n = 7 * h
                v.wait_ge(lg_done, h + 1)
                nc.vector.tensor_copy(S.logits[:, bs, :], LG[h][:, 0:HB * E].rearrange("t (b e) -> t b e", e=E)).then_inc(ch, 1)
                v.wait_ge(ch, n + 1)
                nc.vector.tensor_reduce(S.top[:, bs], S.logits[:, bs, :], AX, ALU.max).then_inc(ch, 1)
                v.wait_ge(ch, n + 2)
                top = S.top[:, bs].unsqueeze(2).to_broadcast([T, HB, E])
                nc.vector.tensor_tensor(S.picked[:, bs, :], S.logits[:, bs, :], top, ALU.is_equal).then_inc(ch, 1)
                nc.vector.tensor_tensor(S.exps[:, bs, :], S.logits[:, bs, :], top, ALU.subtract).then_inc(shifted, 1)
                v.wait_ge(ch, n + 3)
                nc.vector.tensor_tensor(S.picked[:, bs, :], S.picked[:, bs, :], ids, ALU.mult).then_inc(ch, 1)
                v.wait_ge(ch, n + 4)
                nc.vector.tensor_reduce(S.expert[:, bs], S.picked[:, bs, :], AX, ALU.min).then_inc(ch, 1)
                v.wait_ge(ch, n + 5)
                nc.vector.tensor_tensor(onehot, ids, S.expert[:, bs].unsqueeze(2).to_broadcast([T, HB, E]), ALU.is_equal).then_inc(oh_ready, 1)
                nc.vector.tensor_scalar(S.row_f[:, bs], S.expert[:, bs], float(CAP), float(ROWS), ALU.mult, ALU.add)
                v.wait_ge(ex_done, h + 1)
                nc.vector.tensor_reduce(S.sumexp[:, bs], S.exps[:, bs, :], AX, ALU.add).then_inc(ch, 1)
                v.wait_ge(ch, n + 6)
                nc.vector.reciprocal(S.weight[:, bs], S.sumexp[:, bs]).then_inc(ch, 1)

            def place_rows(h):
                bs, onehot = half_of(h)
                n = 7 * h
                v.wait_ge(cum_done, h + 1)
                v.wait_ge(oh_ready, h + 1)
                nc.vector.tensor_tensor(S.picked[:, bs, :], CUM[h][:, 0:HB * E].rearrange("t (b e) -> t b e", e=E), onehot, ALU.mult).then_inc(place, 1)
                v.wait_ge(place, n + 1)
                nc.vector.tensor_reduce(S.pos[:, bs], S.picked[:, bs, :], AX, ALU.add).then_inc(place, 1)
                v.wait_ge(place, n + 2)
                nc.vector.tensor_scalar(S.keep[:, bs], S.pos[:, bs], float(CAP), None, ALU.is_le).then_inc(place, 1)
                v.wait_ge(place, n + 3)
                nc.vector.scalar_tensor_tensor(S.pos[:, bs], S.pos[:, bs], -1.0, S.keep[:, bs], ALU.add, ALU.mult).then_inc(place, 1)
                v.wait_ge(ch, n + 7)
                nc.vector.tensor_tensor(S.weight[:, bs], S.weight[:, bs], S.keep[:, bs], ALU.mult)
                v.wait_ge(place, n + 4)
                nc.vector.tensor_tensor(S.row_f[:, bs], S.row_f[:, bs], S.pos[:, bs], ALU.add).then_inc(place, 1)
                v.wait_ge(place, n + 5)
                nc.vector.tensor_tensor(S.pos[:, bs], S.row_f[:, bs], S.dropped_row[:, bs], ALU.subtract).then_inc(place, 1)
                nc.vector.tensor_copy(S.row_from[:, bs], S.row_f[:, bs])
                v.wait_ge(place, n + 6)
                nc.vector.tensor_tensor(S.pos[:, bs], S.pos[:, bs], S.keep[:, bs], ALU.mult).then_inc(place, 1)
                v.wait_ge(place, n + 7)
                nc.vector.tensor_tensor(S.row_to[:, bs], S.pos[:, bs], S.dropped_row[:, bs], ALU.add).then_inc(rows_ready, 1)

            v.wait_ge(st_ready, B)
            for b in range(B):
                nc.vector.bn_aggr(S.mv_all[:, b, :], S.stats_all[:, b, :]).then_inc(st_ready, 1)
            v.wait_ge(st_ready, 2 * B)
            nc.vector.tensor_scalar(S.var_all[:, :], S.mv_all[:, :, 1], EPS, None, ALU.add).then_inc(ln, 1)
            for q in range(GROUPS):
                bs = slice(q * PER, (q + 1) * PER)
                nc.vector.tensor_tensor(z_all[:, bs, :], x_all[:, bs, :], S.mv_all[:, bs, 0:1].to_broadcast([T, PER, D]), ALU.subtract
                                        ).then_inc(centred, 1)
            v.wait_ge(ln_pow, 1)
            for q in range(GROUPS):
                bs = slice(q * PER, (q + 1) * PER)
                v.wait_ge(centred, q + 1)
                nc.vector.tensor_tensor(z_all[:, bs, :], z_all[:, bs, :], S.rstd_all[:, bs].unsqueeze(2).to_broadcast([T, PER, D]), ALU.mult
                                        ).then_inc(z_ready, 1)

            for h in range(2):
                choose(h)
                place_rows(h)

        @block.scalar
        def _(act):
            for q in range(GROUPS):
                act.wait_ge(xt_done, q + 1)
                nc.scalar.copy(xT[:, q % 2, :], XT[q % 2][:, :]).then_inc(xt_out, 1)
                if q % 2 == 1:
                    h = q // 2
                    act.wait_ge(shifted, h + 1)
                    nc.scalar.activation(S.exps[:, h * HB:(h + 1) * HB, :], S.exps[:, h * HB:(h + 1) * HB, :], ACT.Exp).then_inc(ex_done, 1)

        @block.tensor
        def _(pe):
            def transpose_rows(q):
                pe.wait_ge(z_ready, q + 1)
                if q >= 2:
                    pe.wait_ge(xt_out, q - 1)
                for j in range(PER):
                    mm = nc.tensor.transpose(XT[q % 2][:, j * D:(j + 1) * D], z_all[:, q * PER + j, :], S.eye[:, :])
                mm.then_inc(xt_done, 1)
            def places(h):
                pe.wait_ge(oh_ready, h + 1)
                windows = (h + 1) * HB
                for k in range(windows):
                    start = (B - 1 + h * HB - k) * E
                    mm = nc.tensor.matmul(CUM[h][:, 0:HB * E], (S.ones_bf if k else S.upto)[:, :], S.onehot[:, start:start + HB * E],
                                          start=(k == 0), stop=(k == windows - 1))
                mm.then_inc(cum_done, 1)

            for h in range(2):
                nc.tensor.matmul(LG[h][:, 0:HB * E], S.ones_row[:, :], S.gate_b[:, :].unsqueeze(1).to_broadcast([1, HB, E]), start=True,
                                 stop=False, skip_group_check=True)
            transpose_rows(0)
            for q in range(GROUPS):
                if q + 1 < GROUPS:
                    transpose_rows(q + 1)
                pe.wait_ge(xt_out, q + 1)
                for j in range(PER):
                    b = q * PER + j
                    mm = nc.tensor.matmul(LG[b // HB][:, (b % HB) * E:(b % HB + 1) * E], xT[:, q % 2, j * D:(j + 1) * D], S.gate_t[:, :],
                                          start=False, stop=(b % HB == HB - 1), skip_group_check=True)
                if q % 2 == 1:
                    mm.then_inc(lg_done, 1)
                if q == 2:
                    places(0)
            places(1)


def load_expert(sp, S, A, n):
    e, p = n.i, n.p
    w_in = S.sem(f"e_w_in{p}")
    one = slice(e, e + 1) if isinstance(e, int) else bass.ds(e, 1)
    sp.dma_start(S.ew1[:, p, :], A["L1_ffn_w1"][one].rearrange("e d f -> d (e f)")).then_inc(w_in, 16)
    sp.dma_start(S.eb1[:, p, :], A["L1_ffn_b1"][one].rearrange("e (c f) -> f (e c)", f=D), allow_slow_non_contiguous=True).then_inc(w_in, 16)
    sp.dma_start(S.ew2[:, p, :, :], A["L1_ffn_w2"][one].rearrange("e (c f) d -> f (e c) d", f=D)).then_inc(w_in, 16)
    sp.dma_start(S.eb2[:, p:p + 1], A["L1_ffn_b2"][one, :].rearrange("e d -> d e"), allow_slow_non_contiguous=True).then_inc(w_in, 16)


def experts(nc, S, A):
    last = E
    bank = S.bank
    XT, HID, YT, Y = bank[0], bank[1:5], bank[5], bank[6:8]
    CHUNKS = F // D
    RT = [(r, min(T, CAP - r)) for r in range(0, CAP, T)]

    def sem(n):
        return S.sem(f"e_{n}")

    rows_in = [sem(f"rows_in{p}") for p in range(2)]
    w_in = [sem(f"w_in{p}") for p in range(2)]
    stored = [sem(f"stored{p}") for p in range(2)]
    W_LOADS = 4 * 16
    R_LOADS = 2 * 16
    xt_done, xt_out, h_done, h_act, h_dve, y_done, yt_out, b_done, y_out = (
        sem("xt_done"), sem("xt_out"), sem("h_done"), sem("h_act"), sem("h_dve"), sem("y_done"), sem("yt_out"), sem("b_done"), sem("y_out"))
    full = RT[-1][0]

    with nc.Block() as block:
        @block.sync
        def _(sp):
            def load(n, _):
                e, p = n.i, n.p
                if n.lo >= 2:
                    sp.wait_ge(xt_done, e - 1)
                sp.dma_start(S.erows[:, p, 0:full // T, :], S.dispatch[bass.ds(e * CAP, full), :].rearrange("(r t) d -> t r d", t=T)
                             ).then_inc(rows_in[p], 16)
                sp.dma_start(S.erows[0:CAP - full, p, full // T, :], S.dispatch[bass.ds(e * CAP + full, CAP - full), :]).then_inc(rows_in[p], 16)
                if n.lo >= 2:
                    sp.wait_ge(y_done, e - 1)
                    sp.wait_ge(h_act, e * 2 - 2)
                    sp.wait_ge(h_dve, e * 2 - 2)
                    sp.wait_ge(yt_out, e - 1)
                    load_expert(sp, S, A, n)
            run_steps(sp, load, 0, E - 1, 2, 0)

        @block.gpsimd
        def _(g):
            def store(n, _):
                e, p = n.i, n.p
                pool_fence(nc, S, g, n, y_out, e + 1)
                g.dma_start(S.results[bass.ds(e * CAP, full), :].rearrange("(r t) d -> t r d", t=T), S.eout[:, p, 0:full // T, :]
                            ).then_inc(stored[p], 16)
                g.dma_start(S.results[bass.ds(e * CAP + full, CAP - full), :], S.eout[0:CAP - full, p, full // T, :]).then_inc(stored[p], 16)
            run_steps(g, store, 0, E - 1, 2, 0)
            for p in range(2):
                g.wait_ge(stored[p], 32 * E // 2)

        @block.tensor
        def _(pe):
            def step(s, _):
                n, b = s.next(), s.next(-1)
                cur = 0 <= s.lo < E
                if cur:
                    e, p = s.i, s.p
                    pe.wait_ge(xt_out, e + 1)
                    pe.wait_ge(w_in[p], e * 32 + (64 - 32 * p))
                    if s.lo >= 1:
                        pe.wait_ge(h_act, e * 2)
                        pe.wait_ge(h_dve, e * 2)
                    for c in range(CHUNKS):
                        nc.tensor.matmul(HID[c][:, 0:CAP], S.ew1[:, p, c * D:(c + 1) * D], S.eXT[:, p, :], start=True, stop=True).then_inc(h_done, 1)
                if n.lo < E:
                    pe.wait_ge(rows_in[n.p], n.i * 16 + (32 - 16 * n.p))
                    if n.lo >= 1:
                        pe.wait_ge(xt_out, n.i)
                    for r, (r0, rows) in enumerate(RT):
                        mm = nc.tensor.transpose(XT[:, r0:r0 + rows], S.erows[0:rows, n.p, r, :], S.eye[0:rows, 0:rows])
                    mm.then_inc(xt_done, 1)
                if b.lo >= 0:
                    pe.wait_ge(yt_out, b.i + 1)
                    if b.lo >= 2:
                        pe.wait_ge(y_out, b.i - 1)
                    for r, (r0, rows) in enumerate(RT):
                        mm = nc.tensor.transpose(Y[b.p][0:rows, r * D:(r + 1) * D], S.eyT[:, r0:r0 + rows], S.eye[:, :])
                    mm.then_inc(b_done, 1)
                if cur:
                    for c in range(CHUNKS):
                        if c % 2 == 0:
                            pe.wait_ge(h_act, e * 2 + (c // 2 + 1))
                        else:
                            pe.wait_ge(h_dve, e * 2 + (c // 2 + 1))
                        mm = nc.tensor.matmul(YT[:, 0:CAP], S.ew2[:, p, c, :], S.ehid[:, c, :], start=(c == 0), stop=(c == CHUNKS - 1))
                    mm.then_inc(y_done, 1)
            run_steps(pe, step, -1, last, 4, 2)

        @block.scalar
        def _(act):
            def step(s, _):
                n, b = s.next(), s.next(-1)
                if b.lo >= 0:
                    act.wait_ge(y_done, b.i + 1)
                    if b.lo >= 1:
                        act.wait_ge(b_done, b.i)
                    nc.scalar.activation(S.eyT[:, :], YT[:, 0:CAP], ACT.Identity, bias=S.eb2[:, b.p:b.p + 1]).then_inc(yt_out, 1)
                if 0 <= s.lo < E:
                    for c in (0, 2):
                        act.wait_ge(h_done, s.i * 4 + (c + 1))
                        nc.scalar.activation(S.ehid[:, c, :], HID[c][:, 0:CAP], ACT.Relu, bias=S.eb1[:, s.p, c:c + 1]).then_inc(h_act, 1)
                if n.lo < E:
                    act.wait_ge(xt_done, n.i + 1)
                    nc.scalar.copy(S.eXT[:, n.p, :], XT[:, 0:CAP]).then_inc(xt_out, 1)
            run_steps(act, step, -1, last, 4, 2)

        @block.vector
        def _(v):
            def step(s, _):
                b = s.next(-1)
                if 0 <= s.lo < E:
                    for c in (1, 3):
                        v.wait_ge(h_done, s.i * 4 + (c + 1))
                        if c == 1 and s.lo >= 1:
                            v.wait_ge(y_done, s.i)
                        nc.vector.tensor_scalar(S.ehid[:, c, :], HID[c][:, 0:CAP], S.eb1[:, s.p, c:c + 1], 0.0, ALU.add, ALU.max).then_inc(h_dve, 1)
                if b.lo >= 0:
                    v.wait_ge(b_done, b.i + 1)
                    if b.lo >= 2:
                        v.wait_ge(stored[b.p], b.i * 16 - 16 * b.p)
                    nc.vector.tensor_copy(S.eout[:, b.p, 0:full // T, :].rearrange("t r d -> t (r d)"), Y[b.p][:, 0:full])
                    nc.vector.tensor_copy(S.eout[0:CAP - full, b.p, full // T, :], Y[b.p][0:CAP - full, full:full + D]).then_inc(y_out, 1)
            run_steps(v, step, -1, last, 4, 2)


def combine(nc, S, out):
    GROUPS = ((0, 6), (6, 11), (11, 14), (14, 16))
    gathered = [S.sem(f"c_gathered{q}") for q in range(len(GROUPS))]
    x_ready, written = S.sem("c_x_ready"), S.sem("c_written")
    rows = S.attn[1][:, :, :].rearrange("t p n -> t (p n)")

    with nc.Block() as block:
        @block.gpsimd
        def _(g):
            for q, (first, end) in enumerate(GROUPS):
                for b in range(first, end):
                    nc.gpsimd.indirect_dma_start(out=tile_at(rows, b, D), out_offset=None, in_=S.results[:, :],
                                                 in_offset=bass.IndirectOffsetOnAxis(ap=S.row_from[:, b:b + 1], axis=0)
                                                 ).then_inc(gathered[q], 16)

        @block.vector
        def _(v):
            for q, (first, end) in enumerate(GROUPS):
                v.wait_ge(gathered[q], 16 * (end - first))
                for b in range(first, end):
                    nc.vector.scalar_tensor_tensor(tile_at(S.x, b, D), tile_at(rows, b, D), S.weight[:, b:b + 1], tile_at(S.x, b, D),
                                                   ALU.mult, ALU.add).then_inc(x_ready, 1)

        @block.sync
        def _(sp):
            for first, end in GROUPS:
                sp.wait_ge(x_ready, end)
                sp.dma_start(out[first:end].rearrange("b t d -> t b d"),
                             S.x[:, first * D:end * D].rearrange("t (b d) -> t b d", d=D)).then_inc(written, 16)
            sp.wait_ge(written, 16 * len(GROUPS))


def program(nc, A, out):
    with ExitStack() as ctx:
        S = Store(nc, ctx)
        sb = S.sb
        S.bank = [ctx.enter_context(nc.psum_tensor(f"bank{b}", [D, 512], F32)) for b in range(8)]
        S.bank_bf = [b[:, :].bitcast(BF16) for b in S.bank]
        S.dispatch = nc.dram_tensor("dispatch", (ROWS + B * T, D), F32, kind="Internal").ap()
        S.results = nc.dram_tensor("results", (ROWS, D), F32, kind="Internal").ap()
        S.eye = sb("eye", [D, D])
        S.eye_bf = sb("eye_bf", [D, D], BF16)
        S.x = sb("x", [T, B * D])
        S.cols = sb("cols", [D, 5])
        S.bvcol = sb("bvcol", [D, 8])
        S.wq0, S.wk0, S.wv0, S.wo0 = (sb(w, [D, D]) for w in ("wq0", "wk0", "wv0", "wo0"))
        S.row_o = sb("row_o", [1, 2, D])
        S.negsel = sb("negsel", [D, H * KEYS], BF16)
        S.len_i = sb("len_i", [D, B], I32)
        S.len_f = sb("len_f", [D, B])
        S.w1n = sb("w1n", [D, 4, D])
        S.w2n = sb("w2n", [D, F])
        S.w1t = sb("w1t", [D, F], BF16)
        S.w2t = sb("w2t", [D, F], BF16)
        S.w1q = sb("w1q", [D, F], BF16)
        S.w2q = sb("w2q", [D, F], BF16)
        S.b1bc = sb("b1bc", [D, F])
        S.b2bc = sb("b2bc", [D, D])
        S.bias8 = sb("bias8", [D, 2, 8])
        S.bias_row = sb("bias_row", [1, 2, D])
        S.parts_row = sb("parts_row", [1, 3, 2, D], BF16)
        S.bias3_0 = sb("bias3_0", [3, 2, D], BF16)
        S.parts = sb("parts", [D, 3, 2, 8], BF16)
        S.bias3 = sb("bias3", [3, 2, H * DH1], BF16)
        S.kpos = sb("kpos", [D, 1])
        S.krow = sb("krow", [1, KEYS])
        S.maskrow32 = sb("maskrow32", [1, B, KEYS])
        S.maskrow = sb("maskrow", [1, B * KEYS], BF16)
        S.maskcol = sb("maskcol", [D, B])
        S.mcol = sb("mcol", [KEYS, 2])
        S.wq1, S.wk1, S.wv1 = (sb(w, [D, H * DH1]) for w in ("wq1", "wk1", "wv1"))
        S.wo1 = sb("wo1", [D, 8, D])
        S.cosq = sb("cosq", [T, DH1])
        S.sinq = sb("sinq", [T, DH1])
        S.gate_w = sb("gate_w", [E, D])
        S.gate_b = sb("gate_b", [1, E])
        S.gate_t = sb("gate_t", [D, E])
        S.upto32 = sb("upto32", [D, D])
        S.upto = sb("upto", [D, D], BF16)
        S.expert_ids = sb("expert_ids", [D, E])
        S.dropped_row = sb("dropped_row", [D, B])
        S.ones_row = sb("ones_row", [1, D])
        S.ones_bf = sb("ones_bf", [D, D], BF16)
        S.ones_mean = sb("ones_mean", [D, D])
        S.wabs = sb("wabs", [D, 2])
        S.wmean = sb("wmean", [D, 2])
        S.wscale = sb("wscale", [D, 2])
        S.wmean127 = sb("wmean127", [D, 2])
        S.minus_half = sb("minus_half", [D, 2])
        S.minus_magic = sb("minus_magic", [D, 1])
        S.fence = sb("fence", [D, 1])
        S.fence_x = sb("fence_x", [D, 1])
        S.fence_g = sb("fence_g", [D, 2])
        S.stats = sb("stats", [D, 2, 2, 6])
        S.meanvar = sb("meanvar", [D, 2, 2, 2])
        S.varx = sb("varx", [D, 2, 2])
        S.rstd = sb("rstd", [D, 2, 2])
        S.xn = sb("xn", [T, 2, D])
        S.ctx_in = sb("ctx_in", [KEYS, 2, D])
        S.cn = sb("cn", [KEYS, 2, D])
        S.xT = sb("xT", [D, 2, T])
        S.cT = sb("cT", [D, 2, KEYS])
        S.qT = [sb("qT0", [D, 2, 8, T], BF16), sb("qT1", [D, 2, 8, T])]
        S.kT = [sb("kT0", [D, 2, H, KEYS], BF16), sb("kT1", [D, 2, 8, KEYS])]
        S.qT_bf, S.kT_bf = sb("qT_bf", [D, 8, T], BF16), sb("kT_bf", [D, 8, KEYS], BF16)
        S.qparts, S.kparts = sb("qparts", [T, 8 * D], BF16), sb("kparts", [KEYS, 8 * D], BF16)
        S.qrest, S.krest = sb("qrest", [T, D]), sb("krest", [KEYS, D])
        S.vaug = [sb("vaug0", [KEYS, 2, H, DH0 + 1]), sb("vaug1", [KEYS, 2, H, DH1 + 1])]
        S.rowmax = sb("rowmax", [T, 2, D], BF16)
        S.maxT = sb("maxT", [D, 2, T], BF16)
        S.probs = sb("probs", [KEYS, 2, 2, 4 * T])
        S.attn = [sb("attn0", [T, 2, H * DH0]), sb("attn1", [T, 2, H * DH1])]
        S.attnT = sb("attnT", [D, 8, T])
        S.recip = sb("recip", [T, 2, 4])
        S.qcos = sb("qcos", [T, 2, 512])
        S.qsin = sb("qsin", [T, 2, 512])
        S.qrot = sb("qrot", [T, 2, 512])
        S.kcos = sb("kcos", [KEYS, 2, 512])
        S.ksin = sb("ksin", [KEYS, 2, 512])
        S.krot = sb("krot", [KEYS, 2, 512])
        S.stats_all = sb("stats_all", [T, B, 6])
        S.mv_all = sb("mv_all", [T, B, 2])
        S.var_all = sb("var_all", [T, B])
        S.rstd_all = sb("rstd_all", [T, B])
        S.zmax = sb("zmax", [T, B])
        S.zinv = sb("zinv", [T, B])
        S.zout = sb("zout", [T, B])
        S.zq = sb("zq", [T, 2, 2, D])
        S.zT = sb("zT", [D, 2, 2 * T], BF16)
        S.hid = sb("hid", [T, 2, F])
        S.gsq = sb("gsq", [T, F])
        S.sumsq = sb("sumsq", [T, 2])
        S.meansq = sb("meansq", [T, 2])
        S.rms = sb("rms", [T, 2])
        S.gmax = sb("gmax", [T, 2])
        S.ginv = sb("ginv", [T, 2])
        S.gout = sb("gout", [T, 2, 2])
        S.gq = sb("gq", [T, 2, F])
        S.gT = sb("gT", [D, 2, F], BF16)
        S.logits = sb("logits", [T, B, E])
        S.top = sb("top", [T, B])
        S.picked = sb("picked", [T, B, E])
        S.exps = sb("exps", [T, B, E])
        S.sumexp = sb("sumexp", [T, B])
        S.expert = sb("expert", [T, B])
        S.onehot = sb("onehot", [T, (2 * B - 1) * E], BF16)
        S.pos = sb("pos", [T, B])
        S.keep = sb("keep", [T, B])
        S.row_f = sb("row_f", [T, B])
        S.row_from = sb("row_from", [T, B], I32)
        S.row_to = sb("row_to", [T, B], I32)
        S.weight = sb("weight", [T, B])
        S.erows = sb("erows", [T, 2, 3, D])
        S.eXT = sb("eXT", [D, 2, CAP])
        S.ew1 = sb("ew1", [D, 2, F])
        S.ew2 = sb("ew2", [D, 2, 4, D])
        S.eb1 = sb("eb1", [D, 2, 4])
        S.eb2 = sb("eb2", [D, 2])
        S.eyT = sb("eyT", [D, CAP])
        S.ehid = sb("ehid", [D, 4, CAP])
        S.eout = sb("eout", [T, 2, 3, D])
        with nc.sbuf_tensor("zeros", [D, ROWS // 2], F32) as z, nc.sbuf_tensor("negsel32", [D, H * KEYS], F32) as n32:
            S.zeros, S.negsel32 = z, n32
            setup(nc, S, A)
        for k in STAGES:
            k(nc, S, A, out)


STAGES = [lambda nc, S, A, out: attention(nc, S, A, 0), lambda nc, S, A, out: ffn0(nc, S, A),
          lambda nc, S, A, out: attention(nc, S, A, 1), lambda nc, S, A, out: dispatch(nc, S, A),
          lambda nc, S, A, out: experts(nc, S, A), lambda nc, S, A, out: combine(nc, S, out)]


def shape_constants():
    f = np.float32
    d, h = np.arange(D), np.arange(H)
    t = np.arange(T, dtype=f)
    inv_freq = (f(1.0) / f(10000.0) ** (np.arange(0, DH1, 2, dtype=f) / f(DH1))).astype(f)
    angle = (t[:, None] * inv_freq[None, :]).astype(f)
    cos, sin = np.repeat(np.cos(angle), 2, 1).astype(f), np.repeat(np.sin(angle), 2, 1).astype(f)
    sign = np.where(np.arange(DH1) % 2 == 0, f(-1), f(1))
    return {
        "c_eye": np.eye(D, dtype=f),
        "c_negsel": np.repeat(-(d[:, None] == (64 * (h % 2) + h // 2)[None, :]).astype(f), KEYS, axis=1),
        "c_kpos": d.astype(f).reshape(D, 1),
        "c_krow": np.arange(KEYS, dtype=f).reshape(1, KEYS),
        "c_cosq": cos, "c_sinq": (sin * sign).astype(f),
        "c_upto": (d[:, None] <= d[None, :]).astype(f),
        "c_expert_ids": np.tile(np.arange(E, dtype=f) - E, (D, 1)),
        "c_dropped": (ROWS + np.arange(B)[None, :] * T + d[:, None]).astype(f),
    }


_INS = ['x', 'ctx_1024', '_lenS2', 'L0_xattn_q_w', 'L0_xattn_q_b', 'L0_xattn_k_w', 'L0_xattn_k_b', 'L0_xattn_v_w', 'L0_xattn_v_b',
        'L0_xattn_o_w', 'L0_xattn_o_b', 'L0_ffn_w1', 'L0_ffn_b1', 'L0_ffn_w2', 'L0_ffn_b2', 'L1_xattn_ln_g', 'L1_xattn_ln_b',
        'L1_xattn_Wq', 'L1_xattn_bq', 'L1_xattn_Wk', 'L1_xattn_bk', 'L1_xattn_Wv', 'L1_xattn_bv', 'L1_xattn_Wo', 'L1_xattn_bo',
        'L1_ffn_gate_w', 'L1_ffn_gate_b', 'L1_ffn_w1', 'L1_ffn_b1', 'L1_ffn_w2', 'L1_ffn_b2']


def kernel(**inputs):
    import concourse.bacc as _bacc
    from concourse.bass_utils import run_bass_kernel_spmd as _run

    nc = _bacc.Bacc("TRN2", target_bir_lowering=False, num_devices=1)
    arrays = {name: np.ascontiguousarray(inputs[name]) for name in _INS}
    arrays.update(shape_constants())
    aps = {name: nc.dram_tensor("in_" + name, a.shape, mybir.dt.from_np(a.dtype), kind="ExternalInput").ap() for name, a in arrays.items()}
    out = nc.dram_tensor("out", (B, T, D), F32, kind="ExternalOutput").ap()
    program(nc, aps, out)
    r = _run(nc, [{"in_" + name: a for name, a in arrays.items()}], core_ids=[0])
    return r.results[0]["out"]
```
